# Optimizing a Trainium2 kernel written in Bass

```python
import numpy as np
import jax
import jax.numpy as jnp

def _softmax(x, axis=-1):
    return jax.nn.softmax(x, axis=axis)

def _gelu(x):
    return jax.nn.gelu(x, approximate=True)

def _silu(x):
    return jax.nn.silu(x)

def _sigmoid(x):
    return jax.nn.sigmoid(x)

def _layernorm(x, axis=-1, eps=1e-05):
    m = jnp.mean(x, axis=axis, keepdims=True)
    v = jnp.var(x, axis=axis, keepdims=True)
    return (x - m) / jnp.sqrt(v + eps)

def _scatter_add(tgt, idx, src, axis=0):
    return tgt.at[idx].add(src)

def _segment_sum(src, seg, n):
    return jax.ops.segment_sum(src, seg, n)
kernel_name = 'mk_decoder_postln_d2_seqx_r8_fd1e64'

def setup_inputs(seed: int=0):
    np.random.seed(seed)
    _w = jnp.asarray

    def _rec_inputs():
        import jax
        import jax.numpy as jnp
        _rk = jax.random.key(seed)
        x = 7.22e-05 + 1 * jax.random.normal(jax.random.fold_in(_rk, 1), (32, 128, 128), jnp.float32)
        _lenS = 128 - jax.random.randint(jax.random.fold_in(_rk, 7), (32,), 0, max(1, 128 // 4) + 1, jnp.int32)
        _lenS2 = 128 - jax.random.randint(jax.random.fold_in(_rk, 8), (32,), 0, max(1, 128 // 4) + 1, jnp.int32)
        _ctx_1024P = jax.random.normal(jax.random.fold_in(_rk, 11), (32, 16, 128), jnp.float32)
        _ctx_1024c = jax.random.dirichlet(jax.random.fold_in(_rk, 511), 0.3 * jnp.ones((16,), jnp.float32), (32, 128))
        _ctx_1024t = jnp.einsum('bsk,bkd->bsd', _ctx_1024c, _ctx_1024P)
        _ctx_1024t = _ctx_1024t * jax.lax.rsqrt(jnp.mean(jnp.square(_ctx_1024t)) + 1e-12) * 0.953939
        ctx_1024 = 4.13588e-05 + 0.999923 * (_ctx_1024t + 0.3 * jax.random.normal(jax.random.fold_in(_rk, 611), (32, 128, 128), jnp.float32))
        return (x, ctx_1024)
    x, ctx_1024 = _rec_inputs()

    def _L0_attn_setup():
        import jax, jax.numpy as jnp
        import numpy as np
        import math
        H = 16
        EPS = 1e-06

        def _apply_kernel(x, orf):
            m, d_k = orf.shape
            proj = jnp.einsum('bhld,md->bhlm', x, orf) / d_k ** 0.25
            norm = jnp.sum(x * x, axis=-1, keepdims=True) / (2.0 * math.sqrt(d_k))
            return (jnp.exp(proj - norm) + EPS) / math.sqrt(m)
        key = jax.random.key(seed)
        ks = jax.random.split(key, 10)
        B, L, D, m = (4, 512, 128, 32)
        d_k = D // H
        s = 1.0 / math.sqrt(D)
        return {'x': jax.random.normal(ks[0], (B, L, D), jnp.float32), 'Wq': jax.random.normal(ks[1], (D, D), jnp.float32) * s, 'bq': jax.random.normal(ks[2], (D,), jnp.float32) * s, 'Wk': jax.random.normal(ks[3], (D, D), jnp.float32) * s, 'bk': jax.random.normal(ks[4], (D,), jnp.float32) * s, 'Wv': jax.random.normal(ks[5], (D, D), jnp.float32) * s, 'bv': jax.random.normal(ks[6], (D,), jnp.float32) * s, 'Wo': jax.random.normal(ks[7], (D, D), jnp.float32) * s, 'bo': jax.random.normal(ks[8], (D,), jnp.float32) * s, 'orf': jax.random.normal(ks[9], (m, d_k), jnp.float32)}
    _L0_attn_all = _L0_attn_setup()
    _L0_attn_in = {k: v for k, v in _L0_attn_all.items() if k in ('Wq', 'bq', 'Wk', 'bk', 'Wv', 'bv', 'Wo', 'bo', 'orf')}
    del _L0_attn_all

    def _L0_xattn_setup():
        import jax, jax.numpy as jnp
        import numpy as np
        H = 16
        D_MODEL = 128
        D_K = D_MODEL // H
        key = jax.random.key(seed)
        ks = jax.random.split(key, 11)
        B, S = (4, 256)
        scale = 1.0 / np.sqrt(D_MODEL)
        inp = {'query': jax.random.normal(ks[0], (B, S, D_MODEL), dtype=jnp.float32), 'key': jax.random.normal(ks[1], (B, S, D_MODEL), dtype=jnp.float32), 'value': jax.random.normal(ks[2], (B, S, D_MODEL), dtype=jnp.float32), 'Wq': jax.random.normal(ks[3], (D_MODEL, D_MODEL), dtype=jnp.float32) * scale, 'bq': jnp.zeros((D_MODEL,), dtype=jnp.float32), 'Wk': jax.random.normal(ks[4], (D_MODEL, D_MODEL), dtype=jnp.float32) * scale, 'bk': jnp.zeros((D_MODEL,), dtype=jnp.float32), 'Wv': jax.random.normal(ks[5], (D_MODEL, D_MODEL), dtype=jnp.float32) * scale, 'bv': jnp.zeros((D_MODEL,), dtype=jnp.float32), 'Wo': jax.random.normal(ks[6], (D_MODEL, D_MODEL), dtype=jnp.float32) * scale, 'bo': jnp.zeros((D_MODEL,), dtype=jnp.float32)}
        return inp
    _L0_xattn_all = _L0_xattn_setup()
    _L0_xattn_in = {k: v for k, v in _L0_xattn_all.items() if k in ('Wq', 'bq', 'Wk', 'bk', 'Wv', 'bv', 'Wo', 'bo')}
    del _L0_xattn_all

    def _L0_ffn_setup():
        import jax, jax.numpy as jnp
        import numpy as np
        D_IN, D_HID = (128, 512)

        def _ternary(key, shape):
            return jax.random.randint(key, shape, -1, 2).astype(jnp.float32)

        def _tlin(x, w, s):
            return jnp.einsum('bsi,oi->bso', x, w) * s
        key = jax.random.key(seed)
        ks = jax.random.split(key, 12)
        inv = lambda fan: 1.0 / np.sqrt(fan).astype(np.float32)
        return {'x': jax.random.normal(ks[0], (4, 256, D_IN), dtype=jnp.float32), 'w1_w': _ternary(ks[1], (D_HID, D_IN)), 'w1_s': jax.random.uniform(ks[2], (D_HID,), dtype=jnp.float32) * inv(D_IN), 'w2_w': _ternary(ks[3], (D_HID, D_IN)), 'w2_s': jax.random.uniform(ks[4], (D_HID,), dtype=jnp.float32) * inv(D_IN), 'h1_w': _ternary(ks[5], (D_HID, D_HID)), 'h1_s': jax.random.uniform(ks[6], (D_HID,), dtype=jnp.float32) * inv(D_HID), 'h2_w': _ternary(ks[7], (D_HID, D_HID)), 'h2_s': jax.random.uniform(ks[8], (D_HID,), dtype=jnp.float32) * inv(D_HID), 'w3_w': _ternary(ks[9], (D_IN, D_HID)), 'w3_s': jax.random.uniform(ks[10], (D_IN,), dtype=jnp.float32) * inv(D_HID)}
    _L0_ffn_all = _L0_ffn_setup()
    _L0_ffn_in = {k: v for k, v in _L0_ffn_all.items() if k in ('w1_w', 'w1_s', 'w2_w', 'w2_s', 'h1_w', 'h1_s', 'h2_w', 'h2_s', 'w3_w', 'w3_s')}
    del _L0_ffn_all

    def _L1_attn_setup():
        import jax, jax.numpy as jnp
        import numpy as np
        D_MODEL = 128
        N_HEADS = 16
        D_HEAD = D_MODEL // N_HEADS
        LUT_SIZE = 512
        TWO_PI = 2.0 * np.pi
        SCALE = np.sqrt(2.0 * D_HEAD).astype(np.float32)
        _GRID = (TWO_PI * np.arange(LUT_SIZE) / LUT_SIZE).astype(np.float32)
        _SIN_TABLE = jnp.asarray(np.sin(_GRID))
        _COS_TABLE = jnp.asarray(np.cos(_GRID))

        def _lut_sin_cos(theta):
            idx = jnp.mod(jnp.round(theta * (LUT_SIZE / TWO_PI)).astype(jnp.int32), LUT_SIZE)
            return (_SIN_TABLE[idx], _COS_TABLE[idx])
        key = jax.random.key(seed)
        ks = jax.random.split(key, 7)
        B, S = (2, 256)
        x = jax.random.normal(ks[0], (B, S, D_MODEL), dtype=jnp.float32)
        w_q = 0.02 * jax.random.normal(ks[1], (N_HEADS, D_HEAD), dtype=jnp.float32)
        b_q = jnp.zeros((N_HEADS, D_HEAD), dtype=jnp.float32)
        w_k = 0.02 * jax.random.normal(ks[2], (N_HEADS, D_HEAD), dtype=jnp.float32)
        b_k = jnp.zeros((N_HEADS, D_HEAD), dtype=jnp.float32)
        v_w = jax.random.normal(ks[3], (D_MODEL, D_MODEL), dtype=jnp.float32) / np.sqrt(D_MODEL)
        out_w = jax.random.normal(ks[4], (D_MODEL, D_MODEL), dtype=jnp.float32) / np.sqrt(D_MODEL)
        return {'x': x, 'w_q': w_q, 'b_q': b_q, 'w_k': w_k, 'b_k': b_k, 'v_w': v_w, 'out_w': out_w}
    _L1_attn_all = _L1_attn_setup()
    _L1_attn_in = {k: v for k, v in _L1_attn_all.items() if k in ('w_q', 'b_q', 'w_k', 'b_k', 'v_w', 'out_w')}
    del _L1_attn_all

    def _L1_xattn_setup():
        import jax, jax.numpy as jnp
        import numpy as np
        EMBED_DIM = 128
        N_HEADS = 16
        DK = EMBED_DIM // N_HEADS
        key = jax.random.key(seed)
        ks = jax.random.split(key, 8)
        B, S, D = (2, 256, EMBED_DIM)
        s = 1.0 / np.sqrt(D)
        return {'key': jax.random.normal(ks[0], (B, S, D), jnp.float32), 'query': jax.random.normal(ks[1], (B, S, D), jnp.float32), 'value': jax.random.normal(ks[2], (B, S, D), jnp.float32), 'Wq': jax.random.normal(ks[3], (D, D), jnp.float32) * s, 'Wk': jax.random.normal(ks[4], (D, D), jnp.float32) * s, 'Wv': jax.random.normal(ks[5], (D, D), jnp.float32) * s, 'Wo': jax.random.normal(ks[6], (D, D), jnp.float32) * s, 'bo': jax.random.normal(ks[7], (D,), jnp.float32) * 0.01}
    _L1_xattn_all = _L1_xattn_setup()
    _L1_xattn_in = {k: v for k, v in _L1_xattn_all.items() if k in ('Wq', 'Wk', 'Wv', 'Wo', 'bo')}
    del _L1_xattn_all

    def _L1_ffn_setup():
        import jax, jax.numpy as jnp
        import numpy as np
        NUM_EXPERTS = 8
        TOP_K = 2
        CAP_RATIO = 1.25
        INIT_STD = 0.02
        key = jax.random.key(seed)
        k1, k2, k3, k4 = jax.random.split(key, 4)
        B, T, H, F = (4, 256, 128, 512)
        x = jax.random.normal(k1, (B, T, H), jnp.float32)
        router_w = jax.random.normal(k2, (NUM_EXPERTS, H), jnp.float32) * INIT_STD
        w1 = jax.random.normal(k3, (NUM_EXPERTS, H, F), jnp.float32) * INIT_STD
        w2 = jax.random.normal(k4, (NUM_EXPERTS, F, H), jnp.float32) * INIT_STD
        return {'x': x, 'router_w': router_w, 'w1': w1, 'w2': w2}
    _L1_ffn_all = _L1_ffn_setup()
    _L1_ffn_in = {k: v for k, v in _L1_ffn_all.items() if k in ('router_w', 'w1', 'w2')}
    del _L1_ffn_all
    return {'x': x, 'ctx_1024': ctx_1024, 'L0_attn_Wq': _L0_attn_in['Wq'], 'L0_attn_bq': _L0_attn_in['bq'], 'L0_attn_Wk': _L0_attn_in['Wk'], 'L0_attn_bk': _L0_attn_in['bk'], 'L0_attn_Wv': _L0_attn_in['Wv'], 'L0_attn_bv': _L0_attn_in['bv'], 'L0_attn_Wo': _L0_attn_in['Wo'], 'L0_attn_bo': _L0_attn_in['bo'], 'L0_attn_orf': _L0_attn_in['orf'], 'L0_xattn_Wq': _L0_xattn_in['Wq'], 'L0_xattn_bq': _L0_xattn_in['bq'], 'L0_xattn_Wk': _L0_xattn_in['Wk'], 'L0_xattn_bk': _L0_xattn_in['bk'], 'L0_xattn_Wv': _L0_xattn_in['Wv'], 'L0_xattn_bv': _L0_xattn_in['bv'], 'L0_xattn_Wo': _L0_xattn_in['Wo'], 'L0_xattn_bo': _L0_xattn_in['bo'], 'L0_ffn_w1_w': _L0_ffn_in['w1_w'], 'L0_ffn_w1_s': _L0_ffn_in['w1_s'], 'L0_ffn_w2_w': _L0_ffn_in['w2_w'], 'L0_ffn_w2_s': _L0_ffn_in['w2_s'], 'L0_ffn_h1_w': _L0_ffn_in['h1_w'], 'L0_ffn_h1_s': _L0_ffn_in['h1_s'], 'L0_ffn_h2_w': _L0_ffn_in['h2_w'], 'L0_ffn_h2_s': _L0_ffn_in['h2_s'], 'L0_ffn_w3_w': _L0_ffn_in['w3_w'], 'L0_ffn_w3_s': _L0_ffn_in['w3_s'], 'L1_attn_w_q': _L1_attn_in['w_q'], 'L1_attn_b_q': _L1_attn_in['b_q'], 'L1_attn_w_k': _L1_attn_in['w_k'], 'L1_attn_b_k': _L1_attn_in['b_k'], 'L1_attn_v_w': _L1_attn_in['v_w'], 'L1_attn_out_w': _L1_attn_in['out_w'], 'L1_xattn_Wq': _L1_xattn_in['Wq'], 'L1_xattn_Wk': _L1_xattn_in['Wk'], 'L1_xattn_Wv': _L1_xattn_in['Wv'], 'L1_xattn_Wo': _L1_xattn_in['Wo'], 'L1_xattn_bo': _L1_xattn_in['bo'], 'L1_ffn_router_w': _L1_ffn_in['router_w'], 'L1_ffn_w1': _L1_ffn_in['w1'], 'L1_ffn_w2': _L1_ffn_in['w2']}

def reference(x, ctx_1024, L0_attn_Wq, L0_attn_bq, L0_attn_Wk, L0_attn_bk, L0_attn_Wv, L0_attn_bv, L0_attn_Wo, L0_attn_bo, L0_attn_orf, L0_xattn_Wq, L0_xattn_bq, L0_xattn_Wk, L0_xattn_bk, L0_xattn_Wv, L0_xattn_bv, L0_xattn_Wo, L0_xattn_bo, L0_ffn_w1_w, L0_ffn_w1_s, L0_ffn_w2_w, L0_ffn_w2_s, L0_ffn_h1_w, L0_ffn_h1_s, L0_ffn_h2_w, L0_ffn_h2_s, L0_ffn_w3_w, L0_ffn_w3_s, L1_attn_w_q, L1_attn_b_q, L1_attn_w_k, L1_attn_b_k, L1_attn_v_w, L1_attn_out_w, L1_xattn_Wq, L1_xattn_Wk, L1_xattn_Wv, L1_xattn_Wo, L1_xattn_bo, L1_ffn_router_w, L1_ffn_w1, L1_ffn_w2):
    import jax
    import jax.numpy as jnp

    def _L0_attn_ref(x, Wq, bq, Wk, bk, Wv, bv, Wo, bo, orf):
        import jax, jax.numpy as jnp
        import numpy as np
        import math
        H = 16
        EPS = 1e-06

        def _apply_kernel(x, orf):
            m, d_k = orf.shape
            proj = jnp.einsum('bhld,md->bhlm', x, orf) / d_k ** 0.25
            norm = jnp.sum(x * x, axis=-1, keepdims=True) / (2.0 * math.sqrt(d_k))
            return (jnp.exp(proj - norm) + EPS) / math.sqrt(m)
        B, L, D = x.shape
        d_k = D // H

        def split(y):
            return y.reshape(B, L, H, d_k).transpose(0, 2, 1, 3)
        q = split(x @ Wq.T + bq)
        k = split(x @ Wk.T + bk)
        v = split(x @ Wv.T + bv)
        q_phi = _apply_kernel(q, orf)
        k_phi = _apply_kernel(k, orf)
        kv = jnp.einsum('bhlm,bhld->bhmd', k_phi, v)
        ksum = jnp.sum(k_phi, axis=2)
        num = jnp.einsum('bhlm,bhmd->bhld', q_phi, kv)
        den = jnp.einsum('bhlm,bhm->bhl', q_phi, ksum)
        out = num / den[..., None]
        out = out.transpose(0, 2, 1, 3).reshape(B, L, D)
        return out @ Wo.T + bo

    def _L0_xattn_ref(query, key, value, Wq, bq, Wk, bk, Wv, bv, Wo, bo):
        import jax, jax.numpy as jnp
        import numpy as np
        H = 16
        D_MODEL = 128
        D_K = D_MODEL // H
        B, S, _ = query.shape

        def proj(x, W, b):
            y = jnp.einsum('bsd,ed->bse', x, W) + b
            return y.reshape(B, S, H, D_K).transpose(0, 2, 1, 3)
        q = proj(query, Wq, bq)
        k = proj(key, Wk, bk)
        v = proj(value, Wv, bv)
        scores = jnp.einsum('bhqd,bhkd->bhqk', q, k) / jnp.sqrt(jnp.float32(D_K))
        attn = jax.nn.softmax(scores, axis=-1)
        out = jnp.einsum('bhqk,bhkd->bhqd', attn, v)
        out = out.transpose(0, 2, 1, 3).reshape(B, S, H * D_K)
        return jnp.einsum('bsd,ed->bse', out, Wo) + bo

    def _L0_ffn_ref(x, w1_w, w1_s, w2_w, w2_s, h1_w, h1_s, h2_w, h2_s, w3_w, w3_s):
        import jax, jax.numpy as jnp
        import numpy as np
        D_IN, D_HID = (128, 512)

        def _ternary(key, shape):
            return jax.random.randint(key, shape, -1, 2).astype(jnp.float32)

        def _tlin(x, w, s):
            return jnp.einsum('bsi,oi->bso', x, w) * s
        h = jax.nn.silu(_tlin(x, w1_w, w1_s)) * _tlin(x, w2_w, w2_s)
        h = jax.nn.gelu(_tlin(h, h1_w, h1_s), approximate=False)
        h = jax.nn.gelu(_tlin(h, h2_w, h2_s), approximate=False)
        return _tlin(h, w3_w, w3_s)

    def _L1_attn_ref(x, w_q, b_q, w_k, b_k, v_w, out_w):
        import jax, jax.numpy as jnp
        import numpy as np
        D_MODEL = 128
        N_HEADS = 16
        D_HEAD = D_MODEL // N_HEADS
        LUT_SIZE = 512
        TWO_PI = 2.0 * np.pi
        SCALE = np.sqrt(2.0 * D_HEAD).astype(np.float32)
        _GRID = (TWO_PI * np.arange(LUT_SIZE) / LUT_SIZE).astype(np.float32)
        _SIN_TABLE = jnp.asarray(np.sin(_GRID))
        _COS_TABLE = jnp.asarray(np.cos(_GRID))

        def _lut_sin_cos(theta):
            idx = jnp.mod(jnp.round(theta * (LUT_SIZE / TWO_PI)).astype(jnp.int32), LUT_SIZE)
            return (_SIN_TABLE[idx], _COS_TABLE[idx])
        B, S, D = x.shape
        x_heads = x.reshape(B, S, N_HEADS, D_HEAD)
        theta_q = x_heads / (1.0 + jnp.abs(w_q)) + b_q
        sin_q, cos_q = _lut_sin_cos(theta_q)
        Q = jnp.concatenate([cos_q, sin_q], axis=-1)
        theta_k = x_heads / (1.0 + jnp.abs(w_k)) + b_k
        sin_k, cos_k = _lut_sin_cos(theta_k)
        K = jnp.concatenate([cos_k, sin_k], axis=-1)
        V = (x @ v_w.T).reshape(B, S, N_HEADS, D_HEAD)
        scores = jnp.einsum('bqhe,bkhe->bhqk', Q, K) / SCALE
        causal = jnp.triu(jnp.ones((S, S), dtype=bool), k=1)
        scores = jnp.where(causal, -jnp.inf, scores)
        attn = jax.nn.softmax(scores, axis=-1)
        out = jnp.einsum('bhqk,bkhd->bqhd', attn, V).reshape(B, S, D)
        return out @ out_w.T

    def _L1_xattn_ref(key, query, value, Wq, Wk, Wv, Wo, bo):
        import jax, jax.numpy as jnp
        import numpy as np
        EMBED_DIM = 128
        N_HEADS = 16
        DK = EMBED_DIM // N_HEADS
        B, Sk, D = key.shape
        Sq = query.shape[1]
        H, dk = (N_HEADS, DK)
        Q = (query @ Wq.T).reshape(B, Sq, H, dk).transpose(0, 2, 1, 3)
        K = (key @ Wk.T).reshape(B, Sk, H, dk).transpose(0, 2, 1, 3)
        V = (value @ Wv.T).reshape(B, Sk, H, dk).transpose(0, 2, 1, 3)
        scores = jnp.einsum('bhqd,bhkd->bhqk', Q, K) / jnp.sqrt(jnp.float32(dk))
        attn = jax.nn.softmax(scores, axis=-1)
        ctx = jnp.einsum('bhqk,bhkd->bhqd', attn, V)
        concat = ctx.transpose(0, 2, 1, 3).reshape(B, Sq, H * dk)
        return concat @ Wo.T + bo

    def _L1_ffn_ref(x, router_w, w1, w2):
        import jax, jax.numpy as jnp
        import numpy as np
        NUM_EXPERTS = 8
        TOP_K = 2
        CAP_RATIO = 1.25
        INIT_STD = 0.02
        B, T, H = x.shape
        E, K = (NUM_EXPERTS, TOP_K)
        xf = x.reshape(-1, H)
        N = xf.shape[0]
        P = N * K
        capacity = int(CAP_RATio * N * K / E) + 1 if False else int(CAP_RATIO * N * K / E) + 1
        logits = xf @ router_w.T
        probs = jax.nn.softmax(logits, axis=-1)
        k_probs, k_idx = jax.lax.top_k(probs, K)
        k_probs = k_probs / jnp.sum(k_probs, axis=-1, keepdims=True)
        flat_e = k_idx.reshape(-1)
        onehot = jax.nn.one_hot(flat_e, E, dtype=jnp.int32)
        rank = jnp.take_along_axis(jnp.cumsum(onehot, axis=0) - 1, flat_e[:, None], axis=1)[:, 0]
        keep = rank < capacity
        slot = jnp.minimum(rank, capacity - 1)
        token_id = jnp.arange(P) // K
        dispatched = jnp.where(keep[:, None], xf[token_id], 0.0)
        buf = jnp.zeros((E, capacity, H), x.dtype).at[flat_e, slot].add(dispatched)
        h = jax.nn.silu(jnp.einsum('ech,ehf->ecf', buf, w1))
        out_buf = jnp.einsum('ecf,efh->ech', h, w2)
        pair_out = out_buf[flat_e, slot] * keep[:, None].astype(x.dtype)
        combined = jnp.sum(pair_out.reshape(N, K, H) * k_probs[..., None], axis=1)
        return combined.reshape(B, T, H) + x
    x = _layernorm(x + _L0_attn_ref(x, L0_attn_Wq, L0_attn_bq, L0_attn_Wk, L0_attn_bk, L0_attn_Wv, L0_attn_bv, L0_attn_Wo, L0_attn_bo, L0_attn_orf), axis=-1)
    x = _layernorm(x + _L0_xattn_ref(x, ctx_1024, ctx_1024, L0_xattn_Wq, L0_xattn_bq, L0_xattn_Wk, L0_xattn_bk, L0_xattn_Wv, L0_xattn_bv, L0_xattn_Wo, L0_xattn_bo), axis=-1)
    x = _layernorm(x + _L0_ffn_ref(x, L0_ffn_w1_w, L0_ffn_w1_s, L0_ffn_w2_w, L0_ffn_w2_s, L0_ffn_h1_w, L0_ffn_h1_s, L0_ffn_h2_w, L0_ffn_h2_s, L0_ffn_w3_w, L0_ffn_w3_s), axis=-1)
    x = _layernorm(x + _L1_attn_ref(x, L1_attn_w_q, L1_attn_b_q, L1_attn_w_k, L1_attn_b_k, L1_attn_v_w, L1_attn_out_w), axis=-1)
    x = _layernorm(x + _L1_xattn_ref(ctx_1024, x, ctx_1024, L1_xattn_Wq, L1_xattn_Wk, L1_xattn_Wv, L1_xattn_Wo, L1_xattn_bo), axis=-1)
    x = _layernorm(x + _L1_ffn_ref(x, L1_ffn_router_w, L1_ffn_w1, L1_ffn_w2), axis=-1)
    return x

_drawn_inputs = setup_inputs


def setup_inputs(seed=0):
    import zlib

    import numpy as np

    out = dict(_drawn_inputs(seed))
    spreads = {'L0_xattn_bq': (0.0, 0.419),
     'L0_xattn_bk': (0.0, 0.8),
     'L0_xattn_bv': (0.0, 0.1),
     'L0_xattn_bo': (0.0, 0.1),
     'L1_attn_b_q': (0.0, 0.8),
     'L1_attn_b_k': (0.0, 0.8)}
    factors = {'L0_attn_bq': 4.598,
     'L0_attn_bk': 6.723,
     'L0_ffn_w1_w': 8.0,
     'L0_ffn_w1_s': 8.0,
     'L0_ffn_w2_w': 8.0,
     'L0_ffn_w2_s': 8.0,
     'L0_ffn_h1_w': 8.0,
     'L0_ffn_h1_s': 8.0,
     'L0_ffn_h2_w': 8.0,
     'L0_ffn_h2_s': 8.0,
     'L0_ffn_w3_w': 8.0,
     'L0_ffn_w3_s': 8.0,
     'L1_attn_w_q': 8.0,
     'L1_attn_w_k': 8.0,
     'L1_xattn_bo': 6.933,
     'L1_ffn_router_w': 3.534,
     'L1_ffn_w1': 3.148,
     'L1_ffn_w2': 3.139}
    for name, (base, spread) in spreads.items():
        noise = np.random.default_rng([zlib.crc32(name.encode()), seed]).standard_normal(out[name].shape)
        drawn = base * np.exp(spread * noise) if base else spread * noise
        out[name] = jnp.asarray(drawn.astype(out[name].dtype))
    for name, factor in factors.items():
        out[name] = (out[name] * factor).astype(out[name].dtype)
    return out
```

```python
from contextlib import ExitStack

import concourse.bass as bass
from concourse import mybir

ALU = mybir.AluOpType
ACT = mybir.ActivationFunctionType
F32 = mybir.dt.float32
BF16 = mybir.dt.bfloat16
U32 = mybir.dt.uint32
AX_X = mybir.AxisListType.X

P = 128
NB = 32
H = 16
DK = 8
EPS_LN = 1e-5


class Tile:

    def __init__(self, i, off):
        self.i, self.off = i, off
        self.n = 4 * i + off

    def at(self, k):
        return Tile(self.i, self.off + k)

    @property
    def there(self):
        return not isinstance(self.i, int) or 0 <= self.n < NB

    def buf(self, m):
        return self.off % m

    def lap(self, m):
        return (4 // m) * self.i + self.off // m


def run_slots(eng, slot, first, last):
    for t in range(first, 4):
        slot(Tile(0, t))
    with eng.Fori(1, 7) as i:
        for u in range(4):
            slot(Tile(i, u))
    for t in range(28, last):
        slot(Tile(7, t - 28))


def done(eng, sem, tile, per=1, part=None):
    eng.wait_ge(sem, per * tile.n + (per if part is None else part))


def freed(eng, sem, tile, m, per=1):
    before = tile.at(-m)
    if before.there:
        done(eng, sem, before, per)


def loaded(eng, sems, tile):
    m = len(sems)
    eng.wait_ge(sems[tile.buf(m)], 16 * tile.lap(m) + 16)


class Phase:

    def __init__(self, nc, name, banks):
        self.nc, self.name, self.ctx, self.banks = nc, name, ExitStack(), list(banks)
        self.sems = []

    def sb(self, name, shape, dt=F32):
        return self.ctx.enter_context(self.nc.sbuf_tensor(f"{self.name}_{name}", shape, dt))

    def ps(self):
        return self.banks.pop(0)

    def sem(self, name, n=None):
        if n is not None:
            return [self.sem(f"{name}{k}") for k in range(n)]
        self.sems.append(self.nc.alloc_semaphore(f"{self.name}_{name}"))
        return self.sems[-1]

    def __enter__(self):
        return self

    def __exit__(self, *failed):
        self.ctx.close()
        self.nc.clear_and_free_semaphores(self.sems)
        self.nc.all_engine_barrier()


def softmax_attention(nc, name, banks, x_in, kv_in, x_out, wq, wk, wv, wo, bq, bk, bv, bo, ident, head_of_row):
    ph = Phase(nc, name, banks)
    with ph:
        sb, ps, sem = ph.sb, ph.ps, ph.sem
        idn = sb("idn", [P, P])
        hmask = sb("hmask", [P, H])
        wq_s, wk_s, wv_s, wo_s = (sb(f"w{k}", [P, P]) for k in "qkvo")
        bq_s, bk_s = sb("bq", [P, 1]), sb("bk", [P, 1])
        bv_s, bo_s = sb("bv", [P, P]), sb("bo", [P, P])
        pick = sb("pick", [P, H, P], BF16)
        half, eps = sb("half", [P, 1]), sb("eps", [P, 1])
        x_t = sb("x", [P, 4, P]); c_t = sb("c", [P, 4, P])
        xr_t = sb("xr", [P, 2, P]); xb_t = sb("xb", [P, 2, P])
        xcT = sb("xcT", [P, 2, 2, P])
        qT = sb("qT", [P, 4, P]); kT = sb("kT", [P, 2, P])
        kd = sb("kd", [P, 4, H, P])
        va = sb("va", [P, 4, H, 32])
        nmax = sb("nmax", [P, 2, P])
        nmaxT = sb("nmaxT", [P, 2, P], BF16)
        probs = sb("probs", [P, 2, H, P])
        o1 = sb("o1", [P, 2, 4, P])
        rden = sb("rden", [P, 2, 4, 4])
        o_tok = sb("o_tok", [P, 2, P]); oT = sb("oT", [P, 2, P])
        z = sb("z", [P, 2, P]); mark = sb("mark", [P, 1]); stats = sb("stats", [P, 2, 6]); mv = sb("mv", [P, 2, 2])
        vare = sb("vare", [P, 2, 1]); rstd = sb("rstd", [P, 2, 1]); y_t = sb("y", [P, 4, P])
        p_tr = ps()
        p_pj = ps()
        p_mx = [ps(), ps()]
        p_st = [ps(), ps()]
        p_pv = ps()
        p_on = ps()

        consts = sem("consts_loaded"); ready = sem("consts_ready"); blank = sem("blanks_ready")
        xl, cl, rl = sem("x_loaded", 4), sem("c_loaded", 4), sem("xr_loaded", 2)
        stored = sem("y_stored", 4)
        s_tr = sem("xc_transposed"); s_xc = sem("xc_copied")
        s_pj = sem("qkv_projected"); s_q = sem("q_ready"); s_k = sem("k_ready"); s_v = sem("v_ready")
        s_kd = sem("kd_ready"); s_sq = sem("scores_q"); s_mx = sem("max_ready")
        s_mt = sem("max_transposed"); s_mc = sem("max_copied")
        s_st = sem("scores_k"); s_ex = sem("exp_done"); s_pv = sem("pv_done"); s_o1 = sem("pv_copied")
        s_on = sem("pv_transposed"); s_rd = sem("reciprocals_ready"); s_ot = sem("o_normalised")
        s_oT = sem("o_transposed"); s_oc = sem("o_copied"); s_y = sem("y_projected")
        s_xb = sem("residual_ready"); s_z = sem("z_ready"); s_bs = sem("stats_ready")
        s_mv = sem("mean_var_ready"); s_ve = sem("var_eps_ready"); s_rs = sem("rstd_ready")
        s_ln = sem("normed")

        block = ph.ctx.enter_context(nc.Block())

        @block.sync
        def _(sp):
            for dst, src in ((idn[:, :], ident), (hmask[:, :], head_of_row), (wq_s[:, :], wq), (wk_s[:, :], wk),
                             (wv_s[:, :], wv), (wo_s[:, :], wo)):
                sp.dma_start(dst, src).then_inc(consts, 16)
            if bq is not None:
                sp.dma_start(bq_s[:, :], bq).then_inc(consts, 16)
                sp.dma_start(bk_s[:, :], bk).then_inc(consts, 16)
                sp.dma_start(bv_s[:, :], bv.partition_broadcast(P)).then_inc(consts, 16)
            sp.dma_start(bo_s[:, :], bo.partition_broadcast(P)).then_inc(consts, 16)

            def slot(t):
                a = t.at(4)
                if a.there:
                    freed(sp, s_tr, a, 4)
                    sp.dma_start(x_t[:, a.buf(4), :], x_in[a.n]).then_inc(xl[a.buf(4)], 16)
                    sp.dma_start(c_t[:, a.buf(4), :], kv_in[a.n]).then_inc(cl[a.buf(4)], 16)
                r = t.at(0)
                if r.there:
                    freed(sp, s_xb, r, 2)
                    sp.dma_start(xr_t[:, r.buf(2), :], x_in[r.n]).then_inc(rl[r.buf(2)], 16)
                o = t.at(-3)
                if o.there:
                    done(sp, s_ln, o)
                    sp.dma_start(x_out[o.n], y_t[:, o.buf(4), :]).then_inc(stored[o.buf(4)], 16)

            run_slots(sp, slot, -4, NB + 3)
            for k in range(4):
                sp.wait_ge(stored[k], 16 * NB // 4)

        n_consts = 16 * (10 if bq is not None else 7)

        @block.gpsimd
        def _(pool):
            pool.memset(va[:, :, :, :], 0.0).then_inc(blank, 1)
            pool.wait_ge(blank, 1)
            pool.memset(va[:, :, :, DK:DK + 1], 1.0).then_inc(blank, 1)
            pool.memset(nmax[:, :, :], 0.0).then_inc(blank, 1)
            pool.memset(half[:, :], -0.5).then_inc(blank, 1)
            pool.memset(eps[:, :], EPS_LN).then_inc(blank, 1)
            pool.wait_ge(blank, 5)
            pool.wait_ge(consts, n_consts)

            def slot(t):
                n = t.at(-3)
                if n.there:
                    done(pool, s_mv, n)
                    freed(pool, s_rs, n, 2)
                    pool.tensor_tensor(vare[:, n.buf(2), :], mv[:, n.buf(2), 1:2], eps[:, :], ALU.add).then_inc(s_ve, 1)
                    done(pool, s_ve, n)
                    freed(pool, s_ln, n, 2)
                    pool.tensor_tensor(rstd[:, n.buf(2), :], vare[:, n.buf(2), :], half[:, :],
                                       ALU.pow).then_inc(s_rs, 1)
                k = t.at(2)
                if k.there:
                    done(pool, s_k, k)
                    freed(pool, s_st, k, 4, 4)
                    pool.tensor_tensor(kd[:, k.buf(4), :, :],
                                       kT[:, k.buf(2), :].unsqueeze(1).broadcast_to([P, H, P]),
                                       hmask[:, :].unsqueeze(2).broadcast_to([P, H, P]),
                                       ALU.mult).then_inc(s_kd, 1)
                r = t.at(-1)
                if r.there:
                    loaded(pool, rl, r)
                    freed(pool, s_z, r, 2)
                    pool.tensor_tensor(xb_t[:, r.buf(2), :], xr_t[:, r.buf(2), :], bo_s[:, :],
                                       ALU.add).then_inc(s_xb, 1)

            run_slots(pool, slot, -2, NB + 3)

        @block.tensor
        def _(pe):
            pe.wait_ge(consts, n_consts)
            pe.wait_ge(ready, 1)
            pe.wait_ge(blank, 5)

            def slot(t):
                a = t.at(2)
                if a.there:
                    loaded(pe, xl, a)
                    loaded(pe, cl, a)
                    if t.there:
                        done(pe, s_mc, t)
                    elif a.at(-1).there:
                        done(pe, s_xc, a.at(-1))
                    pe.transpose(p_tr[:, 0:P], x_t[:, a.buf(4), :], idn[:, :])
                    pe.transpose(p_tr[:, P:2 * P], c_t[:, a.buf(4), :], idn[:, :]).then_inc(s_tr, 1)
                m = t.at(1)
                if m.there:
                    done(pe, s_kd, m)
                    done(pe, s_q, m)
                    q_hi = qT[:, m.buf(4), :].bitcast(BF16)[:, 1:2 * P:2]
                    for g in range(4):
                        if g >= 2:
                            done(pe, s_mx, m, 4, g - 1)
                        elif m.at(-1).there:
                            done(pe, s_mx, m.at(-1), 4, g + 3)
                        k_hi = kd[:, m.buf(4), 4 * g:4 * g + 4, :].bitcast(BF16)[:, :, 1:2 * P:2]
                        pe.matmul(p_mx[g % 2][:, :], q_hi, k_hi, start=True, stop=True).then_inc(s_sq, 1)
                v = t.at(-1)
                if v.there:
                    done(pe, s_ex, v, 4)
                    freed(pe, s_o1, v, 1)
                    for k in range(4):
                        for c in range(4):
                            h = 4 * c + k
                            mm = pe.matmul(p_pv[32 * c:32 * c + 32, k * P:(k + 1) * P], va[:, v.buf(4), h, :],
                                           probs[:, v.buf(2), h, :], start=True, stop=True)
                    mm.then_inc(s_pv, 1)
                if a.there:
                    done(pe, s_xc, a)
                    if t.at(-3).there:
                        done(pe, s_z, t.at(-3))
                    elif a.at(-1).there:
                        done(pe, s_v, a.at(-1))
                        done(pe, s_k, a.at(-1))
                    xT, cT = xcT[:, a.buf(2), 0, :], xcT[:, a.buf(2), 1, :]
                    pe.matmul(p_pj[:, 0:P], wq_s[:, :], xT, start=True, stop=True)
                    pe.matmul(p_pj[:, P:2 * P], wk_s[:, :], cT, start=True, stop=True)
                    pe.matmul(p_pj[:, 2 * P:3 * P], cT, wv_s[:, :], start=True, stop=True).then_inc(s_pj, 1)
                o = t.at(-2)
                if o.there:
                    done(pe, s_ot, o)
                    if a.there:
                        done(pe, s_xc, a)
                    elif t.there:
                        done(pe, s_mc, t)
                    else:
                        done(pe, s_oc, o.at(-1))
                    pe.transpose(p_tr[:, 0:P], o_tok[:, o.buf(2), :], idn[:, :]).then_inc(s_oT, 1)
                if t.there:
                    done(pe, s_mc, t)
                    for g in range(4):
                        if g >= 2:
                            done(pe, s_ex, t, 4, g - 1)
                        elif t.at(-1).there:
                            done(pe, s_ex, t.at(-1), 4, g + 3)
                        for j in range(4):
                            out = p_st[g % 2][:, j * P:(j + 1) * P]
                            pe.matmul(out, kd[:, t.buf(4), 4 * g + j, :], qT[:, t.buf(4), :],
                                      start=(j == 0), stop=False, skip_group_check=True)
                            mm = pe.matmul(out, pick[:, 4 * g + j, :], nmaxT[:, t.buf(2), :],
                                           start=False, stop=True, skip_group_check=True)
                        mm.then_inc(s_st, 1)
                if m.there:
                    done(pe, s_mx, m, 4)
                    if o.there:
                        done(pe, s_oc, o)
                    elif a.there:
                        done(pe, s_xc, a)
                    pe.transpose(p_tr[:, 0:P], nmax[:, m.buf(2), :], idn[:, :]).then_inc(s_mt, 1)
                if o.there:
                    done(pe, s_oc, o)
                    if a.there:
                        done(pe, s_v, a)
                        done(pe, s_k, a)
                    else:
                        done(pe, s_z, o.at(-1))
                    pe.matmul(p_pj[:, 0:P], oT[:, o.buf(2), :], wo_s[:, :], start=True, stop=True).then_inc(s_y, 1)
                if v.there:
                    done(pe, s_o1, v)
                    freed(pe, s_ot, v, 1)
                    for k in range(4):
                        mm = pe.transpose(p_on[:, k * P:(k + 1) * P], o1[:, v.buf(2), k, :], idn[:, :])
                    mm.then_inc(s_on, 1)

            run_slots(pe, slot, -2, NB + 2)

        @block.scalar
        def _(act):
            act.wait_ge(consts, n_consts)

            def slot(t):
                a = t.at(2)
                if a.there:
                    done(act, s_tr, a)
                    freed(act, s_pj, a, 2)
                    act.copy(xcT[:, a.buf(2), :, :], p_tr[:, 0:2 * P]).then_inc(s_xc, 1)
                    done(act, s_pj, a)
                    if a.at(-4).there:
                        done(act, s_st, a.at(-4), 4)
                    if bq is not None:
                        act.activation(qT[:, a.buf(4), :], p_pj[:, 0:P], ACT.Identity, bias=bq_s[:, :]).then_inc(s_q, 1)
                    else:
                        act.copy(qT[:, a.buf(4), :], p_pj[:, 0:P]).then_inc(s_q, 1)
                    freed(act, s_kd, a, 2)
                    if bq is not None:
                        act.activation(kT[:, a.buf(2), :], p_pj[:, P:2 * P], ACT.Identity, bias=bk_s[:, :]).then_inc(s_k, 1)
                    else:
                        act.copy(kT[:, a.buf(2), :], p_pj[:, P:2 * P]).then_inc(s_k, 1)
                if t.there:
                    freed(act, s_pv, t, 2)
                    for g in range(4):
                        done(act, s_st, t, 4, g + 1)
                        act.activation(probs[:, t.buf(2), 4 * g:4 * g + 4, :], p_st[g % 2][:, :], ACT.Exp,
                                       scale=float(DK) ** -0.5).then_inc(s_ex, 1)

            run_slots(act, slot, -2, NB)

        @block.vector
        def _(dve):
            dve.wait_ge(consts, n_consts)
            dve.wait_ge(blank, 5)
            dve.tensor_copy(pick[:, :, :], idn[:, 0:H].unsqueeze(2).broadcast_to([P, H, P])).then_inc(ready, 1)

            def slot(t):
                m = t.at(1)
                if m.there:
                    freed(dve, s_mt, m, 2)
                    for g in range(4):
                        done(dve, s_sq, m, 4, g + 1)
                        dve.tensor_reduce(nmax[:, m.buf(2), 4 * g:4 * g + 4],
                                          p_mx[g % 2][:, :].rearrange("p (h k) -> p h k", k=P), AX_X, ALU.max,
                                          negate=True).then_inc(s_mx, 1)
                v = t.at(-1)
                if v.there:
                    done(dve, s_pv, v)
                    freed(dve, s_on, v, 2)
                    dve.tensor_copy(o1[:, v.buf(2), :, :], p_pv[:, :]).then_inc(s_o1, 1)
                a = t.at(2)
                if a.there:
                    done(dve, s_pj, a)
                    done(dve, s_k, a)
                    freed(dve, s_pv, a, 4)
                    vin = p_pj[:, 2 * P:3 * P].rearrange("p (h d) -> p h d", d=DK)
                    if bq is not None:
                        dve.tensor_tensor(va[:, a.buf(4), :, 0:DK], vin,
                                          bv_s[:, :].rearrange("p (h d) -> p h d", d=DK), ALU.add).then_inc(s_v, 1)
                    else:
                        dve.tensor_copy(va[:, a.buf(4), :, 0:DK], vin).then_inc(s_v, 1)
                n = t.at(-3)
                if n.there:
                    done(dve, s_rs, n)
                    if n.at(-4).there:
                        loaded(dve, stored, n.at(-4))
                    dve.tensor_scalar(y_t[:, n.buf(4), :], z[:, n.buf(2), :], mv[:, n.buf(2), 0:1],
                                      rstd[:, n.buf(2), :], ALU.subtract, ALU.mult).then_inc(s_ln, 1)
                o = t.at(-2)
                if o.there:
                    done(dve, s_oT, o)
                    freed(dve, s_y, o, 2)
                    dve.tensor_copy(oT[:, o.buf(2), :], p_tr[:, 0:P]).then_inc(s_oc, 1)
                if m.there:
                    done(dve, s_mt, m)
                    if m.at(-2).there:
                        done(dve, s_st, m.at(-2), 4)
                    dve.tensor_copy(nmaxT[:, m.buf(2), :], p_tr[:, 0:P]).then_inc(s_mc, 1)
                if o.there:
                    done(dve, s_y, o)
                    done(dve, s_xb, o)
                    freed(dve, s_ln, o, 2)
                    dve.tensor_tensor(z[:, o.buf(2), :], p_pj[:, 0:P], xb_t[:, o.buf(2), :], ALU.add).then_inc(s_z, 1)
                    done(dve, s_z, o)
                    dve.bn_stats(stats[:, o.buf(2), :], z[:, o.buf(2), :]).then_inc(s_bs, 1)
                    done(dve, s_bs, o)
                    freed(dve, s_ve, o, 2)
                    dve.tensor_copy(mark[:, :], stats[:, o.buf(2), 0:1])
                    dve.bn_aggr(mv[:, o.buf(2), :], stats[:, o.buf(2), :]).then_inc(s_mv, 1)
                if v.there:
                    done(dve, s_on, v)
                    on = p_on[:, :].rearrange("p (k c e) -> p k c e", k=4, c=4)
                    freed(dve, s_ot, v, 2)
                    dve.reciprocal(rden[:, v.buf(2), :, :], on[:, :, :, DK]).then_inc(s_rd, 1)
                    done(dve, s_rd, v)
                    freed(dve, s_oT, v, 2)
                    dve.tensor_tensor(o_tok[:, v.buf(2), :].rearrange("p (c k d) -> p k c d", c=4, k=4),
                                      on[:, :, :, 0:DK],
                                      rden[:, v.buf(2), :, :].unsqueeze(3).broadcast_to([P, 4, 4, DK]),
                                      ALU.mult).then_inc(s_ot, 1)

            run_slots(dve, slot, -2, NB + 3)


def trig_attention(nc, name, banks, x_in, x_out, w_qk, b_qk, quarter, wv, wo, ident, head_of_row16, causal):
    LUT = 512
    STEP = 2.0 * 3.141592653589793 / LUT
    SCALE = 0.012271845
    ROUND = 1.5 * 2.0 ** 23
    ph = Phase(nc, name, banks)
    with ph:
        sb, ps, sem = ph.sb, ph.ps, ph.sem
        idn = sb("idn", [P, P])
        hmask = sb("hmask", [P, 8])
        tri = sb("tri", [P, P])
        wv_s, wo_s = sb("wv", [P, P]), sb("wo", [P, P])
        w_s, b_s, quar = sb("w", [P, 4]), sb("b", [P, 4]), sb("quar", [P, 1])
        wa, wr = sb("wa", [P, 4]), sb("wr", [P, 4])
        sc, bi = sb("sc", [P, 4]), sb("bi", [P, 4])
        half, eps = sb("half", [P, 1]), sb("eps", [P, 1])
        x_t = sb("x", [P, 4, P]); one = sb("one", [P, 8]); x2 = sb("x2", [P, 2, 2, 8, 2, DK]); xr_t = sb("xr", [P, 2, P]); xT = sb("xT", [P, 2, P])
        u = sb("u", [P, 2, 4, P]); nr = sb("nr", [P, 2, 4, P]); lap = sb("lap", [P, 2, 4, P])
        off = sb("off", [P, 2, 4, P]); an = sb("an", [P, 2, 4, P])
        sn = sb("sn", [P, 4, 4, P])
        kd = sb("kd", [P, 2, H, P])
        va = sb("va", [P, 4, H, 32])
        probs = sb("probs", [P, 2, H, P])
        o1 = sb("o1", [P, 2, 4, P]); rden = sb("rden", [P, 2, 4, 4])
        o_tok = sb("o_tok", [P, 2, P]); oT = sb("oT", [P, 2, P])
        z = sb("z", [P, 2, P]); mark = sb("mark", [P, 1]); stats = sb("stats", [P, 2, 6]); mv = sb("mv", [P, 2, 2])
        vare = sb("vare", [P, 2, 1]); rstd = sb("rstd", [P, 2, 1]); y_t = sb("y", [P, 4, P])
        p_tr, p_oT, p_pj = ps(), ps(), ps()
        p_st = [ps(), ps(), ps()]
        p_pv, p_on = ps(), ps()

        consts = sem("consts_loaded"); ready = sem("consts_ready"); blank = sem("blanks_ready")
        xl, rl, stored = sem("x_loaded", 4), sem("xr_loaded", 2), sem("y_stored", 4)
        s_x2 = sem("x_doubled"); s_tr = sem("x_transposed"); s_xc = sem("x_copied"); s_u = sem("angles_ready")
        s_nr = sem("angles_rounded"); s_lp = sem("laps_counted"); s_of = sem("laps_scaled"); s_an = sem("angles_reduced")
        s_sn = sem("sines_ready"); s_kd = sem("kd_ready")
        s_pj = sem("v_projected"); s_v = sem("v_ready")
        s_st = sem("scores"); s_ex = sem("exp_done"); s_mk = sem("probs_masked"); s_pv = sem("pv_done")
        s_o1 = sem("pv_copied"); s_on = sem("pv_transposed"); s_rd = sem("reciprocals_ready")
        s_ot = sem("o_normalised"); s_oT = sem("o_transposed"); s_oc = sem("o_copied"); s_y = sem("y_projected")
        s_z = sem("z_ready"); s_bs = sem("stats_ready"); s_mv = sem("mean_var_ready")
        s_ve = sem("var_eps_ready"); s_rs = sem("rstd_ready"); s_ln = sem("normed")

        block = ph.ctx.enter_context(nc.Block())
        n_consts = 16 * 8

        @block.sync
        def _(sp):
            for dst, src in ((idn, ident), (hmask, head_of_row16), (tri, causal), (wv_s, wv), (wo_s, wo),
                             (w_s, w_qk), (b_s, b_qk), (quar, quarter)):
                sp.dma_start(dst[:, :], src).then_inc(consts, 16)

            def slot(t):
                a = t.at(4)
                if a.there:
                    freed(sp, s_tr, a, 4)
                    sp.dma_start(x_t[:, a.buf(4), :], x_in[a.n]).then_inc(xl[a.buf(4)], 16)
                if t.there:
                    freed(sp, s_z, t, 2)
                    sp.dma_start(xr_t[:, t.buf(2), :], x_in[t.n]).then_inc(rl[t.buf(2)], 16)
                o = t.at(-3)
                if o.there:
                    done(sp, s_ln, o)
                    sp.dma_start(x_out[o.n], y_t[:, o.buf(4), :]).then_inc(stored[o.buf(4)], 16)

            run_slots(sp, slot, -4, NB + 3)
            for k in range(4):
                sp.wait_ge(stored[k], 16 * NB // 4)

        @block.gpsimd
        def _(pool):
            pool.memset(va[:, :, :, :], 0.0).then_inc(blank, 1)
            pool.wait_ge(blank, 1)
            pool.memset(va[:, :, :, DK:DK + 1], 1.0).then_inc(blank, 1)
            pool.memset(half[:, :], -0.5).then_inc(blank, 1)
            pool.memset(eps[:, :], EPS_LN).then_inc(blank, 1)
            pool.memset(one[:, :], 1.0).then_inc(blank, 1)
            pool.wait_ge(blank, 5)
            pool.wait_ge(consts, n_consts)

            def slot(t):
                n = t.at(-3)
                if n.there:
                    done(pool, s_mv, n)
                    freed(pool, s_rs, n, 2)
                    pool.tensor_tensor(vare[:, n.buf(2), :], mv[:, n.buf(2), 1:2], eps[:, :], ALU.add).then_inc(s_ve, 1)
                    done(pool, s_ve, n)
                    freed(pool, s_ln, n, 2)
                    pool.tensor_tensor(rstd[:, n.buf(2), :], vare[:, n.buf(2), :], half[:, :],
                                       ALU.pow).then_inc(s_rs, 1)
                a = t.at(3)
                if a.there:
                    loaded(pool, xl, a)
                    freed(pool, s_tr, a, 2)
                    for f in range(2):
                        pool.tensor_tensor(x2[:, a.buf(2), f],
                                           x_t[:, a.buf(4), 64 * f:64 * f + 64].rearrange("p (h d) -> p h d", d=DK)
                                           .unsqueeze(2).broadcast_to([P, 8, 2, DK]),
                                           one[:, :].unsqueeze(2).unsqueeze(3).broadcast_to([P, 8, 2, DK]),
                                           ALU.mult).then_inc(s_x2, 1)
                k = t.at(1)
                if k.there:
                    done(pool, s_sn, k)
                    freed(pool, s_st, k, 2, 4)
                    for f in range(2):
                        pool.tensor_tensor(kd[:, k.buf(2), 8 * f:8 * f + 8, :],
                                           sn[:, k.buf(4), 2 + f, :].unsqueeze(1).broadcast_to([P, 8, P]),
                                           hmask[:, :].unsqueeze(2).broadcast_to([P, 8, P]),
                                           ALU.mult).then_inc(s_kd, 1)

            run_slots(pool, slot, -3, NB + 3)

        @block.tensor
        def _(pe):
            pe.wait_ge(consts, n_consts)
            pe.wait_ge(blank, 5)

            def slot(t):
                a = t.at(2)
                if a.there:
                    loaded(pe, xl, a)
                    freed(pe, s_u, a, 1, 4)
                    freed(pe, s_xc, a, 1)
                    done(pe, s_x2, a, 2)
                    for f in range(2):
                        pe.transpose(p_tr[:, f * P:(f + 1) * P],
                                     x2[:, a.buf(2), f].rearrange("p h c d -> p (h c d)"), idn[:, :])
                    pe.transpose(p_tr[:, 2 * P:3 * P], x_t[:, a.buf(4), :], idn[:, :]).then_inc(s_tr, 1)
                v = t.at(-1)
                if v.there:
                    done(pe, s_mk, v, 4)
                    freed(pe, s_o1, v, 1)
                    for k in range(4):
                        for c in range(4):
                            h = 4 * c + k
                            mm = pe.matmul(p_pv[32 * c:32 * c + 32, k * P:(k + 1) * P], va[:, v.buf(4), h, :],
                                           probs[:, v.buf(2), h, :], start=True, stop=True)
                    mm.then_inc(s_pv, 1)
                if a.there:
                    done(pe, s_xc, a)
                    if t.at(-3).there:
                        done(pe, s_z, t.at(-3))
                    elif a.at(-1).there:
                        done(pe, s_v, a.at(-1))
                    pe.matmul(p_pj[:, 0:P], xT[:, a.buf(2), :], wv_s[:, :], start=True, stop=True).then_inc(s_pj, 1)
                o = t.at(-2)
                if o.there:
                    done(pe, s_ot, o)
                    freed(pe, s_oc, o, 1)
                    pe.transpose(p_oT[:, 0:P], o_tok[:, o.buf(2), :], idn[:, :]).then_inc(s_oT, 1)
                if t.there:
                    done(pe, s_kd, t, 2)
                    for g in range(4):
                        if g == 3:
                            done(pe, s_ex, t, 4, 1)
                        elif t.at(-1).there:
                            done(pe, s_ex, t.at(-1), 4, 4 if g == 0 else g + 1)
                        for j in range(4):
                            h = 4 * g + j
                            mm = pe.matmul(p_st[g % 3][:, j * P:(j + 1) * P], kd[:, t.buf(2), h, :],
                                           sn[:, t.buf(4), h // 8, :], start=True, stop=True)
                        mm.then_inc(s_st, 1)
                if o.there:
                    done(pe, s_oc, o)
                    if a.there:
                        done(pe, s_v, a)
                    else:
                        done(pe, s_z, o.at(-1))
                    pe.matmul(p_pj[:, 0:P], oT[:, o.buf(2), :], wo_s[:, :], start=True, stop=True).then_inc(s_y, 1)
                if v.there:
                    done(pe, s_o1, v)
                    freed(pe, s_ot, v, 1)
                    for k in range(4):
                        mm = pe.transpose(p_on[:, k * P:(k + 1) * P], o1[:, v.buf(2), k, :], idn[:, :])
                    mm.then_inc(s_on, 1)

            run_slots(pe, slot, -2, NB + 2)

        @block.scalar
        def _(act):
            act.wait_ge(ready, 5)

            def slot(t):
                a = t.at(2)
                if a.there:
                    done(act, s_tr, a)
                    freed(act, s_pj, a, 2)
                    act.copy(xT[:, a.buf(2), :], p_tr[:, 2 * P:3 * P]).then_inc(s_xc, 1)
                    freed(act, s_nr, a, 2)
                    for f in range(4):
                        act.activation(u[:, a.buf(2), f, :], p_tr[:, (f % 2) * P:(f % 2 + 1) * P], ACT.Identity,
                                       scale=sc[:, f:f + 1], bias=bi[:, f:f + 1]).then_inc(s_u, 1)
                if t.there:
                    freed(act, s_pv, t, 2)
                    for g in range(4):
                        done(act, s_st, t, 4, g + 1)
                        act.activation(probs[:, t.buf(2), 4 * g:4 * g + 4, :], p_st[g % 3][:, :], ACT.Exp,
                                       scale=float(2 * DK) ** -0.5).then_inc(s_ex, 1)
                if a.there:
                    done(act, s_an, a)
                    if a.at(-4).there:
                        done(act, s_st, a.at(-4), 4)
                        done(act, s_kd, a.at(-4), 2)
                    act.activation(sn[:, a.buf(4), :, :], an[:, a.buf(2), :, :], ACT.Sin, scale=SCALE).then_inc(s_sn, 1)

            run_slots(act, slot, -2, NB)

        @block.vector
        def _(dve):
            dve.wait_ge(consts, n_consts)
            dve.wait_ge(blank, 5)
            dve.scalar_tensor_tensor(wa[:, :], w_s[:, :], -1.0, w_s[:, :], ALU.mult, ALU.max).then_inc(ready, 1)
            dve.wait_ge(ready, 1)
            dve.tensor_scalar(wa[:, :], wa[:, :], 1.0, None, ALU.add).then_inc(ready, 1)
            dve.wait_ge(ready, 2)
            dve.reciprocal(wr[:, :], wa[:, :]).then_inc(ready, 1)
            dve.wait_ge(ready, 3)
            dve.tensor_scalar(sc[:, :], wr[:, :], 1.0 / STEP, None, ALU.mult).then_inc(ready, 1)
            dve.tensor_scalar(bi[:, :], b_s[:, :], 1.0 / STEP, quar[:, :], ALU.mult, ALU.add).then_inc(ready, 1)

            def slot(t):
                a = t.at(2)
                if a.there:
                    done(dve, s_u, a, 4)
                    freed(dve, s_an, a, 2)
                    b = a.buf(2)
                    dve.tensor_scalar(nr[:, b], u[:, b], ROUND, ROUND, ALU.add, ALU.subtract).then_inc(s_nr, 1)
                    done(dve, s_nr, a)
                    dve.tensor_scalar(lap[:, b], nr[:, b], 1.0 / LUT, ROUND, ALU.mult, ALU.add).then_inc(s_lp, 1)
                    done(dve, s_lp, a)
                    dve.tensor_scalar(off[:, b], lap[:, b], ROUND, -float(LUT), ALU.subtract, ALU.mult).then_inc(s_of, 1)
                    done(dve, s_of, a)
                    freed(dve, s_sn, a, 2)
                    dve.tensor_tensor(an[:, b], nr[:, b], off[:, b], ALU.add).then_inc(s_an, 1)
                v = t.at(-1)
                if v.there:
                    done(dve, s_pv, v)
                    freed(dve, s_on, v, 2)
                    dve.tensor_copy(o1[:, v.buf(2), :, :], p_pv[:, :]).then_inc(s_o1, 1)
                if a.there:
                    done(dve, s_pj, a)
                    freed(dve, s_pv, a, 4)
                    dve.tensor_copy(va[:, a.buf(4), :, 0:DK],
                                    p_pj[:, 0:P].rearrange("p (h d) -> p h d", d=DK)).then_inc(s_v, 1)
                n = t.at(-3)
                if n.there:
                    done(dve, s_rs, n)
                    if n.at(-4).there:
                        loaded(dve, stored, n.at(-4))
                    dve.tensor_scalar(y_t[:, n.buf(4), :], z[:, n.buf(2), :], mv[:, n.buf(2), 0:1],
                                      rstd[:, n.buf(2), :], ALU.subtract, ALU.mult).then_inc(s_ln, 1)
                o = t.at(-2)
                if o.there:
                    done(dve, s_oT, o)
                    freed(dve, s_y, o, 2)
                    dve.tensor_copy(oT[:, o.buf(2), :], p_oT[:, 0:P]).then_inc(s_oc, 1)
                if t.there:
                    for g in range(4):
                        done(dve, s_ex, t, 4, g + 1)
                        pr = probs[:, t.buf(2), 4 * g:4 * g + 4, :]
                        dve.tensor_tensor(pr, pr, tri[:, :].unsqueeze(1).broadcast_to([P, 4, P]),
                                          ALU.mult).then_inc(s_mk, 1)
                if o.there:
                    done(dve, s_y, o)
                    loaded(dve, rl, o)
                    freed(dve, s_ln, o, 2)
                    dve.tensor_tensor(z[:, o.buf(2), :], p_pj[:, 0:P], xr_t[:, o.buf(2), :], ALU.add).then_inc(s_z, 1)
                    done(dve, s_z, o)
                    dve.bn_stats(stats[:, o.buf(2), :], z[:, o.buf(2), :]).then_inc(s_bs, 1)
                    done(dve, s_bs, o)
                    freed(dve, s_ve, o, 2)
                    dve.tensor_copy(mark[:, :], stats[:, o.buf(2), 0:1])
                    dve.bn_aggr(mv[:, o.buf(2), :], stats[:, o.buf(2), :]).then_inc(s_mv, 1)
                if v.there:
                    done(dve, s_on, v)
                    on = p_on[:, :].rearrange("p (k c e) -> p k c e", k=4, c=4)
                    freed(dve, s_ot, v, 2)
                    dve.reciprocal(rden[:, v.buf(2), :, :], on[:, :, :, DK]).then_inc(s_rd, 1)
                    done(dve, s_rd, v)
                    freed(dve, s_oT, v, 2)
                    dve.tensor_tensor(o_tok[:, v.buf(2), :].rearrange("p (c k d) -> p k c d", c=4, k=4),
                                      on[:, :, :, 0:DK],
                                      rden[:, v.buf(2), :, :].unsqueeze(3).broadcast_to([P, 4, 4, DK]),
                                      ALU.mult).then_inc(s_ot, 1)

            run_slots(dve, slot, -2, NB + 3)


def linear_attention(nc, name, banks, x_in, x_out, wq, wk, wv, wo, bq, bk, bv, bo, feat, norm, ident, own_head):
    M = 32
    G = 4
    VW = DK + 1
    ph = Phase(nc, name, banks)
    with ph:
        sb, ps, sem = ph.sb, ph.ps, ph.sem
        idn = sb("idn", [P, P]); own = sb("own", [P, H, VW])
        wq_s, wk_s, wv_s, wo_s = (sb(f"w{k}", [P, P]) for k in "qkvo")
        bq_s, bk_s = sb("bq", [P, 1]), sb("bk", [P, 1])
        bv_s, bo_s = sb("bv", [P, P]), sb("bo", [P, P])
        ft_raw, ft, nm = sb("ft_raw", [P, H * M]), sb("ft", [P, H * M]), sb("nm", [P, H * M])
        half, eps = sb("half", [P, 1]), sb("eps", [P, 1]); lnm = sb("lnm", [P, 1]); tiny = sb("tiny", [P, P])
        x_t = sb("x", [P, 4, P]); xr_t = sb("xr", [P, 2, P]); xb_t = sb("xb", [P, 2, P])
        xT = sb("xT", [P, 2, P])
        qT = sb("qT", [P, 2, P]); qs = sb("qs", [P, 2, P]); kT = sb("kT", [P, 2, P]); ks = sb("ks", [P, 2, P])
        va = sb("va", [P, 4, H, VW])
        ek = sb("ek", [P, 2, H * M]); eq = sb("eq", [P, 2, G, P])
        kvm = sb("kvm", [P, 2, H, VW]); rden = sb("rden", [P, 2, H])
        o_tok = sb("o_tok", [P, 2, P]); oT = sb("oT", [P, 2, P])
        z = sb("z", [P, 2, P]); mark = sb("mark", [P, 1]); stats = sb("stats", [P, 2, 6]); mv = sb("mv", [P, 2, 2])
        vare = sb("vare", [P, 2, 1]); rstd = sb("rstd", [P, 2, 1]); y_t = sb("y", [P, 4, P])
        p_tr, p_oT, p_pj, p_y = ps(), ps(), ps(), ps()
        p_zq, p_zk, p_kv, p_on = ps(), ps(), ps(), ps()

        consts = sem("consts_loaded"); ready = sem("feat_ready"); blank = sem("blanks_ready")
        xl, rl, stored = sem("x_loaded", 4), sem("xr_loaded", 2), sem("y_stored", 4)
        s_tr = sem("x_transposed"); s_xc = sem("x_copied"); s_pj = sem("qkv_projected")
        s_q = sem("q_and_k_ready"); s_v = sem("v_ready"); s_zq = sem("zq_done"); s_zk = sem("zk_done")
        s_eq = sem("q_features"); s_ek = sem("k_features"); s_kv = sem("kv_done"); s_kc = sem("kv_copied")
        s_on = sem("outputs_done"); s_rd = sem("reciprocals_ready")
        s_ot = sem("o_normalised"); s_oT = sem("o_transposed"); s_oc = sem("o_copied"); s_y = sem("y_projected")
        s_xb = sem("residual_ready"); s_z = sem("z_ready"); s_bs = sem("stats_ready"); s_mv = sem("mean_var_ready")
        s_ve = sem("var_eps_ready"); s_rs = sem("rstd_ready"); s_ln = sem("normed")

        block = ph.ctx.enter_context(nc.Block())
        n_consts = 16 * 12

        @block.sync
        def _(sp):
            for dst, src in ((idn[:, :], ident), (own[:, :, :], own_head), (wq_s[:, :], wq), (wk_s[:, :], wk),
                             (wv_s[:, :], wv), (wo_s[:, :], wo), (bq_s[:, :], bq), (bk_s[:, :], bk),
                             (bv_s[:, :], bv.partition_broadcast(P)), (bo_s[:, :], bo.partition_broadcast(P)),
                             (ft_raw[:, :], feat), (nm[:, :], norm)):
                sp.dma_start(dst, src).then_inc(consts, 16)

            def slot(t):
                a = t.at(4)
                if a.there:
                    freed(sp, s_tr, a, 4)
                    sp.dma_start(x_t[:, a.buf(4), :], x_in[a.n]).then_inc(xl[a.buf(4)], 16)
                if t.there:
                    freed(sp, s_xb, t, 2)
                    sp.dma_start(xr_t[:, t.buf(2), :], x_in[t.n]).then_inc(rl[t.buf(2)], 16)
                o = t.at(-2)
                if o.there:
                    done(sp, s_ln, o)
                    sp.dma_start(x_out[o.n], y_t[:, o.buf(4), :]).then_inc(stored[o.buf(4)], 16)

            run_slots(sp, slot, -4, NB + 2)
            for k in range(4):
                sp.wait_ge(stored[k], 16 * NB // 4)

        @block.gpsimd
        def _(pool):
            pool.memset(va[:, :, :, DK:DK + 1], 1.0).then_inc(blank, 1)
            pool.memset(half[:, :], -0.5).then_inc(blank, 1)
            pool.memset(eps[:, :], EPS_LN).then_inc(blank, 1)
            pool.memset(lnm[:, :], -1.7328679513998633).then_inc(blank, 1)
            pool.memset(tiny[:, :], 1e-6 / M ** 0.5).then_inc(blank, 1)
            pool.wait_ge(blank, 5)
            pool.wait_ge(consts, n_consts)

            def slot(t):
                n = t.at(-2)
                if n.there:
                    done(pool, s_mv, n)
                    freed(pool, s_rs, n, 2)
                    pool.tensor_tensor(vare[:, n.buf(2), :], mv[:, n.buf(2), 1:2], eps[:, :], ALU.add).then_inc(s_ve, 1)
                    done(pool, s_ve, n)
                    freed(pool, s_ln, n, 2)
                    pool.tensor_tensor(rstd[:, n.buf(2), :], vare[:, n.buf(2), :], half[:, :],
                                       ALU.pow).then_inc(s_rs, 1)
                if t.there:
                    loaded(pool, rl, t)
                    freed(pool, s_z, t, 2)
                    pool.tensor_tensor(xb_t[:, t.buf(2), :], xr_t[:, t.buf(2), :], bo_s[:, :],
                                       ALU.add).then_inc(s_xb, 1)

            run_slots(pool, slot, 0, NB + 2)

        @block.tensor
        def _(pe):
            pe.wait_ge(consts, n_consts)
            pe.wait_ge(blank, 5)
            pe.wait_ge(ready, 1)

            def slot(t):
                a = t.at(2)
                if a.there:
                    loaded(pe, xl, a)
                    freed(pe, s_xc, a, 1)
                    pe.transpose(p_tr[:, 0:P], x_t[:, a.buf(4), :], idn[:, :]).then_inc(s_tr, 1)
                if t.there:
                    done(pe, s_ek, t)
                    freed(pe, s_kc, t, 1)
                    pe.matmul(p_kv[:, 0:H * VW], tiny[:, :], va[:, t.buf(4)], start=True, stop=False,
                              skip_group_check=True)
                    for g in range(G):
                        mm = pe.matmul(p_kv[:, 4 * g * VW:4 * (g + 1) * VW], ek[:, t.buf(2), g * P:(g + 1) * P],
                                       va[:, t.buf(4), 4 * g:4 * g + 4, :], start=False, stop=True,
                                       skip_group_check=True)
                    mm.then_inc(s_kv, 1)
                if a.there:
                    done(pe, s_xc, a)
                    freed(pe, s_v, a, 1)
                    freed(pe, s_q, a, 1, 4)
                    x = xT[:, a.buf(2), :]
                    pe.matmul(p_pj[:, 0:P], wq_s[:, :], x, start=True, stop=True)
                    pe.matmul(p_pj[:, P:2 * P], wk_s[:, :], x, start=True, stop=True)
                    pe.matmul(p_pj[:, 2 * P:3 * P], x, wv_s[:, :], start=True, stop=True).then_inc(s_pj, 1)
                o = t.at(-1)
                if o.there:
                    done(pe, s_ot, o)
                    freed(pe, s_oc, o, 1)
                    pe.transpose(p_oT[:, 0:P], o_tok[:, o.buf(2), :], idn[:, :]).then_inc(s_oT, 1)
                b = t.at(1)
                if b.there:
                    done(pe, s_q, b, 4)
                    freed(pe, s_eq, b, 1)
                    for g in range(G):
                        out = p_zq[:, g * P:(g + 1) * P]
                        pe.matmul(out, ft[:, g * P:(g + 1) * P], qT[:, b.buf(2), :], start=True, stop=False)
                        mm = pe.matmul(out, nm[:, g * P:(g + 1) * P], qs[:, b.buf(2), :], start=False, stop=True)
                    mm.then_inc(s_zq, 1)
                if t.there:
                    done(pe, s_kc, t)
                    done(pe, s_eq, t)
                    freed(pe, s_ot, t, 1)
                    pe.matmul(p_on[:, 0:H * VW], tiny[:, :], kvm[:, t.buf(2)], start=True, stop=False,
                              skip_group_check=True)
                    for g in range(G):
                        mm = pe.matmul(p_on[:, 4 * g * VW:4 * (g + 1) * VW], eq[:, t.buf(2), g, :],
                                       kvm[:, t.buf(2), 4 * g:4 * g + 4, :], start=False, stop=True,
                                       skip_group_check=True)
                    mm.then_inc(s_on, 1)
                if b.there:
                    freed(pe, s_ek, b, 1)
                    pe.matmul(p_zk[:, :], kT[:, b.buf(2), :], ft[:, :], start=True, stop=False)
                    pe.matmul(p_zk[:, :], ks[:, b.buf(2), :], nm[:, :], start=False, stop=True).then_inc(s_zk, 1)
                if o.there:
                    done(pe, s_oc, o)
                    freed(pe, s_z, o, 1)
                    pe.matmul(p_y[:, 0:P], oT[:, o.buf(2), :], wo_s[:, :], start=True, stop=True).then_inc(s_y, 1)

            run_slots(pe, slot, -2, NB + 1)

        @block.scalar
        def _(act):
            act.wait_ge(consts, n_consts)
            act.wait_ge(blank, 5)

            def slot(t):
                a = t.at(2)
                if a.there:
                    done(act, s_tr, a)
                    freed(act, s_pj, a, 2)
                    act.copy(xT[:, a.buf(2), :], p_tr[:, 0:P]).then_inc(s_xc, 1)
                    done(act, s_pj, a)
                    freed(act, s_zk, a, 2)
                    for dst, fn, k, bias in ((qT, ACT.Identity, 0, bq_s), (qs, ACT.Square, 0, bq_s),
                                             (kT, ACT.Identity, 1, bk_s), (ks, ACT.Square, 1, bk_s)):
                        act.activation(dst[:, a.buf(2), :], p_pj[:, k * P:(k + 1) * P], fn,
                                       bias=bias[:, :]).then_inc(s_q, 1)
                b = t.at(1)
                if b.there:
                    done(act, s_zq, b)
                    freed(act, s_on, b, 2)
                    act.activation(eq[:, b.buf(2)], p_zq[:, :], ACT.Exp, bias=lnm[:, :]).then_inc(s_eq, 1)
                    done(act, s_zk, b)
                    freed(act, s_kv, b, 2)
                    act.activation(ek[:, b.buf(2), :], p_zk[:, :], ACT.Exp, bias=lnm[:, :]).then_inc(s_ek, 1)

            run_slots(act, slot, -2, NB)

        @block.vector
        def _(dve):
            dve.wait_ge(consts, n_consts)
            dve.wait_ge(blank, 5)
            dve.tensor_scalar(ft[:, :], ft_raw[:, :], float(DK) ** -0.25, None, ALU.mult).then_inc(ready, 1)

            def slot(t):
                if t.there:
                    done(dve, s_kv, t)
                    freed(dve, s_on, t, 2)
                    dve.tensor_tensor(kvm[:, t.buf(2)], p_kv[:, 0:H * VW], own[:, :, :],
                                      ALU.mult).then_inc(s_kc, 1)
                a = t.at(2)
                if a.there:
                    done(dve, s_pj, a)
                    done(dve, s_q, a, 4)
                    freed(dve, s_kv, a, 4)
                    dve.tensor_tensor(va[:, a.buf(4), :, 0:DK], p_pj[:, 2 * P:3 * P].rearrange("p (h d) -> p h d", d=DK),
                                      bv_s[:, :].rearrange("p (h d) -> p h d", d=DK), ALU.add).then_inc(s_v, 1)
                n = t.at(-2)
                if n.there:
                    done(dve, s_rs, n)
                    if n.at(-4).there:
                        loaded(dve, stored, n.at(-4))
                    dve.tensor_scalar(y_t[:, n.buf(4), :], z[:, n.buf(2), :], mv[:, n.buf(2), 0:1],
                                      rstd[:, n.buf(2), :], ALU.subtract, ALU.mult).then_inc(s_ln, 1)
                o = t.at(-1)
                if o.there:
                    done(dve, s_oT, o)
                    freed(dve, s_y, o, 2)
                    dve.tensor_copy(oT[:, o.buf(2), :], p_oT[:, 0:P]).then_inc(s_oc, 1)
                if t.there:
                    done(dve, s_on, t)
                    on = p_on[:, 0:H * VW].rearrange("p (h e) -> p h e", e=VW)
                    freed(dve, s_ot, t, 2)
                    dve.reciprocal(rden[:, t.buf(2), :], on[:, :, DK]).then_inc(s_rd, 1)
                    done(dve, s_rd, t)
                    freed(dve, s_oT, t, 2)
                    dve.tensor_tensor(o_tok[:, t.buf(2), :].rearrange("p (h d) -> p h d", d=DK), on[:, :, 0:DK],
                                      rden[:, t.buf(2), :].unsqueeze(2).broadcast_to([P, H, DK]),
                                      ALU.mult).then_inc(s_ot, 1)
                if o.there:
                    done(dve, s_y, o)
                    done(dve, s_xb, o)
                    freed(dve, s_ln, o, 2)
                    dve.tensor_tensor(z[:, o.buf(2), :], p_y[:, 0:P], xb_t[:, o.buf(2), :], ALU.add).then_inc(s_z, 1)
                    done(dve, s_z, o)
                    dve.bn_stats(stats[:, o.buf(2), :], z[:, o.buf(2), :]).then_inc(s_bs, 1)
                    done(dve, s_bs, o)
                    freed(dve, s_ve, o, 2)
                    dve.tensor_copy(mark[:, :], stats[:, o.buf(2), 0:1])
                    dve.bn_aggr(mv[:, o.buf(2), :], stats[:, o.buf(2), :]).then_inc(s_mv, 1)

            run_slots(dve, slot, -2, NB + 2)


CT = 4
NC = NB // CT


def run_chunks(eng, body):
    body(0)
    with eng.Fori(1, NC) as c:
        body(c)


def later(c):
    return not isinstance(c, int) or c > 0


def feed_forward(nc, name, banks, x_in, x_out, w1, w2, h1, h2, w3, s_hidden, s_out, ident):
    F = 4
    ph = Phase(nc, name, banks)
    with ph:
        sb, ps, sem = ph.sb, ph.ps, ph.sem
        idn = sb("idn", [P, P])
        w1_s, w2_s = sb("w1", [P, F * P]), sb("w2", [P, F * P])
        h1_s, h2_s, w3_s = sb("h1", [P, F, F * P]), sb("h2", [P, F, F * P]), sb("w3", [P, F, P])
        sh = sb("sh", [P, 4, F])
        so = sb("so", [P, P]); w3_o = sb("w3o", [P, F, P])
        half, eps = sb("half", [P, CT]), sb("eps", [P, CT])
        x_t = sb("x", [P, CT, P]); xr_t = sb("xr", [P, CT, P]); xT = sb("xT", [P, CT, P])
        gate = sb("gate", [P, 2, CT * P]); a0 = sb("a0", [P, F, CT * P])
        a1 = sb("a1", [P, F, CT * P]); a2 = sb("a2", [P, F, CT * P])
        z = sb("z", [P, CT, P]); mark = sb("mark", [P, CT]); stats = sb("stats", [P, CT, 6]); mv = sb("mv", [P, CT, 2])
        vare = sb("vare", [P, CT]); rstd = sb("rstd", [P, CT]); y_t = sb("y", [P, CT, P])
        p_u = [ps(), ps()]; p_v = [ps(), ps()]
        p_h = [ps(), ps()]; p_tr, p_y = ps(), ps()

        consts = sem("consts_loaded"); ready = sem("w3_scaled"); blank = sem("blanks_ready")
        xl, rl, stored = sem("x_loaded"), sem("xr_loaded"), sem("y_stored")
        s_tr = sem("x_transposed"); s_xc = sem("x_copied")
        s_u = sem("u_done"); s_v = sem("v_done"); s_g = sem("gate_ready"); s_a0 = sem("a0_ready")
        s_m1 = sem("h1_done"); s_a1 = sem("a1_ready"); s_m2 = sem("h2_done"); s_a2 = sem("a2_ready")
        s_y = sem("y_done"); s_z = sem("z_ready"); s_bs = sem("stats_ready"); s_mv = sem("mean_var_ready")
        s_ve = sem("var_eps_ready"); s_rs = sem("rstd_ready"); s_ln = sem("normed")

        block = ph.ctx.enter_context(nc.Block())
        n_consts = 16 * 8

        @block.sync
        def _(sp):
            for dst, src in ((idn[:, :], ident), (w1_s[:, :], w1), (w2_s[:, :], w2), (h1_s[:, :, :], h1),
                             (h2_s[:, :, :], h2), (w3_s[:, :, :], w3), (sh[:, :, :], s_hidden),
                             (so[:, :], s_out.partition_broadcast(P))):
                sp.dma_start(dst, src).then_inc(consts, 16)

            def body(c):
                if later(c):
                    sp.wait_ge(s_tr, c)
                sp.dma_start(x_t[:, :, :], x_in[c].rearrange("t p d -> p t d")).then_inc(xl, 16)
                if later(c):
                    sp.wait_ge(s_ln, 4 * c)
                    sp.dma_start(x_out[c - 1].rearrange("t p d -> p t d"), y_t[:, :, :]).then_inc(stored, 16)
                sp.dma_start(xr_t[:, :, :], x_in[c].rearrange("t p d -> p t d")).then_inc(rl, 16)

            run_chunks(sp, body)
            sp.wait_ge(s_ln, 4 * NC)
            sp.dma_start(x_out[NC - 1].rearrange("t p d -> p t d"), y_t[:, :, :]).then_inc(stored, 16)
            sp.wait_ge(stored, 16 * NC)

        @block.gpsimd
        def _(pool):
            pool.memset(half[:, :], -0.5).then_inc(blank, 1)
            pool.memset(eps[:, :], EPS_LN).then_inc(blank, 1)
            pool.wait_ge(blank, 2)

            def body(c):
                pool.wait_ge(s_mv, 4 * c + 4)
                pool.tensor_tensor(vare[:, :], mv[:, :, 1], eps[:, :], ALU.add).then_inc(s_ve, 1)
                pool.wait_ge(s_ve, c + 1)
                if later(c):
                    pool.wait_ge(s_ln, 4 * c)
                pool.tensor_tensor(rstd[:, :], vare[:, :], half[:, :], ALU.pow).then_inc(s_rs, 1)

            run_chunks(pool, body)

        @block.tensor
        def _(pe):
            pe.wait_ge(consts, n_consts)
            pe.wait_ge(ready, F)

            def body(c):
                pe.wait_ge(xl, 16 * c + 16)
                if later(c):
                    pe.wait_ge(s_xc, c)
                for k in range(CT):
                    mm = pe.transpose(p_tr[:, k * P:(k + 1) * P], x_t[:, k, :], idn[:, :])
                mm.then_inc(s_tr, 1)
                pe.wait_ge(s_xc, c + 1)
                for m in range(F):
                    if m >= 2:
                        pe.wait_ge(s_a0, F * c + m - 1)
                    elif later(c):
                        pe.wait_ge(s_a0, F * c)
                    pe.matmul(p_u[m % 2][:, :], w1_s[:, m * P:(m + 1) * P], xT[:, :, :], start=True,
                              stop=True).then_inc(s_u, 1)
                    pe.matmul(p_v[m % 2][:, :], w2_s[:, m * P:(m + 1) * P], xT[:, :, :], start=True,
                              stop=True).then_inc(s_v, 1)
                for w, src, s_src, s_out_, s_read in ((h1_s, a0, s_a0, s_m1, s_a1), (h2_s, a1, s_a1, s_m2, s_a2)):
                    for m in range(F):
                        if m >= 2:
                            pe.wait_ge(s_read, F * c + m - 1)
                        elif s_read is s_a2:
                            pe.wait_ge(s_a1, F * c + m + 3)
                        elif later(c):
                            pe.wait_ge(s_a2, F * c)
                        for k in range(F):
                            if m == 0:
                                pe.wait_ge(s_src, F * c + k + 1)
                            mm = pe.matmul(p_h[m % 2][:, :], w[:, k, m * P:(m + 1) * P], src[:, k, :],
                                           start=(k == 0), stop=(k == F - 1))
                        mm.then_inc(s_out_, 1)
                if later(c):
                    pe.wait_ge(s_z, c)
                pe.wait_ge(s_a2, F * c + F)
                for j in range(CT):
                    for k in range(F):
                        mm = pe.matmul(p_y[:, j * P:(j + 1) * P], a2[:, k, j * P:(j + 1) * P], w3_o[:, k, :],
                                       start=(k == 0), stop=(k == F - 1))
                mm.then_inc(s_y, 1)

            run_chunks(pe, body)

        @block.scalar
        def _(act):
            act.wait_ge(consts, n_consts)

            def body(c):
                act.wait_ge(s_tr, c + 1)
                if later(c):
                    act.wait_ge(s_v, F * c)
                act.copy(xT[:, :, :], p_tr[:, :]).then_inc(s_xc, 1)
                for m in range(F):
                    act.wait_ge(s_u, F * c + m + 1)
                    if m >= 2:
                        act.wait_ge(s_a0, F * c + m - 1)
                    elif later(c):
                        act.wait_ge(s_a0, F * c + m - 1)
                    act.activation(gate[:, m % 2, :], p_u[m % 2][:, :], ACT.Silu, scale=sh[:, 0, m:m + 1]).then_inc(s_g, 1)
                for lay, dst, s_in, s_done, s_next in ((2, a1, s_m1, s_a1, s_m2), (3, a2, s_m2, s_a2, s_y)):
                    for m in range(F):
                        act.wait_ge(s_in, F * c + m + 1)
                        if later(c) and m == 0:
                            act.wait_ge(s_next, (F if s_next is s_m2 else 1) * c)
                        act.activation(dst[:, m, :], p_h[m % 2][:, :], ACT.Gelu,
                                       scale=sh[:, lay, m:m + 1]).then_inc(s_done, 1)

            run_chunks(act, body)

        @block.vector
        def _(dve):
            dve.wait_ge(consts, n_consts)
            for k in range(F):
                dve.tensor_tensor(w3_o[:, k, :], w3_s[:, k, :], so[:, :], ALU.mult).then_inc(ready, 1)

            def body(c):
                for m in range(F):
                    dve.wait_ge(s_g, F * c + m + 1)
                    dve.wait_ge(s_v, F * c + m + 1)
                    if later(c) and m == 0:
                        dve.wait_ge(s_m1, F * c)
                    dve.scalar_tensor_tensor(a0[:, m, :], p_v[m % 2][:, :], sh[:, 1, m:m + 1], gate[:, m % 2, :],
                                             ALU.mult, ALU.mult).then_inc(s_a0, 1)
                dve.wait_ge(s_y, c + 1)
                dve.wait_ge(rl, 16 * c + 16)
                if later(c):
                    dve.wait_ge(s_ln, 4 * c)
                dve.tensor_tensor(z[:, :, :], p_y[:, :].rearrange("p (t d) -> p t d", d=P), xr_t[:, :, :],
                                  ALU.add).then_inc(s_z, 1)
                dve.wait_ge(s_z, c + 1)
                for j in range(CT):
                    dve.bn_stats(stats[:, j, :], z[:, j, :]).then_inc(s_bs, 1)
                if later(c):
                    dve.wait_ge(s_ve, c)
                for j in range(CT):
                    dve.wait_ge(s_bs, 4 * c + j + 1)
                    dve.tensor_copy(mark[:, j:j + 1], stats[:, j, 0:1])
                    dve.bn_aggr(mv[:, j, :], stats[:, j, :]).then_inc(s_mv, 1)
                dve.wait_ge(s_rs, c + 1)
                if later(c):
                    dve.wait_ge(stored, 16 * c)
                for j in range(CT):
                    dve.tensor_scalar(y_t[:, j, :], z[:, j, :], mv[:, j, 0:1], rstd[:, j:j + 1], ALU.subtract,
                                      ALU.mult).then_inc(s_ln, 1)

            run_chunks(dve, body)


def mixture(nc, name, banks, x_in, x_out, router, w1, w2, ident, before, iota):
    E, TOP_K, F = 8, 2, 4
    CAP = int(1.25 * NB * P * TOP_K / E) + 1
    TE = NB * E
    ph = Phase(nc, name, banks)
    with ph:
        sb, ps, sem = ph.sb, ph.ps, ph.sem
        xT = sb("xT", [P, NB, P])
        w1_s, w2_s = sb("w1", [P, E, F * P]), sb("w2", [P, E, F, P])
        gates = sb("gates", [P, NB, E])
        half, eps = sb("half", [P, CT]), sb("eps", [P, CT])
        p = [ps() for k in range(8)]
        wl = sem("experts_loaded")

        with ExitStack() as g:
            def gs(n, shape):
                return g.enter_context(nc.sbuf_tensor(f"{name}_{n}", shape, F32))

            idn, bef, io, rw = gs("idn", [P, P]), gs("bef", [P, P]), gs("io", [P, E]), gs("rw", [P, E])
            ones = gs("ones", [P, P])
            x_t, xc = gs("x", [P, CT, P]), gs("xc", [P, CT, P])
            lg = gs("lg", [P, NB, E])
            v = {n: gs(n, [P, NB, E]) for n in ("sh", "ex", "pr", "eq", "far", "o1", "p2", "eq2", "far2", "o2",
                                                 "both", "wa", "wb", "wsum", "cnt", "keep", "gate0", "tot", "c0", "c1", "tin")}
            r = {n: gs(n, [P, NB]) for n in ("mx", "sm", "rs", "m1", "i1", "m2", "i2", "dn", "rd")}
            consts, xl, s_tr, s_xc = sem("consts"), sem("x_loaded"), sem("x_transposed"), sem("x_copied")
            s_xa, s_lg, s_lc = sem("xT_kept"), sem("logits_done"), sem("logits_copied")
            chain = sem("vector_steps"); s_ex = sem("exp_done"); s_cn = sem("counts_done"); blank = sem("blank")
            N_BOTH = 18
            block = g.enter_context(nc.Block())

            @block.sync
            def _(sp):
                for dst, src in ((idn, ident), (bef, before), (io, iota), (rw, router)):
                    sp.dma_start(dst[:, :], src).then_inc(consts, 16)

                def body(c):
                    if later(c):
                        sp.wait_ge(s_tr, c)
                    sp.dma_start(x_t[:, :, :], x_in[c].rearrange("t p d -> p t d")).then_inc(xl, 16)

                run_chunks(sp, body)
                sp.dma_start(w1_s[:, :, :], w1).then_inc(wl, 16)
                sp.dma_start(w2_s[:, :, :, :], w2).then_inc(wl, 16)

            @block.gpsimd
            def _(pool):
                pool.memset(ones[:, :], 1.0).then_inc(blank, 1)
                pool.memset(half[:, :], -0.5).then_inc(blank, 1)
                pool.memset(eps[:, :], EPS_LN).then_inc(blank, 1)

                def body(c):
                    pool.wait_ge(s_xc, c + 1)
                    pool.tensor_copy(xT[:, bass.ds(4 * c, CT), :], xc[:, :, :]).then_inc(s_xa, 1)

                run_chunks(pool, body)

            @block.tensor
            def _(pe):
                pe.wait_ge(consts, 64)
                pe.wait_ge(blank, 3)

                def body(c):
                    pe.wait_ge(xl, 16 * c + 16)
                    if later(c):
                        pe.wait_ge(s_xc, c)
                    for k in range(CT):
                        mm = pe.transpose(p[0][:, k * P:(k + 1) * P], x_t[:, k, :], idn[:, :])
                    mm.then_inc(s_tr, 1)
                    pe.wait_ge(s_xc, c + 1)
                    if later(c):
                        pe.wait_ge(s_lc, c)
                    for k in range(CT):
                        mm = pe.matmul(p[1][:, k * E:(k + 1) * E], xc[:, k, :], rw[:, :], start=True, stop=True)
                    mm.then_inc(s_lg, 1)

                run_chunks(pe, body)
                pe.wait_ge(chain, N_BOTH)
                pe.matmul(p[2][:, 0:TE], bef[:, :], v["both"][:, :, :], start=True, stop=True)
                pe.matmul(p[3][:, 0:TE], ones[:, :], v["both"][:, :, :], start=True, stop=True).then_inc(s_cn, 1)

            @block.scalar
            def _(act):
                def body(c):
                    act.wait_ge(s_tr, c + 1)
                    if later(c):
                        act.wait_ge(s_lg, c)
                        act.wait_ge(s_xa, c)
                    act.copy(xc[:, :, :], p[0][:, :]).then_inc(s_xc, 1)

                run_chunks(act, body)
                act.wait_ge(chain, 2)
                act.activation(v["ex"][:, :, :], v["sh"][:, :, :], ACT.Exp).then_inc(s_ex, 1)

            @block.vector
            def _(dve):
                steps = [0]

                def then(ins):
                    steps[0] += 1
                    ins.then_inc(chain, 1)
                    dve.wait_ge(chain, steps[0])

                def wide(a):
                    return a[:, :].unsqueeze(2).broadcast_to([P, NB, E])

                def tt(out, a, b, op):
                    then(dve.tensor_tensor(out, a, b, op))

                def body(c):
                    dve.wait_ge(s_lg, c + 1)
                    dve.tensor_copy(lg[:, bass.ds(4 * c, CT), :], p[1][:, 0:CT * E]).then_inc(s_lc, 1)

                dve.wait_ge(consts, 64)
                run_chunks(dve, body)
                dve.wait_ge(s_lc, NC)
                col = io[:, :].unsqueeze(1).broadcast_to([P, NB, E])
                then(dve.tensor_reduce(r["mx"][:, :], lg[:, :, :], AX_X, ALU.max))
                tt(v["sh"][:, :, :], lg[:, :, :], wide(r["mx"]), ALU.subtract)
                dve.wait_ge(s_ex, 1)
                then(dve.tensor_reduce(r["sm"][:, :], v["ex"][:, :, :], AX_X, ALU.add))
                then(dve.reciprocal(r["rs"][:, :], r["sm"][:, :]))
                tt(v["pr"][:, :, :], v["ex"][:, :, :], wide(r["rs"]), ALU.mult)
                then(dve.tensor_reduce(r["m1"][:, :], v["pr"][:, :, :], AX_X, ALU.max))
                tt(v["eq"][:, :, :], v["pr"][:, :, :], wide(r["m1"]), ALU.is_equal)
                then(dve.scalar_tensor_tensor(v["far"][:, :, :], v["eq"][:, :, :], -float(E), col, ALU.mult, ALU.add))
                then(dve.tensor_reduce(r["i1"][:, :], v["far"][:, :, :], AX_X, ALU.min))
                tt(v["o1"][:, :, :], v["far"][:, :, :], wide(r["i1"]), ALU.is_equal)
                then(dve.scalar_tensor_tensor(v["p2"][:, :, :], v["o1"][:, :, :], -2.0, v["pr"][:, :, :], ALU.mult, ALU.add))
                then(dve.tensor_reduce(r["m2"][:, :], v["p2"][:, :, :], AX_X, ALU.max))
                tt(v["eq2"][:, :, :], v["p2"][:, :, :], wide(r["m2"]), ALU.is_equal)
                then(dve.scalar_tensor_tensor(v["far2"][:, :, :], v["eq2"][:, :, :], -float(E), col, ALU.mult, ALU.add))
                then(dve.tensor_reduce(r["i2"][:, :], v["far2"][:, :, :], AX_X, ALU.min))
                tt(v["o2"][:, :, :], v["far2"][:, :, :], wide(r["i2"]), ALU.is_equal)
                tt(v["wa"][:, :, :], v["o1"][:, :, :], wide(r["m1"]), ALU.mult)
                tt(v["both"][:, :, :], v["o1"][:, :, :], v["o2"][:, :, :], ALU.add)
                assert steps[0] == N_BOTH
                tt(v["wb"][:, :, :], v["o2"][:, :, :], wide(r["m2"]), ALU.mult)
                tt(v["wsum"][:, :, :], v["wa"][:, :, :], v["wb"][:, :, :], ALU.add)
                tt(r["dn"][:, :], r["m1"][:, :], r["m2"][:, :], ALU.add)
                then(dve.reciprocal(r["rd"][:, :], r["dn"][:, :]))
                tt(v["gate0"][:, :, :], v["wsum"][:, :, :], wide(r["rd"]), ALU.mult)
                dve.wait_ge(s_cn, 1)
                then(dve.tensor_copy(v["tot"][:, :, :], p[3][:, 0:TE]))
                then(dve.tensor_copy(v["tin"][:, :, :], p[2][:, 0:TE]))
                src, dst, other, d = v["tot"], v["c0"], v["c1"], 1
                while d < NB:
                    then(dve.tensor_copy(dst[:, 0:d, :], src[:, 0:d, :]))
                    tt(dst[:, d:NB, :], src[:, d:NB, :], src[:, 0:NB - d, :], ALU.add)
                    src, dst, other, d = dst, other, dst, 2 * d
                tt(v["cnt"][:, :, :], src[:, :, :], v["tot"][:, :, :], ALU.subtract)
                tt(v["wa"][:, :, :], v["cnt"][:, :, :], v["tin"][:, :, :], ALU.add)
                then(dve.tensor_scalar(v["keep"][:, :, :], v["wa"][:, :, :], float(CAP), None, ALU.is_lt))
                tt(gates[:, :, :], v["gate0"][:, :, :], v["keep"][:, :, :], ALU.mult)

        with ExitStack() as g:
            def gs(n, shape):
                return g.enter_context(nc.sbuf_tensor(f"{name}_{n}", shape, F32))

            xr_t = gs("xr", [P, CT, P]); gc = gs("gc", [P, CT, E])
            hid = gs("hid", [P, 2, F, CT * P])
            acc = gs("acc", [P, 2, CT, P])
            mark = gs("mark", [P, CT]); stats = gs("stats", [P, CT, 6]); mv = gs("mv", [P, CT, 2])
            vare = gs("vare", [P, CT]); rstd = gs("rstd", [P, CT]); y_t = gs("y", [P, CT, P])
            rl, stored = sem("xr_loaded"), sem("y_stored")
            s_gc, s_x2, s_h, s_si = sem("gates_copied"), sem("sum_started"), sem("hidden_done"), sem("silu_done")
            s_y, s_ac = sem("expert_done"), sem("expert_added")
            s_bs, s_mv, s_ve, s_rs, s_ln = (sem(n) for n in ("stats_ready", "mean_var_ready", "var_eps_ready",
                                                               "rstd_ready", "normed"))
            p_h, p_y = p[0:4], p[4:6]
            block = g.enter_context(nc.Block())

            @block.sync
            def _(sp):
                def body(c):
                    if later(c):
                        sp.wait_ge(s_x2, c)
                    sp.dma_start(xr_t[:, :, :], x_in[c].rearrange("t p d -> p t d")).then_inc(rl, 16)
                    sp.wait_ge(s_ln, 4 * c + 4)
                    sp.dma_start(x_out[c].rearrange("t p d -> p t d"), y_t[:, :, :]).then_inc(stored, 16)

                run_chunks(sp, body)
                sp.wait_ge(stored, 16 * NC)

            @block.gpsimd
            def _(pool):
                def body(c):
                    pool.wait_ge(s_mv, 4 * c + 4)
                    pool.tensor_tensor(vare[:, :], mv[:, :, 1], eps[:, :], ALU.add).then_inc(s_ve, 1)
                    pool.wait_ge(s_ve, c + 1)
                    if later(c):
                        pool.wait_ge(s_ln, 4 * c)
                    pool.tensor_tensor(rstd[:, :], vare[:, :], half[:, :], ALU.pow).then_inc(s_rs, 1)

                run_chunks(pool, body)

            @block.tensor
            def _(pe):
                pe.wait_ge(wl, 32)

                def body(c):
                    def hidden(e):
                        for f in range(F):
                            if e > 0:
                                pe.wait_ge(s_si, F * (E * c + e - 1) + f + 1)
                            elif later(c):
                                pe.wait_ge(s_si, F * (E * c - 1) + f + 1)
                            pe.matmul(p_h[f][:, :], w1_s[:, e, f * P:(f + 1) * P], xT[:, bass.ds(4 * c, CT), :],
                                      start=True, stop=True).then_inc(s_h, 1)

                    def output(e):
                        pe.wait_ge(s_si, F * (E * c + e) + F)
                        if e >= 2:
                            pe.wait_ge(s_ac, CT * (E * c + e - 1))
                        elif later(c):
                            pe.wait_ge(s_ac, CT * (E * c + e - 1))
                        for j in range(CT):
                            for f in range(F):
                                mm = pe.matmul(p_y[e % 2][:, j * P:(j + 1) * P], hid[:, e % 2, f, j * P:(j + 1) * P],
                                               w2_s[:, e, f, :], start=(f == 0), stop=(f == F - 1))
                        mm.then_inc(s_y, 1)

                    for e in range(E + 1):
                        if e < E:
                            hidden(e)
                        if e > 0:
                            output(e - 1)

                run_chunks(pe, body)

            @block.scalar
            def _(act):
                def body(c):
                    for e in range(E):
                        if e >= 2 or later(c):
                            act.wait_ge(s_y, E * c + e - 1)
                        for f in range(F):
                            act.wait_ge(s_h, F * (E * c + e) + f + 1)
                            act.activation(hid[:, e % 2, f, :], p_h[f][:, :], ACT.Silu).then_inc(s_si, 1)

                run_chunks(act, body)

            @block.vector
            def _(dve):
                def body(c):
                    dve.wait_ge(rl, 16 * c + 16)
                    if later(c):
                        dve.wait_ge(s_ac, CT * E * c)
                        dve.wait_ge(s_ln, 4 * c)
                    dve.tensor_copy(gc[:, :, :], gates[:, bass.ds(4 * c, CT), :]).then_inc(s_gc, 1)
                    dve.tensor_scalar(acc[:, 1, :, :], xr_t[:, :, :], 2.0, None, ALU.mult).then_inc(s_x2, 1)
                    dve.wait_ge(s_gc, c + 1)
                    dve.wait_ge(s_x2, c + 1)
                    for e in range(E):
                        dve.wait_ge(s_y, E * c + e + 1)
                        for j in range(CT):
                            if e > 0:
                                dve.wait_ge(s_ac, CT * (E * c + e - 1) + j + 1)
                            dve.scalar_tensor_tensor(acc[:, e % 2, j, :], p_y[e % 2][:, j * P:(j + 1) * P],
                                                     gc[:, j, e:e + 1], acc[:, 1 - e % 2, j, :], ALU.mult,
                                                     ALU.add).then_inc(s_ac, 1)
                    for j in range(CT):
                        dve.wait_ge(s_ac, CT * (E * c + E - 1) + j + 1)
                        dve.bn_stats(stats[:, j, :], acc[:, 1, j, :]).then_inc(s_bs, 1)
                    if later(c):
                        dve.wait_ge(s_ve, c)
                    for j in range(CT):
                        dve.wait_ge(s_bs, 4 * c + j + 1)
                        dve.tensor_copy(mark[:, j:j + 1], stats[:, j, 0:1])
                        dve.bn_aggr(mv[:, j, :], stats[:, j, :]).then_inc(s_mv, 1)
                    dve.wait_ge(s_rs, c + 1)
                    if later(c):
                        dve.wait_ge(stored, 16 * c)
                    for j in range(CT):
                        dve.tensor_scalar(y_t[:, j, :], acc[:, 1, j, :], mv[:, j, 0:1], rstd[:, j:j + 1],
                                          ALU.subtract, ALU.mult).then_inc(s_ln, 1)

                run_chunks(dve, body)


def build_decoder(nc, d, out):
    keep = [nc.dram_tensor(f"between{k}", (NB, P, P), F32, kind="Internal").ap() for k in range(5)]

    banks = [nc.alloc_psum_tensor(f"bank{k}", [P, 512], F32) for k in range(8)]

    def chunks(a):
        return a.rearrange("(c t) p d -> c t p d", t=CT)

    linear_attention(nc, "L0a", banks, d["x"], keep[0], d["wq0"], d["wk0"], d["wv0"], d["wo0"], d["bq0"], d["bk0"],
                     d["bv0"], d["bo0"], d["feat"], d["norm"], d["ident"], d["own_head"])
    softmax_attention(nc, "L0x", banks, keep[0], d["ctx"], keep[1], d["wq1"], d["wk1"], d["wv1"], d["wo1"], d["bq1"],
                      d["bk1"], d["bv1"], d["bo1"], d["ident"], d["head8"])
    feed_forward(nc, "L0f", banks, chunks(keep[1]), chunks(keep[2]), d["w1"], d["w2"], d["h1"], d["h2"], d["w3"],
                 d["s_hidden"], d["s_out"], d["ident"])
    trig_attention(nc, "L1a", banks, keep[2], keep[3], d["w_qk"], d["b_qk"], d["quarter"], d["wv2"], d["wo2"],
                   d["ident"], d["head16"], d["causal"])
    softmax_attention(nc, "L1x", banks, keep[3], d["ctx"], keep[4], d["wq3"], d["wk3"], d["wv3"], d["wo3"], None, None,
                      None, d["bo3"], d["ident"], d["head8"])
    mixture(nc, "L1f", banks, chunks(keep[4]), chunks(out), d["router"], d["e1"], d["e2"], d["ident"], d["before"],
            d["experts"])


def lay_out(inp):
    import numpy as np

    a = {k: np.asarray(v) for k, v in inp.items()}
    f32 = np.float32
    M = a["L0_attn_orf"].shape[0]
    E, _, FF = a["L1_ffn_w1"].shape
    F = FF // P
    d = {"x": a["x"], "ctx": a["ctx_1024"]}
    for n, pre in ((0, "L0_attn_"), (1, "L0_xattn_"), (3, "L1_xattn_")):
        for w in "qkvo":
            d[f"w{w}{n}"] = a[f"{pre}W{w}"].T
        if n != 3:
            d[f"bq{n}"], d[f"bk{n}"] = a[f"{pre}bq"][:, None], a[f"{pre}bk"][:, None]
            d[f"bv{n}"] = a[f"{pre}bv"]
        d[f"bo{n}"] = a[f"{pre}bo"]
    feat, norm = np.zeros((H, DK, H, M), f32), np.zeros((H, DK, H, M), f32)
    for h in range(H):
        feat[h, :, h, :] = a["L0_attn_orf"].T
        norm[h, :, h, :] = -1.0 / (2.0 * DK ** 0.5)
    d["feat"], d["norm"] = feat.reshape(P, H * M), norm.reshape(P, H * M)
    own = np.zeros((4, M, 4, 4, DK + 1), f32)
    for j in range(4):
        own[j, :, :, j, :] = 1.0
    d["own_head"] = own.reshape(P, H, DK + 1)
    d["w1"], d["w2"] = a["L0_ffn_w1_w"].T, a["L0_ffn_w2_w"].T
    for n in ("h1", "h2"):
        d[n] = a[f"L0_ffn_{n}_w"].T.reshape(F, P, FF).transpose(1, 0, 2)
    d["w3"] = a["L0_ffn_w3_w"].T.reshape(F, P, P).transpose(1, 0, 2)
    d["s_hidden"] = np.stack([a[f"L0_ffn_{n}_s"].reshape(F, P).T for n in ("w1", "w2", "h1", "h2")], 1)
    d["s_out"] = a["L0_ffn_w3_s"]

    def rows(w):
        return np.broadcast_to(w.reshape(2, 8, 1, DK), (2, 8, 2, DK)).reshape(2, P).T

    for n in "wb":
        d[f"{n}_qk"] = np.concatenate([rows(a[f"L1_attn_{n}_q"]), rows(a[f"L1_attn_{n}_k"])], 1)
    quarter = np.zeros((8, 2, DK), f32)
    quarter[:, 0] = 512 // 4
    d["quarter"] = quarter.reshape(P, 1)
    d["wv2"], d["wo2"] = a["L1_attn_v_w"].T, a["L1_attn_out_w"].T
    d["router"] = a["L1_ffn_router_w"].T
    d["e1"] = a["L1_ffn_w1"].transpose(1, 0, 2)
    d["e2"] = a["L1_ffn_w2"].reshape(E, F, P, P).transpose(2, 0, 1, 3)
    row, col = np.arange(P)[:, None], np.arange(P)[None, :]
    d["ident"] = (row == col).astype(f32)
    d["causal"] = (row <= col).astype(f32)
    d["before"] = (row < col).astype(f32)
    d["head8"] = (row // DK == np.arange(H)[None, :]).astype(f32)
    d["head16"] = (row // (2 * DK) == np.arange(8)[None, :]).astype(f32)
    d["experts"] = np.broadcast_to(np.arange(E, dtype=f32), (P, E))
    return {k: np.ascontiguousarray(v) for k, v in d.items()}


def kernel(**inputs):
    import concourse.bacc as bacc
    from concourse.bass_utils import run_bass_kernel_spmd

    arrays = lay_out(inputs)
    nc = bacc.Bacc("TRN2", target_bir_lowering=False, num_devices=1)
    d = {n: nc.dram_tensor(f"in_{n}", a.shape, mybir.dt.from_np(a.dtype), kind="ExternalInput").ap()
         for n, a in arrays.items()}
    out = nc.dram_tensor("out_0", (NB, P, P), F32, kind="ExternalOutput").ap()
    build_decoder(nc, d, out)
    r = run_bass_kernel_spmd(nc, [{f"in_{n}": a for n, a in arrays.items()}], core_ids=[0])
    return r.results[0]["out_0"]
```

```python
from contextlib import ExitStack

import concourse.bass as bass
from concourse import mybir

ALU = mybir.AluOpType
ACT = mybir.ActivationFunctionType
F32 = mybir.dt.float32
F32R = mybir.dt.float32r
BF16 = mybir.dt.bfloat16
AX_X = mybir.AxisListType.X

P = 128
NB = 32
H = 16
DK = 8
EPS_LN = 1e-5


class Tile:

    def __init__(self, i, off):
        self.i, self.off = i, off
        self.n = 4 * i + off

    def at(self, k):
        return Tile(self.i, self.off + k)

    @property
    def there(self):
        return not isinstance(self.i, int) or 0 <= self.n < NB

    def buf(self, m):
        return self.off % m

    def lap(self, m):
        return (4 // m) * self.i + self.off // m


def run_slots(eng, slot, first, last, laps=7):
    for t in range(first, 4):
        slot(Tile(0, t))
    with eng.Fori(1, laps) as i:
        for u in range(4):
            slot(Tile(i, u))
    for t in range(4 * laps, last):
        slot(Tile(laps, t - 4 * laps))


def done(eng, sem, tile, per=1, part=None):
    eng.wait_ge(sem, per * tile.n + (per if part is None else part))


def freed(eng, sem, tile, m, per=1):
    before = tile.at(-m)
    if before.there:
        done(eng, sem, before, per)


def loaded(eng, sems, tile):
    m = len(sems)
    eng.wait_ge(sems[tile.buf(m)], 16 * tile.lap(m) + 16)


def high(eng, out, whole):
    return eng.tensor_copy(out.bitcast(F32R), whole)


def low(eng, out, whole, high_part):
    return eng.tensor_tensor(out.bitcast(F32R), whole, high_part, ALU.subtract)


def products(pe, out, w_high, w_low, x_high, x_low, start=True, stop=True):
    passes = ((w_high, x_high), (w_high, x_low), (w_low, x_high))
    for k, (w, x) in enumerate(passes):
        mm = pe.matmul(out, w.bitcast(F32R), x.bitcast(F32R), start=start and k == 0, stop=stop and k == 2)
    return mm


class Phase:

    def __init__(self, nc, name, banks):
        self.nc, self.name, self.ctx, self.banks = nc, name, ExitStack(), list(banks)
        self.sems = []

    def sb(self, name, shape, dt=F32):
        return self.ctx.enter_context(self.nc.sbuf_tensor(f"{self.name}_{name}", shape, dt))

    def ps(self):
        return self.banks.pop(0)

    def sem(self, name, n=None):
        if n is not None:
            return [self.sem(f"{name}{k}") for k in range(n)]
        self.sems.append(self.nc.alloc_semaphore(f"{self.name}_{name}"))
        return self.sems[-1]

    def __enter__(self):
        return self

    def __exit__(self, *failed):
        self.ctx.close()
        self.nc.clear_and_free_semaphores(self.sems)
        self.nc.all_engine_barrier()


def softmax_attention(nc, name, banks, x_in, kv_in, x_out, wq, wk, wv, wo, bq, bk, bv, bo, ident, head_of_row):
    ph = Phase(nc, name, banks)
    with ph:
        sb, ps, sem = ph.sb, ph.ps, ph.sem
        idn = sb("idn", [P, P])
        hmask = sb("hmask", [P, H])
        wq_s, wk_s, wv_s, wo_s = (sb(f"w{k}", [P, P]) for k in "qkvo")
        bq_s, bk_s = sb("bq", [P, 1]), sb("bk", [P, 1])
        bv_s, bo_s = sb("bv", [P, P]), sb("bo", [P, P])
        pick = sb("pick", [P, H, P], BF16)
        half, eps = sb("half", [P, 1]), sb("eps", [P, 1])
        x_t = sb("x", [P, 4, P]); c_t = sb("c", [P, 4, P])
        xr_t = sb("xr", [P, 2, P]); xb_t = sb("xb", [P, 2, P])
        xcT = sb("xcT", [P, 2, 2, P])
        qT = sb("qT", [P, 4, P]); kT = sb("kT", [P, 2, P])
        kd = sb("kd", [P, 4, H, P])
        va = sb("va", [P, 4, H, 32])
        nmax = sb("nmax", [P, 2, P])
        nmaxT = sb("nmaxT", [P, 2, P], BF16)
        probs = sb("probs", [P, 2, H, P])
        o1 = sb("o1", [P, 2, 4, P])
        rden = sb("rden", [P, 2, 4, 4])
        o_tok = sb("o_tok", [P, 2, P]); oT = sb("oT", [P, 2, P])
        z = sb("z", [P, 2, P]); mark = sb("mark", [P, 1]); stats = sb("stats", [P, 2, 6]); mv = sb("mv", [P, 2, 2])
        vare = sb("vare", [P, 2, 1]); rstd = sb("rstd", [P, 2, 1]); y_t = sb("y", [P, 4, P])
        p_tr = ps()
        p_pj = ps()
        p_mx = [ps(), ps()]
        p_st = [ps(), ps()]
        p_pv = ps()
        p_on = ps()

        consts = sem("consts_loaded"); ready = sem("consts_ready"); blank = sem("blanks_ready")
        xl, cl, rl = sem("x_loaded", 4), sem("c_loaded", 4), sem("xr_loaded", 2)
        stored = sem("y_stored", 4)
        s_tr = sem("xc_transposed"); s_xc = sem("xc_copied")
        s_pj = sem("qkv_projected"); s_q = sem("q_ready"); s_k = sem("k_ready"); s_v = sem("v_ready")
        s_kd = sem("kd_ready"); s_sq = sem("scores_q"); s_mx = sem("max_ready")
        s_mt = sem("max_transposed"); s_mc = sem("max_copied")
        s_st = sem("scores_k"); s_ex = sem("exp_done"); s_pv = sem("pv_done"); s_o1 = sem("pv_copied")
        s_on = sem("pv_transposed"); s_rd = sem("reciprocals_ready"); s_ot = sem("o_normalised")
        s_oT = sem("o_transposed"); s_oc = sem("o_copied"); s_y = sem("y_projected")
        s_xb = sem("residual_ready"); s_z = sem("z_ready"); s_bs = sem("stats_ready")
        s_mv = sem("mean_var_ready"); s_ve = sem("var_eps_ready"); s_rs = sem("rstd_ready")
        s_ln = sem("normed")

        block = ph.ctx.enter_context(nc.Block())

        @block.sync
        def _(sp):
            for dst, src in ((idn[:, :], ident), (hmask[:, :], head_of_row), (wq_s[:, :], wq), (wk_s[:, :], wk),
                             (wv_s[:, :], wv), (wo_s[:, :], wo)):
                sp.dma_start(dst, src).then_inc(consts, 16)
            if bq is not None:
                sp.dma_start(bq_s[:, :], bq).then_inc(consts, 16)
                sp.dma_start(bk_s[:, :], bk).then_inc(consts, 16)
                sp.dma_start(bv_s[:, :], bv.partition_broadcast(P)).then_inc(consts, 16)
            sp.dma_start(bo_s[:, :], bo.partition_broadcast(P)).then_inc(consts, 16)

            def slot(t):
                a = t.at(4)
                if a.there:
                    freed(sp, s_tr, a, 4)
                    sp.dma_start(x_t[:, a.buf(4), :], x_in[a.n]).then_inc(xl[a.buf(4)], 16)
                    sp.dma_start(c_t[:, a.buf(4), :], kv_in[a.n]).then_inc(cl[a.buf(4)], 16)
                r = t.at(0)
                if r.there:
                    freed(sp, s_xb, r, 2)
                    sp.dma_start(xr_t[:, r.buf(2), :], x_in[r.n]).then_inc(rl[r.buf(2)], 16)
                o = t.at(-3)
                if o.there:
                    done(sp, s_ln, o)
                    sp.dma_start(x_out[o.n], y_t[:, o.buf(4), :]).then_inc(stored[o.buf(4)], 16)

            run_slots(sp, slot, -4, NB + 3)
            for k in range(4):
                sp.wait_ge(stored[k], 16 * NB // 4)

        n_consts = 16 * (10 if bq is not None else 7)

        @block.gpsimd
        def _(pool):
            pool.memset(va[:, :, :, :], 0.0).then_inc(blank, 1)
            pool.wait_ge(blank, 1)
            pool.memset(va[:, :, :, DK:DK + 1], 1.0).then_inc(blank, 1)
            pool.memset(nmax[:, :, :], 0.0).then_inc(blank, 1)
            pool.memset(half[:, :], -0.5).then_inc(blank, 1)
            pool.memset(eps[:, :], EPS_LN).then_inc(blank, 1)
            pool.wait_ge(blank, 5)
            pool.wait_ge(consts, n_consts)

            def slot(t):
                n = t.at(-3)
                if n.there:
                    done(pool, s_mv, n)
                    freed(pool, s_rs, n, 2)
                    pool.tensor_tensor(vare[:, n.buf(2), :], mv[:, n.buf(2), 1:2], eps[:, :], ALU.add).then_inc(s_ve, 1)
                    done(pool, s_ve, n)
                    freed(pool, s_ln, n, 2)
                    pool.tensor_tensor(rstd[:, n.buf(2), :], vare[:, n.buf(2), :], half[:, :],
                                       ALU.pow).then_inc(s_rs, 1)
                k = t.at(2)
                if k.there:
                    done(pool, s_k, k)
                    freed(pool, s_st, k, 4, 4)
                    pool.tensor_tensor(kd[:, k.buf(4), :, :],
                                       kT[:, k.buf(2), :].unsqueeze(1).broadcast_to([P, H, P]),
                                       hmask[:, :].unsqueeze(2).broadcast_to([P, H, P]),
                                       ALU.mult).then_inc(s_kd, 1)
                r = t.at(-1)
                if r.there:
                    loaded(pool, rl, r)
                    freed(pool, s_z, r, 2)
                    pool.tensor_tensor(xb_t[:, r.buf(2), :], xr_t[:, r.buf(2), :], bo_s[:, :],
                                       ALU.add).then_inc(s_xb, 1)

            run_slots(pool, slot, -2, NB + 3)

        @block.tensor
        def _(pe):
            pe.wait_ge(consts, n_consts)
            pe.wait_ge(ready, 1)
            pe.wait_ge(blank, 5)

            def slot(t):
                a = t.at(2)
                if a.there:
                    loaded(pe, xl, a)
                    loaded(pe, cl, a)
                    if t.there:
                        done(pe, s_mc, t)
                    elif a.at(-1).there:
                        done(pe, s_xc, a.at(-1))
                    pe.transpose(p_tr[:, 0:P], x_t[:, a.buf(4), :], idn[:, :])
                    pe.transpose(p_tr[:, P:2 * P], c_t[:, a.buf(4), :], idn[:, :]).then_inc(s_tr, 1)
                v = t.at(-1)
                if v.there:
                    done(pe, s_ex, v, 4)
                    freed(pe, s_o1, v, 1)
                    for k in range(4):
                        for c in range(4):
                            h = 4 * c + k
                            mm = pe.matmul(p_pv[32 * c:32 * c + 32, k * P:(k + 1) * P], va[:, v.buf(4), h, :],
                                           probs[:, v.buf(2), h, :], start=True, stop=True)
                    mm.then_inc(s_pv, 1)
                if a.there:
                    done(pe, s_xc, a)
                    if t.at(-3).there:
                        done(pe, s_z, t.at(-3))
                    elif a.at(-1).there:
                        done(pe, s_v, a.at(-1))
                        done(pe, s_k, a.at(-1))
                    xT, cT = xcT[:, a.buf(2), 0, :], xcT[:, a.buf(2), 1, :]
                    pe.matmul(p_pj[:, 0:P], wq_s[:, :], xT, start=True, stop=True)
                    pe.matmul(p_pj[:, P:2 * P], wk_s[:, :], cT, start=True, stop=True)
                    pe.matmul(p_pj[:, 2 * P:3 * P], cT, wv_s[:, :], start=True, stop=True).then_inc(s_pj, 1)
                m = t.at(1)
                if m.there:
                    done(pe, s_kd, m)
                    done(pe, s_q, m)

                def rows_scores(g):
                    if g >= 2:
                        done(pe, s_mx, m, 4, g - 1)
                    elif m.at(-1).there:
                        done(pe, s_mx, m.at(-1), 4, g + 3)
                    q_hi = qT[:, m.buf(4), :].bitcast(BF16)[:, 1:2 * P:2]
                    k_hi = kd[:, m.buf(4), 4 * g:4 * g + 4, :].bitcast(BF16)[:, :, 1:2 * P:2]
                    pe.matmul(p_mx[g % 2][:, :], q_hi, k_hi, start=True, stop=True).then_inc(s_sq, 1)

                if m.there:
                    rows_scores(0)
                    rows_scores(1)
                o = t.at(-2)
                if o.there:
                    done(pe, s_ot, o)
                    if a.there:
                        done(pe, s_xc, a)
                    elif t.there:
                        done(pe, s_mc, t)
                    else:
                        done(pe, s_oc, o.at(-1))
                    pe.transpose(p_tr[:, 0:P], o_tok[:, o.buf(2), :], idn[:, :]).then_inc(s_oT, 1)
                if t.there:
                    done(pe, s_mc, t)
                for g in range(4):
                    if t.there:
                        if g >= 2:
                            done(pe, s_ex, t, 4, g - 1)
                        elif t.at(-1).there:
                            done(pe, s_ex, t.at(-1), 4, g + 3)
                        for j in range(4):
                            out = p_st[g % 2][:, j * P:(j + 1) * P]
                            pe.matmul(out, kd[:, t.buf(4), 4 * g + j, :], qT[:, t.buf(4), :],
                                      start=(j == 0), stop=False, skip_group_check=True)
                            mm = pe.matmul(out, pick[:, 4 * g + j, :], nmaxT[:, t.buf(2), :],
                                           start=False, stop=True, skip_group_check=True)
                        mm.then_inc(s_st, 1)
                    if m.there and g in (1, 2):
                        rows_scores(g + 1)
                if m.there:
                    done(pe, s_mx, m, 4)
                    if o.there:
                        done(pe, s_oc, o)
                    elif a.there:
                        done(pe, s_xc, a)
                    pe.transpose(p_tr[:, 0:P], nmax[:, m.buf(2), :], idn[:, :]).then_inc(s_mt, 1)
                if o.there:
                    done(pe, s_oc, o)
                    if a.there:
                        done(pe, s_v, a)
                        done(pe, s_k, a)
                    else:
                        done(pe, s_z, o.at(-1))
                    pe.matmul(p_pj[:, 0:P], oT[:, o.buf(2), :], wo_s[:, :], start=True, stop=True).then_inc(s_y, 1)
                if v.there:
                    done(pe, s_o1, v)
                    freed(pe, s_ot, v, 1)
                    for k in range(4):
                        mm = pe.transpose(p_on[:, k * P:(k + 1) * P], o1[:, v.buf(2), k, :], idn[:, :])
                    mm.then_inc(s_on, 1)

            run_slots(pe, slot, -2, NB + 2)

        @block.scalar
        def _(act):
            act.wait_ge(consts, n_consts)

            def slot(t):
                a = t.at(2)
                if a.there:
                    done(act, s_tr, a)
                    freed(act, s_pj, a, 2)
                    act.copy(xcT[:, a.buf(2), :, :], p_tr[:, 0:2 * P]).then_inc(s_xc, 1)
                    done(act, s_pj, a)
                    if a.at(-4).there:
                        done(act, s_st, a.at(-4), 4)
                    if bq is not None:
                        act.activation(qT[:, a.buf(4), :], p_pj[:, 0:P], ACT.Identity, bias=bq_s[:, :]).then_inc(s_q, 1)
                    else:
                        act.copy(qT[:, a.buf(4), :], p_pj[:, 0:P]).then_inc(s_q, 1)
                    freed(act, s_kd, a, 2)
                    if bq is not None:
                        act.activation(kT[:, a.buf(2), :], p_pj[:, P:2 * P], ACT.Identity, bias=bk_s[:, :]).then_inc(s_k, 1)
                    else:
                        act.copy(kT[:, a.buf(2), :], p_pj[:, P:2 * P]).then_inc(s_k, 1)
                if t.there:
                    freed(act, s_pv, t, 2)
                    for g in range(4):
                        done(act, s_st, t, 4, g + 1)
                        act.activation(probs[:, t.buf(2), 4 * g:4 * g + 4, :], p_st[g % 2][:, :], ACT.Exp,
                                       scale=float(DK) ** -0.5).then_inc(s_ex, 1)

            run_slots(act, slot, -2, NB)

        @block.vector
        def _(dve):
            dve.wait_ge(consts, n_consts)
            dve.wait_ge(blank, 5)
            dve.tensor_copy(pick[:, :, :], idn[:, 0:H].unsqueeze(2).broadcast_to([P, H, P])).then_inc(ready, 1)

            def slot(t):
                v = t.at(-1)
                if v.there:
                    done(dve, s_pv, v)
                    freed(dve, s_on, v, 2)
                    dve.tensor_copy(o1[:, v.buf(2), :, :], p_pv[:, :]).then_inc(s_o1, 1)
                a = t.at(2)
                if a.there:
                    done(dve, s_pj, a)
                    done(dve, s_k, a)
                    freed(dve, s_pv, a, 4)
                    vin = p_pj[:, 2 * P:3 * P].rearrange("p (h d) -> p h d", d=DK)
                    if bq is not None:
                        dve.tensor_tensor(va[:, a.buf(4), :, 0:DK], vin,
                                          bv_s[:, :].rearrange("p (h d) -> p h d", d=DK), ALU.add).then_inc(s_v, 1)
                    else:
                        dve.tensor_copy(va[:, a.buf(4), :, 0:DK], vin).then_inc(s_v, 1)
                m = t.at(1)

                def maxima(g):
                    done(dve, s_sq, m, 4, g + 1)
                    dve.tensor_reduce(nmax[:, m.buf(2), 4 * g:4 * g + 4],
                                      p_mx[g % 2][:, :].rearrange("p (h k) -> p h k", k=P), AX_X, ALU.max,
                                      negate=True).then_inc(s_mx, 1)

                if m.there:
                    freed(dve, s_mt, m, 2)
                    maxima(0)
                    maxima(1)
                n = t.at(-3)
                if n.there:
                    done(dve, s_rs, n)
                    if n.at(-4).there:
                        loaded(dve, stored, n.at(-4))
                    dve.tensor_scalar(y_t[:, n.buf(4), :], z[:, n.buf(2), :], mv[:, n.buf(2), 0:1],
                                      rstd[:, n.buf(2), :], ALU.subtract, ALU.mult).then_inc(s_ln, 1)
                o = t.at(-2)
                if o.there:
                    done(dve, s_oT, o)
                    freed(dve, s_y, o, 2)
                    dve.tensor_copy(oT[:, o.buf(2), :], p_tr[:, 0:P]).then_inc(s_oc, 1)
                if m.there:
                    maxima(2)
                    maxima(3)
                if m.there:
                    done(dve, s_mt, m)
                    if m.at(-2).there:
                        done(dve, s_st, m.at(-2), 4)
                    dve.tensor_copy(nmaxT[:, m.buf(2), :], p_tr[:, 0:P]).then_inc(s_mc, 1)
                if o.there:
                    done(dve, s_y, o)
                    done(dve, s_xb, o)
                    freed(dve, s_ln, o, 2)
                    dve.tensor_tensor(z[:, o.buf(2), :], p_pj[:, 0:P], xb_t[:, o.buf(2), :], ALU.add).then_inc(s_z, 1)
                    done(dve, s_z, o)
                    dve.bn_stats(stats[:, o.buf(2), :], z[:, o.buf(2), :]).then_inc(s_bs, 1)
                    done(dve, s_bs, o)
                    freed(dve, s_ve, o, 2)
                    dve.tensor_copy(mark[:, :], stats[:, o.buf(2), 0:1])
                    dve.bn_aggr(mv[:, o.buf(2), :], stats[:, o.buf(2), :]).then_inc(s_mv, 1)
                if v.there:
                    done(dve, s_on, v)
                    on = p_on[:, :].rearrange("p (k c e) -> p k c e", k=4, c=4)
                    freed(dve, s_ot, v, 2)
                    dve.reciprocal(rden[:, v.buf(2), :, :], on[:, :, :, DK]).then_inc(s_rd, 1)
                    done(dve, s_rd, v)
                    freed(dve, s_oT, v, 2)
                    dve.tensor_tensor(o_tok[:, v.buf(2), :].rearrange("p (c k d) -> p k c d", c=4, k=4),
                                      on[:, :, :, 0:DK],
                                      rden[:, v.buf(2), :, :].unsqueeze(3).broadcast_to([P, 4, 4, DK]),
                                      ALU.mult).then_inc(s_ot, 1)

            run_slots(dve, slot, -2, NB + 3)


def trig_attention(nc, name, banks, x_in, x_out, w_qk, b_qk, quarter, wv, wo, ident, head_of_row16, causal):
    LUT = 512
    STEP = 2.0 * 3.141592653589793 / LUT
    SCALE = 0.012271845
    ROUND = 1.5 * 2.0 ** 23
    ph = Phase(nc, name, banks)
    with ph:
        sb, ps, sem = ph.sb, ph.ps, ph.sem
        idn = sb("idn", [P, P])
        hmask = sb("hmask", [P, 8])
        tri = sb("tri", [P, P])
        keep = sb("keep", [P, P])
        tri4, idn_b = sb("tri4", [P, 4, P], BF16), sb("idn_b", [P, P], BF16)
        wv_s, wo_s = sb("wv", [P, P]), sb("wo", [P, P])
        w_s, b_s, quar = sb("w", [P, 4]), sb("b", [P, 4]), sb("quar", [P, 1])
        wa, wr = sb("wa", [P, 4]), sb("wr", [P, 4])
        sc, bi = sb("sc", [P, 4]), sb("bi", [P, 4])
        half, eps = sb("half", [P, 1]), sb("eps", [P, 1])
        x_t = sb("x", [P, 4, P]); one = sb("one", [P, 8]); x2 = sb("x2", [P, 2, 2, 8, 2, DK]); xr_t = sb("xr", [P, 2, P]); xT = sb("xT", [P, 2, P])
        u = sb("u", [P, 2, 4, P]); nr = sb("nr", [P, 2, 4, P]); lap = sb("lap", [P, 2, 4, P])
        off = sb("off", [P, 2, 4, P]); an = sb("an", [P, 2, 4, P])
        sn = sb("sn", [P, 4, 4, P])
        kd = sb("kd", [P, 2, H, P])
        va = sb("va", [P, 4, H, 32])
        probs = sb("probs", [P, 2, H, P])
        o1 = sb("o1", [P, 2, 4, P]); rden = sb("rden", [P, 2, 4, 4])
        o_tok = sb("o_tok", [P, 2, P]); oT = sb("oT", [P, 2, P])
        z = sb("z", [P, 2, P]); mark = sb("mark", [P, 1]); stats = sb("stats", [P, 2, 6]); mv = sb("mv", [P, 2, 2])
        vare = sb("vare", [P, 2, 1]); rstd = sb("rstd", [P, 2, 1]); y_t = sb("y", [P, 4, P])
        p_tr, p_oT, p_pj = ps(), ps(), ps()
        p_st = [ps(), ps(), ps()]
        p_pv, p_on = ps(), ps()

        consts = sem("consts_loaded"); ready = sem("consts_ready"); blank = sem("blanks_ready")
        xl, rl, stored = sem("x_loaded", 4), sem("xr_loaded", 2), sem("y_stored", 4)
        s_x2 = sem("x_doubled"); s_tr = sem("x_transposed"); s_xc = sem("x_copied"); s_u = sem("angles_ready")
        s_nr = sem("angles_rounded"); s_lp = sem("laps_counted"); s_of = sem("laps_scaled"); s_an = sem("angles_reduced")
        s_sn = sem("sines_ready"); s_kd = sem("kd_ready")
        s_pj = sem("v_projected"); s_v = sem("v_ready")
        s_st = sem("scores"); s_mk = sem("probs_masked"); s_ex = sem("exp_done"); s_pv = sem("pv_done")
        s_o1 = sem("pv_copied"); s_on = sem("pv_transposed"); s_rd = sem("reciprocals_ready")
        s_ot = sem("o_normalised"); s_oT = sem("o_transposed"); s_oc = sem("o_copied"); s_y = sem("y_projected")
        s_z = sem("z_ready"); s_bs = sem("stats_ready"); s_mv = sem("mean_var_ready")
        s_ve = sem("var_eps_ready"); s_rs = sem("rstd_ready"); s_ln = sem("normed")

        block = ph.ctx.enter_context(nc.Block())
        n_consts = 16 * 8

        @block.sync
        def _(sp):
            for dst, src in ((idn, ident), (hmask, head_of_row16), (tri, causal), (wv_s, wv), (wo_s, wo),
                             (w_s, w_qk), (b_s, b_qk), (quar, quarter)):
                sp.dma_start(dst[:, :], src).then_inc(consts, 16)

            def slot(t):
                a = t.at(5)
                if a.there:
                    freed(sp, s_tr, a, 4)
                    sp.dma_start(x_t[:, a.buf(4), :], x_in[a.n]).then_inc(xl[a.buf(4)], 16)
                if t.there:
                    freed(sp, s_z, t, 2)
                    sp.dma_start(xr_t[:, t.buf(2), :], x_in[t.n]).then_inc(rl[t.buf(2)], 16)
                o = t.at(-3)
                if o.there:
                    done(sp, s_ln, o)
                    sp.dma_start(x_out[o.n], y_t[:, o.buf(4), :]).then_inc(stored[o.buf(4)], 16)

            run_slots(sp, slot, -5, NB + 3, 6)
            for k in range(4):
                sp.wait_ge(stored[k], 16 * NB // 4)

        @block.gpsimd
        def _(pool):
            pool.memset(va[:, :, :, :], 0.0).then_inc(blank, 1)
            pool.wait_ge(blank, 1)
            pool.memset(va[:, :, :, DK:DK + 1], 1.0).then_inc(blank, 1)
            pool.memset(half[:, :], -0.5).then_inc(blank, 1)
            pool.memset(eps[:, :], EPS_LN).then_inc(blank, 1)
            pool.memset(one[:, :], 1.0).then_inc(blank, 1)
            pool.wait_ge(blank, 5)
            pool.wait_ge(consts, n_consts)

            def slot(t):
                n = t.at(-3)
                if n.there:
                    done(pool, s_mv, n)
                    freed(pool, s_rs, n, 2)
                    pool.tensor_tensor(vare[:, n.buf(2), :], mv[:, n.buf(2), 1:2], eps[:, :], ALU.add).then_inc(s_ve, 1)
                    done(pool, s_ve, n)
                    freed(pool, s_ln, n, 2)
                    pool.tensor_tensor(rstd[:, n.buf(2), :], vare[:, n.buf(2), :], half[:, :],
                                       ALU.pow).then_inc(s_rs, 1)
                a = t.at(4)
                if a.there:
                    loaded(pool, xl, a)
                    freed(pool, s_tr, a, 2)
                    for f in range(2):
                        pool.tensor_tensor(x2[:, a.buf(2), f],
                                           x_t[:, a.buf(4), 64 * f:64 * f + 64].rearrange("p (h d) -> p h d", d=DK)
                                           .unsqueeze(2).broadcast_to([P, 8, 2, DK]),
                                           one[:, :].unsqueeze(2).unsqueeze(3).broadcast_to([P, 8, 2, DK]),
                                           ALU.mult).then_inc(s_x2, 1)
                k = t.at(1)
                if k.there:
                    done(pool, s_sn, k)
                    freed(pool, s_st, k, 2, 4)
                    for f in range(2):
                        pool.tensor_tensor(kd[:, k.buf(2), 8 * f:8 * f + 8, :],
                                           sn[:, k.buf(4), 2 + f, :].unsqueeze(1).broadcast_to([P, 8, P]),
                                           hmask[:, :].unsqueeze(2).broadcast_to([P, 8, P]),
                                           ALU.mult).then_inc(s_kd, 1)

            run_slots(pool, slot, -4, NB + 3, 6)

        @block.tensor
        def _(pe):
            pe.wait_ge(consts, n_consts)
            pe.wait_ge(blank, 5)
            pe.wait_ge(ready, 8)

            def slot(t):
                a = t.at(3)
                if a.there:
                    loaded(pe, xl, a)
                    freed(pe, s_u, a, 1, 4)
                    freed(pe, s_xc, a, 1)
                    done(pe, s_x2, a, 2)
                    for f in range(2):
                        pe.transpose(p_tr[:, f * P:(f + 1) * P],
                                     x2[:, a.buf(2), f].rearrange("p h c d -> p (h c d)"), idn[:, :])
                    pe.transpose(p_tr[:, 2 * P:3 * P], x_t[:, a.buf(4), :], idn[:, :]).then_inc(s_tr, 1)
                def scores(g):
                    if g == 3:
                        done(pe, s_ex, t, 4, 1)
                    elif t.at(-1).there:
                        done(pe, s_ex, t.at(-1), 4, 4 if g == 0 else g + 1)
                    if g >= 2:
                        pe.matmul(p_st[g % 3][:, :], idn_b[:, :], tri4[:, :, :], start=True, stop=False,
                                  skip_group_check=True)
                    for j in range(4):
                        h = 4 * g + j
                        mm = pe.matmul(p_st[g % 3][:, j * P:(j + 1) * P], kd[:, t.buf(2), h, :],
                                       sn[:, t.buf(4), h // 8, :], start=(g < 2), stop=True, skip_group_check=True)
                    mm.then_inc(s_st, 1)

                if t.there:
                    done(pe, s_kd, t, 2)
                    scores(0)
                    scores(1)
                o = t.at(-2)
                if o.there:
                    done(pe, s_ot, o)
                    freed(pe, s_oc, o, 1)
                    pe.transpose(p_oT[:, 0:P], o_tok[:, o.buf(2), :], idn[:, :]).then_inc(s_oT, 1)
                if a.there:
                    done(pe, s_xc, a)
                    if t.at(-3).there:
                        done(pe, s_z, t.at(-3))
                    elif a.at(-1).there:
                        done(pe, s_v, a.at(-1))
                    pe.matmul(p_pj[:, 0:P], xT[:, a.buf(2), :], wv_s[:, :], start=True, stop=True).then_inc(s_pj, 1)
                v = t.at(-1)
                if v.there:
                    done(pe, s_ex, v, 4)
                    done(pe, s_mk, v, 2)
                    freed(pe, s_o1, v, 1)
                    for k in range(4):
                        for c in range(4):
                            h = 4 * c + k
                            mm = pe.matmul(p_pv[32 * c:32 * c + 32, k * P:(k + 1) * P], va[:, v.buf(4), h, :],
                                           probs[:, v.buf(2), h, :], start=True, stop=True)
                    mm.then_inc(s_pv, 1)
                if t.there:
                    scores(2)
                    scores(3)
                if o.there:
                    done(pe, s_oc, o)
                    if a.there:
                        done(pe, s_v, a)
                    else:
                        done(pe, s_z, o.at(-1))
                    pe.matmul(p_pj[:, 0:P], oT[:, o.buf(2), :], wo_s[:, :], start=True, stop=True).then_inc(s_y, 1)
                if v.there:
                    done(pe, s_o1, v)
                    freed(pe, s_ot, v, 1)
                    for k in range(4):
                        mm = pe.transpose(p_on[:, k * P:(k + 1) * P], o1[:, v.buf(2), k, :], idn[:, :])
                    mm.then_inc(s_on, 1)

            run_slots(pe, slot, -3, NB + 2, 6)

        @block.scalar
        def _(act):
            act.wait_ge(ready, 8)

            def slot(t):
                a = t.at(3)
                if a.there:
                    done(act, s_tr, a)
                    freed(act, s_pj, a, 2)
                    act.copy(xT[:, a.buf(2), :], p_tr[:, 2 * P:3 * P]).then_inc(s_xc, 1)
                    freed(act, s_nr, a, 2)
                    for f in range(4):
                        act.activation(u[:, a.buf(2), f, :], p_tr[:, (f % 2) * P:(f % 2 + 1) * P], ACT.Identity,
                                       scale=sc[:, f:f + 1], bias=bi[:, f:f + 1]).then_inc(s_u, 1)
                def exps(g):
                    done(act, s_st, t, 4, g + 1)
                    act.activation(probs[:, t.buf(2), 4 * g:4 * g + 4, :], p_st[g % 3][:, :], ACT.Exp,
                                   scale=float(2 * DK) ** -0.5).then_inc(s_ex, 1)

                if t.there:
                    freed(act, s_pv, t, 2)
                    exps(0)
                    exps(1)
                v = t.at(-1)
                if v.there:
                    done(act, s_pv, v)
                    freed(act, s_on, v, 2)
                    act.copy(o1[:, v.buf(2), :, :], p_pv[:, :]).then_inc(s_o1, 1)
                if t.there:
                    exps(2)
                    exps(3)
                if t.off % 2 == 0 and a.there:
                    done(act, s_an, a)
                    if a.at(-4).there:
                        done(act, s_st, a.at(-4), 4)
                        done(act, s_kd, a.at(-4), 2)
                    b = a.at(-1).buf(4)
                    act.activation(sn[:, b:b + 2, :, :], an[:, :, :, :], ACT.Sin, scale=SCALE).then_inc(s_sn, 2)

            run_slots(act, slot, -3, NB + 1, 6)

        @block.vector
        def _(dve):
            dve.wait_ge(consts, n_consts)
            dve.wait_ge(blank, 5)
            dve.scalar_tensor_tensor(wa[:, :], w_s[:, :], -1.0, w_s[:, :], ALU.mult, ALU.max).then_inc(ready, 1)
            dve.wait_ge(ready, 1)
            dve.tensor_scalar(wa[:, :], wa[:, :], 1.0, None, ALU.add).then_inc(ready, 1)
            dve.wait_ge(ready, 2)
            dve.reciprocal(wr[:, :], wa[:, :]).then_inc(ready, 1)
            dve.wait_ge(ready, 3)
            dve.tensor_scalar(sc[:, :], wr[:, :], 1.0 / STEP, None, ALU.mult).then_inc(ready, 1)
            dve.tensor_scalar(keep[:, :], tri[:, :], 0.0, None, ALU.is_equal).then_inc(ready, 1)
            dve.tensor_copy(idn_b[:, :], idn[:, :]).then_inc(ready, 1)
            dve.tensor_copy(tri4[:, :, :], tri[:, :].unsqueeze(1).broadcast_to([P, 4, P])).then_inc(ready, 1)
            dve.tensor_scalar(bi[:, :], b_s[:, :], 1.0 / STEP, quar[:, :], ALU.mult, ALU.add).then_inc(ready, 1)

            def slot(t):
                a = t.at(3)
                if a.there:
                    done(dve, s_u, a, 4)
                    freed(dve, s_an, a, 2)
                    b = a.buf(2)
                    dve.tensor_scalar(nr[:, b], u[:, b], ROUND, ROUND, ALU.add, ALU.subtract).then_inc(s_nr, 1)
                    done(dve, s_nr, a)
                    dve.tensor_scalar(lap[:, b], nr[:, b], 1.0 / LUT, ROUND, ALU.mult, ALU.add).then_inc(s_lp, 1)
                    done(dve, s_lp, a)
                    dve.tensor_scalar(off[:, b], lap[:, b], ROUND, -float(LUT), ALU.subtract, ALU.mult).then_inc(s_of, 1)
                    done(dve, s_of, a)
                    freed(dve, s_sn, a, 2)
                    dve.tensor_tensor(an[:, b], nr[:, b], off[:, b], ALU.add).then_inc(s_an, 1)
                o = t.at(-2)
                if o.there:
                    done(dve, s_oT, o)
                    freed(dve, s_y, o, 2)
                    dve.tensor_copy(oT[:, o.buf(2), :], p_oT[:, 0:P]).then_inc(s_oc, 1)
                if a.there:
                    done(dve, s_pj, a)
                    freed(dve, s_pv, a, 4)
                    dve.tensor_copy(va[:, a.buf(4), :, 0:DK],
                                    p_pj[:, 0:P].rearrange("p (h d) -> p h d", d=DK)).then_inc(s_v, 1)
                if t.there:
                    for g in range(2):
                        done(dve, s_ex, t, 4, g + 1)
                        pr = probs[:, t.buf(2), 4 * g:4 * g + 4, :]
                        dve.tensor_tensor(pr, pr, keep[:, :].unsqueeze(1).broadcast_to([P, 4, P]),
                                          ALU.mult).then_inc(s_mk, 1)
                n = t.at(-3)
                if n.there:
                    done(dve, s_rs, n)
                    if n.at(-4).there:
                        loaded(dve, stored, n.at(-4))
                    dve.tensor_scalar(y_t[:, n.buf(4), :], z[:, n.buf(2), :], mv[:, n.buf(2), 0:1],
                                      rstd[:, n.buf(2), :], ALU.subtract, ALU.mult).then_inc(s_ln, 1)
                if o.there:
                    done(dve, s_y, o)
                    loaded(dve, rl, o)
                    freed(dve, s_ln, o, 2)
                    dve.tensor_tensor(z[:, o.buf(2), :], p_pj[:, 0:P], xr_t[:, o.buf(2), :], ALU.add).then_inc(s_z, 1)
                    done(dve, s_z, o)
                    dve.bn_stats(stats[:, o.buf(2), :], z[:, o.buf(2), :]).then_inc(s_bs, 1)
                    done(dve, s_bs, o)
                    freed(dve, s_ve, o, 2)
                    dve.tensor_copy(mark[:, :], stats[:, o.buf(2), 0:1])
                    dve.bn_aggr(mv[:, o.buf(2), :], stats[:, o.buf(2), :]).then_inc(s_mv, 1)
                v = t.at(-1)
                if v.there:
                    done(dve, s_on, v)
                    on = p_on[:, :].rearrange("p (k c e) -> p k c e", k=4, c=4)
                    freed(dve, s_ot, v, 2)
                    dve.reciprocal(rden[:, v.buf(2), :, :], on[:, :, :, DK]).then_inc(s_rd, 1)
                    done(dve, s_rd, v)
                    freed(dve, s_oT, v, 2)
                    dve.tensor_tensor(o_tok[:, v.buf(2), :].rearrange("p (c k d) -> p k c d", c=4, k=4),
                                      on[:, :, :, 0:DK],
                                      rden[:, v.buf(2), :, :].unsqueeze(3).broadcast_to([P, 4, 4, DK]),
                                      ALU.mult).then_inc(s_ot, 1)

            run_slots(dve, slot, -3, NB + 3, 6)


def linear_attention(nc, name, banks, x_in, x_out, wq, wk, wv, wo, bq, bk, bv, bo, feat, norm, ident, own_head):
    M = 32
    G = 4
    VW = DK + 1
    root = float(DK) ** -0.25
    ph = Phase(nc, name, banks)
    with ph:
        sb, ps, sem = ph.sb, ph.ps, ph.sem
        idn = sb("idn", [P, P]); own = sb("own", [P, H, VW])
        wq_s, wk_s, wv_s, wo_s = (sb(f"w{k}", [P, P]) for k in "qkvo")
        bq_s, bk_s = sb("bq", [P, 1]), sb("bk", [P, 1])
        bv_s, bo_s = sb("bv", [P, P]), sb("bo", [P, P])
        ft_raw, ft, nm = sb("ft_raw", [P, H * M]), sb("ft", [P, H * M]), sb("nm", [P, H * M])
        half, eps = sb("half", [P, 1]), sb("eps", [P, 1]); lnm = sb("lnm", [P, 1])
        bqs, bks = sb("bqs", [P, 1]), sb("bks", [P, 1])
        ft_h, ft_l, nm_h = sb("ft_high", [P, H * M]), sb("ft_low", [P, H * M]), sb("nm_high", [P, H * M])
        k_h, k_l = sb("k_high", [P, 2, P]), sb("k_low", [P, 2, P])
        ks_h, ks_l = sb("ks_high", [P, 2, P]), sb("ks_low", [P, 2, P])
        x_t = sb("x", [P, 4, P]); xr_t = sb("xr", [P, 2, P]); xb_t = sb("xb", [P, 2, P])
        xT = sb("xT", [P, 2, P])
        qT = sb("qT", [P, 2, P]); qs = sb("qs", [P, 2, P]); kT = sb("kT", [P, 2, P]); ks = sb("ks", [P, 2, P])
        va = sb("va", [P, 4, H, VW])
        ek = sb("ek", [P, 2, H * M]); eq = sb("eq", [P, 2, G, P])
        kvm = sb("kvm", [P, 2, H, VW]); rden = sb("rden", [P, 2, H])
        o_tok = sb("o_tok", [P, 2, P]); oT = sb("oT", [P, 2, P])
        z = sb("z", [P, 2, P]); mark = sb("mark", [P, 1]); stats = sb("stats", [P, 2, 6]); mv = sb("mv", [P, 2, 2])
        vare = sb("vare", [P, 2, 1]); rstd = sb("rstd", [P, 2, 1]); y_t = sb("y", [P, 4, P])
        p_tr, p_oT, p_pj, p_y = ps(), ps(), ps(), ps()
        p_zq, p_zk, p_kv, p_on = ps(), ps(), ps(), ps()

        consts = sem("consts_loaded"); ready = sem("feat_ready"); blank = sem("blanks_ready")
        xl, rl, stored = sem("x_loaded", 4), sem("xr_loaded", 2), sem("y_stored", 4)
        s_tr = sem("x_transposed"); s_xc = sem("x_copied"); s_pj = sem("qkv_projected")
        s_q = sem("q_and_k_ready"); s_v = sem("v_ready"); s_zq = sem("zq_done"); s_zk = sem("zk_done")
        s_eq = sem("q_features"); s_ek = sem("k_features"); s_kv = sem("kv_done"); s_kc = sem("kv_copied")
        s_on = sem("outputs_done"); s_rd = sem("reciprocals_ready")
        s_ot = sem("o_normalised"); s_oT = sem("o_transposed"); s_oc = sem("o_copied"); s_y = sem("y_projected")
        s_kh = sem("k_high_parts"); s_kl = sem("k_low_parts"); s_ee = sem("k_features_raised")
        s_qe = sem("q_features_raised")
        s_xb = sem("residual_ready"); s_z = sem("z_ready"); s_bs = sem("stats_ready"); s_mv = sem("mean_var_ready")
        s_ve = sem("var_eps_ready"); s_rs = sem("rstd_ready"); s_ln = sem("normed")

        block = ph.ctx.enter_context(nc.Block())
        n_consts = 16 * 12

        @block.sync
        def _(sp):
            for dst, src in ((idn[:, :], ident), (own[:, :, :], own_head), (wq_s[:, :], wq), (wk_s[:, :], wk),
                             (wv_s[:, :], wv), (wo_s[:, :], wo), (bq_s[:, :], bq), (bk_s[:, :], bk),
                             (bv_s[:, :], bv.partition_broadcast(P)), (bo_s[:, :], bo.partition_broadcast(P)),
                             (ft_raw[:, :], feat), (nm[:, :], norm)):
                sp.dma_start(dst, src).then_inc(consts, 16)

            def slot(t):
                a = t.at(4)
                if a.there:
                    freed(sp, s_tr, a, 4)
                    sp.dma_start(x_t[:, a.buf(4), :], x_in[a.n]).then_inc(xl[a.buf(4)], 16)
                if t.there:
                    freed(sp, s_xb, t, 2)
                    sp.dma_start(xr_t[:, t.buf(2), :], x_in[t.n]).then_inc(rl[t.buf(2)], 16)
                o = t.at(-2)
                if o.there:
                    done(sp, s_ln, o)
                    sp.dma_start(x_out[o.n], y_t[:, o.buf(4), :]).then_inc(stored[o.buf(4)], 16)

            run_slots(sp, slot, -4, NB + 2)
            for k in range(4):
                sp.wait_ge(stored[k], 16 * NB // 4)

        @block.gpsimd
        def _(pool):
            pool.memset(va[:, :, :, DK:DK + 1], 1.0).then_inc(blank, 1)
            pool.memset(half[:, :], -0.5).then_inc(blank, 1)
            pool.memset(eps[:, :], EPS_LN).then_inc(blank, 1)
            pool.memset(lnm[:, :], -1.7328679513998633).then_inc(blank, 1)
            pool.wait_ge(blank, 4)
            pool.wait_ge(consts, n_consts)

            def slot(t):
                n = t.at(-2)
                if n.there:
                    done(pool, s_mv, n)
                    freed(pool, s_rs, n, 2)
                    pool.tensor_tensor(vare[:, n.buf(2), :], mv[:, n.buf(2), 1:2], eps[:, :], ALU.add).then_inc(s_ve, 1)
                    done(pool, s_ve, n)
                    freed(pool, s_ln, n, 2)
                    pool.tensor_tensor(rstd[:, n.buf(2), :], vare[:, n.buf(2), :], half[:, :],
                                       ALU.pow).then_inc(s_rs, 1)
                if t.there:
                    loaded(pool, rl, t)
                    freed(pool, s_z, t, 2)
                    pool.tensor_tensor(xb_t[:, t.buf(2), :], xr_t[:, t.buf(2), :], bo_s[:, :],
                                       ALU.add).then_inc(s_xb, 1)

            run_slots(pool, slot, 0, NB + 2)

        @block.tensor
        def _(pe):
            pe.wait_ge(consts, n_consts)
            pe.wait_ge(blank, 4)
            pe.wait_ge(ready, 6)

            def slot(t):
                a = t.at(2)
                if a.there:
                    loaded(pe, xl, a)
                    freed(pe, s_xc, a, 1)
                    pe.transpose(p_tr[:, 0:P], x_t[:, a.buf(4), :], idn[:, :]).then_inc(s_tr, 1)
                if t.there:
                    done(pe, s_ee, t)
                    freed(pe, s_kc, t, 1)
                    for g in range(G):
                        mm = pe.matmul(p_kv[:, 4 * g * VW:4 * (g + 1) * VW], ek[:, t.buf(2), g * P:(g + 1) * P],
                                       va[:, t.buf(4), 4 * g:4 * g + 4, :], start=True, stop=True)
                    mm.then_inc(s_kv, 1)
                if a.there:
                    done(pe, s_xc, a)
                    freed(pe, s_v, a, 1)
                    freed(pe, s_q, a, 1, 4)
                    x = xT[:, a.buf(2), :]
                    pe.matmul(p_pj[:, 0:P], wq_s[:, :], x, start=True, stop=True)
                    pe.matmul(p_pj[:, P:2 * P], wk_s[:, :], x, start=True, stop=True)
                    pe.matmul(p_pj[:, 2 * P:3 * P], x, wv_s[:, :], start=True, stop=True).then_inc(s_pj, 1)
                o = t.at(-1)
                if o.there:
                    done(pe, s_ot, o)
                    freed(pe, s_oc, o, 1)
                    pe.transpose(p_oT[:, 0:P], o_tok[:, o.buf(2), :], idn[:, :]).then_inc(s_oT, 1)
                b = t.at(1)
                if b.there:
                    done(pe, s_kl, b, 2)
                    freed(pe, s_ek, b, 1)
                    i = b.buf(2)
                    products(pe, p_zk[:, :], k_h[:, i, :], k_l[:, i, :], ft_h[:, :], ft_l[:, :], stop=False)
                    pe.matmul(p_zk[:, :], ks_h[:, i, :].bitcast(F32R), nm_h[:, :].bitcast(F32R), start=False,
                              stop=False)
                    pe.matmul(p_zk[:, :], ks_l[:, i, :].bitcast(F32R), nm_h[:, :].bitcast(F32R), start=False,
                              stop=True).then_inc(s_zk, 1)
                if t.there:
                    done(pe, s_kc, t)
                    done(pe, s_qe, t)
                    freed(pe, s_ot, t, 1)
                    for g in range(G):
                        mm = pe.matmul(p_on[:, 4 * g * VW:4 * (g + 1) * VW], eq[:, t.buf(2), g, :],
                                       kvm[:, t.buf(2), 4 * g:4 * g + 4, :], start=True, stop=True)
                    mm.then_inc(s_on, 1)
                if b.there:
                    done(pe, s_q, b, 4)
                    freed(pe, s_eq, b, 1)
                    for g in range(G):
                        out = p_zq[:, g * P:(g + 1) * P]
                        pe.matmul(out, ft[:, g * P:(g + 1) * P], qT[:, b.buf(2), :], start=True, stop=False)
                        mm = pe.matmul(out, nm[:, g * P:(g + 1) * P], qs[:, b.buf(2), :], start=False, stop=True)
                    mm.then_inc(s_zq, 1)
                if o.there:
                    done(pe, s_oc, o)
                    freed(pe, s_z, o, 1)
                    pe.matmul(p_y[:, 0:P], oT[:, o.buf(2), :], wo_s[:, :], start=True, stop=True).then_inc(s_y, 1)

            run_slots(pe, slot, -2, NB + 1)

        @block.scalar
        def _(act):
            act.wait_ge(consts, n_consts)
            act.wait_ge(ready, 6)
            act.wait_ge(blank, 4)

            def slot(t):
                a = t.at(2)
                if a.there:
                    done(act, s_tr, a)
                    freed(act, s_pj, a, 2)
                    act.copy(xT[:, a.buf(2), :], p_tr[:, 0:P]).then_inc(s_xc, 1)
                    done(act, s_pj, a)
                    freed(act, s_zq, a, 2)
                    freed(act, s_kl, a, 2, 2)
                    for dst, fn, k, bias, scale in ((qT, ACT.Identity, 0, bq_s, 1.0), (qs, ACT.Square, 0, bqs, root),
                                                    (kT, ACT.Identity, 1, bk_s, 1.0), (ks, ACT.Square, 1, bks, root)):
                        act.activation(dst[:, a.buf(2), :], p_pj[:, k * P:(k + 1) * P], fn,
                                       bias=bias[:, :], scale=scale).then_inc(s_q, 1)
                b = t.at(1)
                if b.there:
                    done(act, s_zk, b)
                    freed(act, s_kv, b, 2)
                    act.activation(ek[:, b.buf(2), :], p_zk[:, :], ACT.Exp, bias=lnm[:, :]).then_inc(s_ek, 1)
                    done(act, s_zq, b)
                    freed(act, s_on, b, 2)
                    act.activation(eq[:, b.buf(2)], p_zq[:, :], ACT.Exp, bias=lnm[:, :]).then_inc(s_eq, 1)

            run_slots(act, slot, -2, NB)

        @block.vector
        def _(dve):
            dve.wait_ge(consts, n_consts)
            dve.wait_ge(blank, 4)
            dve.tensor_scalar(ft[:, :], ft_raw[:, :], root, None, ALU.mult).then_inc(ready, 1)
            dve.tensor_scalar(bqs[:, :], bq_s[:, :], root, None, ALU.mult).then_inc(ready, 1)
            dve.tensor_scalar(bks[:, :], bk_s[:, :], root, None, ALU.mult).then_inc(ready, 1)
            high(dve, nm_h[:, :], nm[:, :]).then_inc(ready, 1)
            dve.wait_ge(ready, 4)
            high(dve, ft_h[:, :], ft[:, :]).then_inc(ready, 1)
            dve.wait_ge(ready, 5)
            low(dve, ft_l[:, :], ft[:, :], ft_h[:, :]).then_inc(ready, 1)

            def slot(t):
                if t.there:
                    done(dve, s_kv, t)
                    freed(dve, s_on, t, 2)
                    dve.tensor_tensor(kvm[:, t.buf(2)], p_kv[:, 0:H * VW], own[:, :, :],
                                      ALU.mult).then_inc(s_kc, 1)
                a = t.at(2)
                if a.there:
                    done(dve, s_pj, a)
                    done(dve, s_q, a, 4)
                    freed(dve, s_kv, a, 4)
                    dve.tensor_tensor(va[:, a.buf(4), :, 0:DK], p_pj[:, 2 * P:3 * P].rearrange("p (h d) -> p h d", d=DK),
                                      bv_s[:, :].rearrange("p (h d) -> p h d", d=DK), ALU.add).then_inc(s_v, 1)
                    i = a.buf(2)
                    freed(dve, s_zk, a, 2)
                    high(dve, k_h[:, i, :], kT[:, i, :]).then_inc(s_kh, 1)
                    high(dve, ks_h[:, i, :], ks[:, i, :]).then_inc(s_kh, 1)
                    done(dve, s_kh, a, 2)
                    low(dve, k_l[:, i, :], kT[:, i, :], k_h[:, i, :]).then_inc(s_kl, 1)
                    low(dve, ks_l[:, i, :], ks[:, i, :], ks_h[:, i, :]).then_inc(s_kl, 1)
                n = t.at(-2)
                if n.there:
                    done(dve, s_rs, n)
                    if n.at(-4).there:
                        loaded(dve, stored, n.at(-4))
                    dve.tensor_scalar(y_t[:, n.buf(4), :], z[:, n.buf(2), :], mv[:, n.buf(2), 0:1],
                                      rstd[:, n.buf(2), :], ALU.subtract, ALU.mult).then_inc(s_ln, 1)
                o = t.at(-1)
                if o.there:
                    done(dve, s_oT, o)
                    freed(dve, s_y, o, 2)
                    dve.tensor_copy(oT[:, o.buf(2), :], p_oT[:, 0:P]).then_inc(s_oc, 1)
                b = t.at(1)
                if b.there:
                    done(dve, s_ek, b)
                    dve.tensor_scalar(ek[:, b.buf(2), :], ek[:, b.buf(2), :], 1e-6 / M ** 0.5, None,
                                      ALU.add).then_inc(s_ee, 1)
                if t.there:
                    done(dve, s_on, t)
                    on = p_on[:, 0:H * VW].rearrange("p (h e) -> p h e", e=VW)
                    freed(dve, s_ot, t, 2)
                    dve.reciprocal(rden[:, t.buf(2), :], on[:, :, DK]).then_inc(s_rd, 1)
                    done(dve, s_rd, t)
                    freed(dve, s_oT, t, 2)
                    dve.tensor_tensor(o_tok[:, t.buf(2), :].rearrange("p (h d) -> p h d", d=DK), on[:, :, 0:DK],
                                      rden[:, t.buf(2), :].unsqueeze(2).broadcast_to([P, H, DK]),
                                      ALU.mult).then_inc(s_ot, 1)
                if o.there:
                    done(dve, s_y, o)
                    done(dve, s_xb, o)
                    freed(dve, s_ln, o, 2)
                    dve.tensor_tensor(z[:, o.buf(2), :], p_y[:, 0:P], xb_t[:, o.buf(2), :], ALU.add).then_inc(s_z, 1)
                    done(dve, s_z, o)
                    dve.bn_stats(stats[:, o.buf(2), :], z[:, o.buf(2), :]).then_inc(s_bs, 1)
                    done(dve, s_bs, o)
                    freed(dve, s_ve, o, 2)
                    dve.tensor_copy(mark[:, :], stats[:, o.buf(2), 0:1])
                    dve.bn_aggr(mv[:, o.buf(2), :], stats[:, o.buf(2), :]).then_inc(s_mv, 1)
                if b.there:
                    done(dve, s_eq, b)
                    dve.tensor_scalar(eq[:, b.buf(2)], eq[:, b.buf(2)], 1e-6 / M ** 0.5, None,
                                      ALU.add).then_inc(s_qe, 1)

            run_slots(dve, slot, -2, NB + 2)


CT = 4
NC = NB // CT


def run_chunks(eng, body):
    body(0)
    with eng.Fori(1, NC) as c:
        body(c)


def later(c):
    return not isinstance(c, int) or c > 0


def has(c):
    return not isinstance(c, int) or 0 <= c < NC


def since(eng, sem, count):
    if not isinstance(count, int) or count > 0:
        eng.wait_ge(sem, count)


def run_paired(eng, slot):
    for c in (0, 1):
        slot(c, c, 0)
    with eng.Fori(1, NC // 2 - 1) as lap:
        for u in (0, 1):
            slot(2 * lap + u, u, lap)
    for c in (NC - 2, NC - 1, NC):
        slot(c, c % 2, c // 2)


def run_staggered(eng, slot):
    slot(0)
    slot(1)
    with eng.Fori(2, NC - 1) as c:
        slot(c)
    slot(NC - 1)
    slot(NC)


def feed_forward(nc, name, banks, x_in, x_out, w1, w2, h1, h2, w3, s_hidden, s_out, ident):
    F = 4
    ph = Phase(nc, name, banks)
    with ph:
        sb, ps, sem = ph.sb, ph.ps, ph.sem
        idn = sb("idn", [P, P])
        w1_s, w2_s = sb("w1", [P, F * P]), sb("w2", [P, F * P])
        w1_h, w2_h = sb("w1_high", [P, F * P]), sb("w2_high", [P, F * P])
        w1_l, w2_l = sb("w1_low", [P, F * P]), sb("w2_low", [P, F * P])
        h1_s, h2_s, w3_s = sb("h1", [P, F, F * P]), sb("h2", [P, F, F * P]), sb("w3", [P, F, P])
        h1_h, h2_h = sb("h1_high", [P, F, F * P]), sb("h2_high", [P, F, F * P])
        h1_l, h2_l = sb("h1_low", [P, F, F * P]), sb("h2_low", [P, F, F * P])
        sh = sb("sh", [P, 4, F])
        so = sb("so", [P, P]); w3_o = sb("w3o", [P, F, P])
        half, eps = sb("half", [P, CT]), sb("eps", [P, CT])
        x_t = sb("x", [P, CT, P]); xr_t = sb("xr", [P, CT, P])
        xT = sb("xT", [P, CT, P]); xT_h = sb("xT_high", [P, CT, P]); xT_l = sb("xT_low", [P, CT, P])
        gate = sb("gate", [P, 2, CT * P])
        a0, a0_h, a0_l = sb("a0", [P, F, CT * P]), sb("a0_high", [P, F, CT * P]), sb("a0_low", [P, F, CT * P])
        a1, a1_h, a1_l = sb("a1", [P, F, CT * P]), sb("a1_high", [P, F, CT * P]), sb("a1_low", [P, F, CT * P])
        a2 = sb("a2", [P, F, CT * P])
        z = sb("z", [P, CT, P]); mark = sb("mark", [P, CT]); stats = sb("stats", [P, CT, 6])
        mv = sb("mv", [P, CT, 2]); vare = sb("vare", [P, CT]); rstd = sb("rstd", [P, CT])
        y_t = sb("y", [P, CT, P])
        p_u = [ps(), ps()]; p_v = [ps(), ps()]
        p_h = [ps(), ps()]; p_tr, p_y = ps(), ps()

        consts = sem("gate_loaded"); hidden = sem("hidden_loaded")
        ready = sem("w3_scaled"); blank = sem("blanks_ready")
        s_wh = sem("weights_high"); s_wl = sem("weights_low")
        xl, rl, stored = sem("x_loaded"), sem("xr_loaded"), sem("y_stored")
        s_tr = sem("x_transposed"); s_xc = sem("x_copied"); s_xh = sem("x_high"); s_xl = sem("x_low")
        s_u = sem("u_done"); s_v = sem("v_done"); s_g = sem("gate_ready"); s_a0 = sem("a0_ready")
        s_h0 = sem("a0_high_ready"); s_l0 = sem("a0_low_ready")
        s_m1 = sem("h1_done"); s_a1 = sem("a1_ready"); s_m2 = sem("h2_done"); s_a2 = sem("a2_ready")
        s_h1 = sem("a1_high_ready"); s_l1 = sem("a1_low_ready")
        s_y = sem("y_done"); s_z = sem("z_ready"); s_bs = sem("stats_ready"); s_mv = sem("mean_var_ready")
        s_ve = sem("var_eps_ready"); s_rs = sem("rstd_ready"); s_ln = sem("normed")

        block = ph.ctx.enter_context(nc.Block())

        def rows(a):
            return a.rearrange("t p d -> p t d")

        @block.sync
        def _(sp):
            sp.dma_start(x_t[:, :, :], rows(x_in[0])).then_inc(xl, 16)
            for dst, src in ((idn[:, :], ident), (sh[:, :, :], s_hidden), (w1_s[:, :], w1), (w2_s[:, :], w2)):
                sp.dma_start(dst, src).then_inc(consts, 16)
            for dst, src in ((h1_s[:, :, :], h1), (h2_s[:, :, :], h2), (w3_s[:, :, :], w3),
                             (so[:, :], s_out.partition_broadcast(P))):
                sp.dma_start(dst, src).then_inc(hidden, 16)

            def slot(c):
                if has(c + 1):
                    sp.wait_ge(s_tr, c + 1)
                    sp.dma_start(x_t[:, :, :], rows(x_in[c + 1])).then_inc(xl, 16)
                if has(c - 1):
                    since(sp, s_z, c - 1)
                    sp.dma_start(xr_t[:, :, :], rows(x_in[c - 1])).then_inc(rl, 16)
                if has(c - 2):
                    sp.wait_ge(s_ln, 4 * (c - 1))
                    sp.dma_start(rows(x_out[c - 2]), y_t[:, :, :]).then_inc(stored, 16)

            run_staggered(sp, slot)
            sp.wait_ge(s_ln, 4 * NC)
            sp.dma_start(rows(x_out[NC - 1]), y_t[:, :, :]).then_inc(stored, 16)
            sp.wait_ge(stored, 16 * NC)

        @block.gpsimd
        def _(pool):
            pool.memset(half[:, :], -0.5).then_inc(blank, 1)
            pool.memset(eps[:, :], EPS_LN).then_inc(blank, 1)
            pool.wait_ge(blank, 2)
            for n, (w_l, w, w_h) in enumerate(((w1_l[:, :], w1_s[:, :], w1_h[:, :]),
                                               (w2_l[:, :], w2_s[:, :], w2_h[:, :]),
                                               (h1_l[:, :, :], h1_s[:, :, :], h1_h[:, :, :]),
                                               (h2_l[:, :, :], h2_s[:, :, :], h2_h[:, :, :]))):
                pool.wait_ge(s_wh, n + 1)
                low(pool, w_l, w, w_h).then_inc(s_wl, 1)

            def slot(c):
                if has(c - 1):
                    pool.wait_ge(s_mv, 4 * c)
                    pool.tensor_tensor(vare[:, :], mv[:, :, 1], eps[:, :], ALU.add).then_inc(s_ve, 1)
                    pool.wait_ge(s_ve, c)
                    since(pool, s_ln, 4 * (c - 1))
                    pool.tensor_tensor(rstd[:, :], vare[:, :], half[:, :], ALU.pow).then_inc(s_rs, 1)

            run_staggered(pool, slot)

        @block.tensor
        def _(pe):
            def transposes(c):
                pe.wait_ge(xl, 16 * (c + 1))
                since(pe, s_xc, c)
                for k in range(CT):
                    mm = pe.transpose(p_tr[:, k * P:(k + 1) * P], x_t[:, k, :], idn[:, :])
                mm.then_inc(s_tr, 1)

            def gated(c):
                pe.wait_ge(s_xl, c + 1)
                for m in range(F):
                    cols = slice(m * P, (m + 1) * P)
                    since(pe, s_a0, F * c + m - 1)
                    products(pe, p_u[m % 2][:, :], w1_h[:, cols], w1_l[:, cols], xT_h[:, :, :],
                             xT_l[:, :, :]).then_inc(s_u, 1)
                    products(pe, p_v[m % 2][:, :], w2_h[:, cols], w2_l[:, cols], xT_h[:, :, :],
                             xT_l[:, :, :]).then_inc(s_v, 1)

            def hidden_layer(c, w_l, w_h, a_l, a_h, s_low, s_done, s_read, s_before):
                for m in range(F):
                    if m >= 2:
                        pe.wait_ge(s_read, F * c + m - 1)
                    else:
                        since(pe, *s_before(m))
                    cols = slice(m * P, (m + 1) * P)
                    for k in range(F):
                        if m == 0:
                            pe.wait_ge(s_low, F * c + k + 1)
                        mm = products(pe, p_h[m % 2][:, :], w_h[:, k, cols], w_l[:, k, cols], a_h[:, k, :],
                                      a_l[:, k, :], start=(k == 0), stop=(k == F - 1))
                    mm.then_inc(s_done, 1)

            def output(c):
                since(pe, s_z, c)
                pe.wait_ge(s_a2, F * c + F)
                for j in range(CT):
                    for k in range(F):
                        mm = pe.matmul(p_y[:, j * P:(j + 1) * P], a2[:, k, j * P:(j + 1) * P], w3_o[:, k, :],
                                       start=(k == 0), stop=(k == F - 1))
                mm.then_inc(s_y, 1)

            def slot(c):
                first = isinstance(c, int) and c == 0
                if has(c):
                    gated(c)
                if has(c - 1):
                    output(c - 1)
                if has(c):
                    if first:
                        pe.wait_ge(s_wl, 3)
                    hidden_layer(c, h1_l, h1_h, a0_l, a0_h, s_l0, s_m1, s_a1, lambda m: (s_a2, F * c - 2 + m + 1))
                if has(c + 1):
                    transposes(c + 1)
                if has(c):
                    if first:
                        pe.wait_ge(s_wl, 4)
                        pe.wait_ge(ready, F)
                    hidden_layer(c, h2_l, h2_h, a1_l, a1_h, s_l1, s_m2, s_a2, lambda m: (s_a1, F * c + m + 3))

            pe.wait_ge(consts, 64)
            transposes(0)
            pe.wait_ge(s_wl, 2)
            run_staggered(pe, slot)

        @block.scalar
        def _(act):
            def copy_x(c):
                act.wait_ge(s_tr, c + 1)
                since(act, s_v, F * c)
                act.copy(xT[:, :, :], p_tr[:, :]).then_inc(s_xc, 1)

            def slot(c):
                if has(c):
                    for m in range(F):
                        act.wait_ge(s_u, F * c + m + 1)
                        since(act, s_a0, F * c + m - 1)
                        act.activation(gate[:, m % 2, :], p_u[m % 2][:, :], ACT.Silu,
                                       scale=sh[:, 0, m:m + 1]).then_inc(s_g, 1)
                    for m in range(F):
                        act.wait_ge(s_m1, F * c + m + 1)
                        if m == 0:
                            since(act, s_m2, F * c)
                        act.activation(a1[:, m, :], p_h[m % 2][:, :], ACT.Gelu,
                                       scale=sh[:, 2, m:m + 1]).then_inc(s_a1, 1)
                if has(c + 1):
                    copy_x(c + 1)
                if has(c):
                    for m in range(F):
                        act.wait_ge(s_m2, F * c + m + 1)
                        if m == 0:
                            since(act, s_y, c)
                        act.activation(a2[:, m, :], p_h[m % 2][:, :], ACT.Gelu,
                                       scale=sh[:, 3, m:m + 1]).then_inc(s_a2, 1)

            act.wait_ge(consts, 64)
            copy_x(0)
            run_staggered(act, slot)

        @block.vector
        def _(dve):
            def split(whole, high_part, low_part, s_whole, s_high, s_low, count):
                dve.wait_ge(s_whole, count)
                high(dve, high_part, whole).then_inc(s_high, 1)
                dve.wait_ge(s_high, count)
                low(dve, low_part, whole, high_part).then_inc(s_low, 1)

            def split_x(c):
                since(dve, s_v, F * c)
                split(xT[:, :, :], xT_h[:, :, :], xT_l[:, :, :], s_xc, s_xh, s_xl, c + 1)

            def slot(c):
                if has(c):
                    since(dve, s_m1, F * c)
                    for m in range(F):
                        dve.wait_ge(s_g, F * c + m + 1)
                        dve.wait_ge(s_v, F * c + m + 1)
                        dve.scalar_tensor_tensor(a0[:, m, :], p_v[m % 2][:, :], sh[:, 1, m:m + 1],
                                                 gate[:, m % 2, :], ALU.mult, ALU.mult).then_inc(s_a0, 1)
                        split(a0[:, m, :], a0_h[:, m, :], a0_l[:, m, :], s_a0, s_h0, s_l0, F * c + m + 1)
                if has(c - 1):
                    dve.wait_ge(s_y, c)
                    dve.wait_ge(rl, 16 * c)
                    since(dve, s_ln, 4 * (c - 1))
                    dve.tensor_tensor(z[:, :, :], p_y[:, :].rearrange("p (t d) -> p t d", d=P), xr_t[:, :, :],
                                      ALU.add).then_inc(s_z, 1)
                    dve.wait_ge(s_z, c)
                    for j in range(CT):
                        dve.bn_stats(stats[:, j, :], z[:, j, :]).then_inc(s_bs, 1)
                    since(dve, s_ve, c - 1)
                    for j in range(CT):
                        dve.wait_ge(s_bs, 4 * (c - 1) + j + 1)
                        dve.tensor_copy(mark[:, j:j + 1], stats[:, j, 0:1])
                        dve.bn_aggr(mv[:, j, :], stats[:, j, :]).then_inc(s_mv, 1)
                if has(c):
                    since(dve, s_m2, F * c)
                    for m in range(F):
                        split(a1[:, m, :], a1_h[:, m, :], a1_l[:, m, :], s_a1, s_h1, s_l1, F * c + m + 1)
                if has(c - 1):
                    dve.wait_ge(s_rs, c)
                    since(dve, stored, 16 * (c - 1))
                    for j in range(CT):
                        dve.tensor_scalar(y_t[:, j, :], z[:, j, :], mv[:, j, 0:1], rstd[:, j:j + 1],
                                          ALU.subtract, ALU.mult).then_inc(s_ln, 1)
                if has(c + 1):
                    split_x(c + 1)

            dve.wait_ge(consts, 64)
            high(dve, w1_h[:, :], w1_s[:, :]).then_inc(s_wh, 1)
            high(dve, w2_h[:, :], w2_s[:, :]).then_inc(s_wh, 1)
            split_x(0)
            dve.wait_ge(hidden, 64)
            high(dve, h1_h[:, :, :], h1_s[:, :, :]).then_inc(s_wh, 1)
            high(dve, h2_h[:, :, :], h2_s[:, :, :]).then_inc(s_wh, 1)
            for k in range(F):
                dve.tensor_tensor(w3_o[:, k, :], w3_s[:, k, :], so[:, :], ALU.mult).then_inc(ready, 1)
            run_staggered(dve, slot)


def mixture(nc, name, banks, x_in, x_out, router, w1, w2, ident, before, iota):
    E, TOP_K, F = 8, 2, 4
    CAP = int(1.25 * NB * P * TOP_K / E) + 1
    TE = NB * E
    ph = Phase(nc, name, banks)
    with ph:
        sb, ps, sem = ph.sb, ph.ps, ph.sem
        xh, xl_ = sb("x_high", [P, NB, P]), sb("x_low", [P, NB, P])
        w1_h, w1_l = sb("w1_high", [P, E, F * P]), sb("w1_low", [P, E, F * P])
        w1_s, w2_s = sb("w1", [P, E, F * P]), sb("w2", [P, E, F, P])
        gates = sb("gates", [P, NB, E])
        half, eps = sb("half", [P, CT]), sb("eps", [P, CT])
        p = [ps() for k in range(8)]
        wl, wl2 = sem("w1_loaded"), sem("w2_loaded")
        idn, bef, io, rw = sb("idn", [P, P]), sb("bef", [P, P]), sb("io", [P, E]), sb("rw", [P, E])
        ones = sb("ones", [P, P])
        x_t, xc = sb("x", [P, 2, CT, P]), sb("xc", [P, 2, CT, P])
        lg = sb("lg", [P, NB, E])
        v = {n: sb(n, [P, NB, E]) for n in ("sh", "ex", "pr", "eq", "far", "o1", "p2", "eq2", "far2", "o2",
                                             "both", "wa", "wb", "wsum", "cnt", "keep", "gate0", "tot", "c0", "c1", "tin")}
        r = {n: sb(n, [P, NB]) for n in ("mx", "sm", "rs", "m1", "i1", "m2", "i2", "dn", "rd")}
        consts, xl, s_tr, s_xc = sem("consts"), sem("x_loaded", 2), sem("x_transposed"), sem("x_copied")
        s_xh = sem("x_high_kept")
        s_xa, s_lg, s_lc = sem("x_low_kept"), sem("logits_done"), sem("logits_copied")
        chain = sem("vector_steps"); s_ex = sem("exp_done"); s_cn = sem("counts_done"); blank = sem("blank")
        N_BOTH = 18
        xr_t = sb("xr", [P, CT, P]); gc = sb("gc", [P, CT, E])
        hid = sb("hid", [P, 2, F, CT * P])
        acc = sb("acc", [P, 2, CT, P])
        mark = sb("mark", [P, CT]); stats = sb("stats", [P, CT, 6]); mv = sb("mv", [P, CT, 2])
        vare = sb("vare", [P, CT]); rstd = sb("rstd", [P, CT]); y_t = sb("y", [P, CT, P])
        rl, stored = sem("xr_loaded"), sem("y_stored")
        s_gc, s_x2, s_h, s_si = sem("gates_copied"), sem("sum_started"), sem("hidden_done"), sem("silu_done")
        s_y, s_ac = sem("expert_done"), sem("expert_added")
        s_bs, s_mv, s_ve, s_rs, s_ln = (sem(n) for n in ("stats_ready", "mean_var_ready", "var_eps_ready",
                                                           "rstd_ready", "normed"))
        s_wh, s_wl = sem("expert_high"), sem("expert_low")
        p_h, p_y = p[0:4], p[4:6]
        block = ph.ctx.enter_context(nc.Block())

        @block.sync
        def _(sp):
            for dst, src in ((idn, ident), (bef, before), (io, iota), (rw, router)):
                sp.dma_start(dst[:, :], src).then_inc(consts, 16)

            def routed(c, u, lap):
                if has(c):
                    since(sp, s_tr, c - 1)
                    sp.dma_start(x_t[:, u, :, :], x_in[c].rearrange("t p d -> p t d")).then_inc(xl[u], 16)

            run_paired(sp, routed)
            sp.dma_start(w2_s[:, :, :, :], w2).then_inc(wl2, 16)

            def body(c):
                if later(c):
                    sp.wait_ge(s_x2, c)
                sp.dma_start(xr_t[:, :, :], x_in[c].rearrange("t p d -> p t d")).then_inc(rl, 16)
                sp.wait_ge(s_ln, 4 * c + 4)
                sp.dma_start(x_out[c].rearrange("t p d -> p t d"), y_t[:, :, :]).then_inc(stored, 16)

            run_chunks(sp, body)
            sp.wait_ge(stored, 16 * NC)

        @block.gpsimd
        def _(pool):
            pool.memset(ones[:, :], 1.0).then_inc(blank, 1)
            pool.memset(half[:, :], -0.5).then_inc(blank, 1)
            pool.memset(eps[:, :], EPS_LN).then_inc(blank, 1)
            pool.wait_ge(blank, 3)
            for e in range(E):
                pool.wait_ge(s_wh, e + 1)
                low(pool, w1_l[:, e, :], w1_s[:, e, :], w1_h[:, e, :]).then_inc(s_wl, 1)

            def body(c):
                pool.wait_ge(s_mv, 4 * c + 4)
                pool.tensor_tensor(vare[:, :], mv[:, :, 1], eps[:, :], ALU.add).then_inc(s_ve, 1)
                pool.wait_ge(s_ve, c + 1)
                if later(c):
                    pool.wait_ge(s_ln, 4 * c)
                pool.tensor_tensor(rstd[:, :], vare[:, :], half[:, :], ALU.pow).then_inc(s_rs, 1)

            run_chunks(pool, body)

        @block.tensor
        def _(pe):
            pe.wait_ge(consts, 64)
            pe.wait_ge(blank, 3)

            def routed(c, u, lap):
                if has(c):
                    pe.wait_ge(xl[u], 16 * (lap + 1))
                    since(pe, s_xc, c - 1)
                    for k in range(CT):
                        mm = pe.transpose(p[u][:, k * P:(k + 1) * P], x_t[:, u, k, :], idn[:, :])
                    mm.then_inc(s_tr, 1)
                if has(c - 1):
                    pe.wait_ge(s_xc, c)
                    since(pe, s_lc, c - 1)
                    for k in range(CT):
                        mm = pe.matmul(p[2][:, k * E:(k + 1) * E], xc[:, 1 - u, k, :], rw[:, :], start=True,
                                       stop=True)
                    mm.then_inc(s_lg, 1)

            def counts():
                pe.wait_ge(chain, N_BOTH)
                pe.matmul(p[6][:, 0:TE], bef[:, :], v["both"][:, :, :], start=True, stop=True)
                pe.matmul(p[7][:, 0:TE], ones[:, :], v["both"][:, :, :], start=True, stop=True).then_inc(s_cn, 1)

            run_paired(pe, routed)
            pe.wait_ge(s_lc, NC)
            pe.wait_ge(s_xa, NC)

            def body(c):
                def hidden(e):
                    if not later(c):
                        pe.wait_ge(s_wl, e + 1)
                    for f in range(F):
                        if e > 0:
                            pe.wait_ge(s_si, F * (E * c + e - 1) + f + 1)
                        elif later(c):
                            pe.wait_ge(s_si, F * (E * c - 1) + f + 1)
                        cols, toks = slice(f * P, (f + 1) * P), bass.ds(4 * c, CT)
                        products(pe, p_h[f][:, :], w1_h[:, e, cols], w1_l[:, e, cols], xh[:, toks, :],
                                 xl_[:, toks, :]).then_inc(s_h, 1)

                def output(e):
                    pe.wait_ge(s_si, F * (E * c + e) + F)
                    if e >= 2:
                        pe.wait_ge(s_ac, CT * (E * c + e - 1))
                    elif later(c):
                        pe.wait_ge(s_ac, CT * (E * c + e - 1))
                    for j in range(CT):
                        for f in range(F):
                            toks = slice(j * P, (j + 1) * P)
                            mm = pe.matmul(p_y[e % 2][:, toks], hid[:, e % 2, f, toks], w2_s[:, e, f, :],
                                           start=(f == 0), stop=(f == F - 1))
                    mm.then_inc(s_y, 1)

                for e in range(E + 1):
                    if e < E:
                        hidden(e)
                    if e == 1 and not later(c):
                        pe.wait_ge(wl2, 16)
                    if e > 0:
                        output(e - 1)
                    if e == 1 and not later(c):
                        counts()

            run_chunks(pe, body)

        @block.scalar
        def _(act):
            act.wait_ge(consts, 64)
            act.wait_ge(xl[0], 16)
            act.dma_start(w1_s[:, :, :], w1).then_inc(wl, 16)

            def routed(c, u, lap):
                if has(c):
                    act.wait_ge(s_tr, c + 1)
                    since(act, s_lg, c - 1)
                    since(act, s_xa, c - 1)
                    act.copy(xc[:, u, :, :], p[u][:, :]).then_inc(s_xc, 1)

            run_paired(act, routed)
            act.wait_ge(wl, 16)
            for e in range(E):
                act.copy(w1_h[:, e, :].bitcast(F32R), w1_s[:, e, :]).then_inc(s_wh, 1)
            act.wait_ge(chain, 2)
            act.activation(v["ex"][:, :, :], v["sh"][:, :, :], ACT.Exp).then_inc(s_ex, 1)

            def body(c):
                for e in range(E):
                    if e >= 2 or later(c):
                        act.wait_ge(s_y, E * c + e - 1)
                    for f in range(F):
                        act.wait_ge(s_h, F * (E * c + e) + f + 1)
                        act.activation(hid[:, e % 2, f, :], p_h[f][:, :], ACT.Silu).then_inc(s_si, 1)

            run_chunks(act, body)

        @block.vector
        def _(dve):
            steps = [0]

            def then(ins):
                steps[0] += 1
                ins.then_inc(chain, 1)
                dve.wait_ge(chain, steps[0])

            def wide(a):
                return a[:, :].unsqueeze(2).broadcast_to([P, NB, E])

            def tt(out, a, b, op):
                then(dve.tensor_tensor(out, a, b, op))

            def routed(c, u, lap):
                if has(c):
                    dve.wait_ge(s_xc, c + 1)
                    toks = bass.ds(4 * c, CT)
                    high(dve, xh[:, toks, :], xc[:, u, :, :]).then_inc(s_xh, 1)
                    dve.wait_ge(s_xh, c + 1)
                    low(dve, xl_[:, toks, :], xc[:, u, :, :], xh[:, toks, :]).then_inc(s_xa, 1)
                if has(c - 1):
                    dve.wait_ge(s_lg, c)
                    dve.tensor_copy(lg[:, bass.ds(4 * (c - 1), CT), :], p[2][:, 0:CT * E]).then_inc(s_lc, 1)

            dve.wait_ge(consts, 64)
            run_paired(dve, routed)
            dve.wait_ge(s_lc, NC)
            col = io[:, :].unsqueeze(1).broadcast_to([P, NB, E])
            then(dve.tensor_reduce(r["mx"][:, :], lg[:, :, :], AX_X, ALU.max))
            tt(v["sh"][:, :, :], lg[:, :, :], wide(r["mx"]), ALU.subtract)
            dve.wait_ge(s_ex, 1)
            then(dve.tensor_reduce(r["sm"][:, :], v["ex"][:, :, :], AX_X, ALU.add))
            then(dve.reciprocal(r["rs"][:, :], r["sm"][:, :]))
            tt(v["pr"][:, :, :], v["ex"][:, :, :], wide(r["rs"]), ALU.mult)
            then(dve.tensor_reduce(r["m1"][:, :], v["pr"][:, :, :], AX_X, ALU.max))
            tt(v["eq"][:, :, :], v["pr"][:, :, :], wide(r["m1"]), ALU.is_equal)
            then(dve.scalar_tensor_tensor(v["far"][:, :, :], v["eq"][:, :, :], -float(E), col, ALU.mult, ALU.add))
            then(dve.tensor_reduce(r["i1"][:, :], v["far"][:, :, :], AX_X, ALU.min))
            tt(v["o1"][:, :, :], v["far"][:, :, :], wide(r["i1"]), ALU.is_equal)
            then(dve.scalar_tensor_tensor(v["p2"][:, :, :], v["o1"][:, :, :], -2.0, v["pr"][:, :, :], ALU.mult, ALU.add))
            then(dve.tensor_reduce(r["m2"][:, :], v["p2"][:, :, :], AX_X, ALU.max))
            tt(v["eq2"][:, :, :], v["p2"][:, :, :], wide(r["m2"]), ALU.is_equal)
            then(dve.scalar_tensor_tensor(v["far2"][:, :, :], v["eq2"][:, :, :], -float(E), col, ALU.mult, ALU.add))
            then(dve.tensor_reduce(r["i2"][:, :], v["far2"][:, :, :], AX_X, ALU.min))
            tt(v["o2"][:, :, :], v["far2"][:, :, :], wide(r["i2"]), ALU.is_equal)
            tt(v["wa"][:, :, :], v["o1"][:, :, :], wide(r["m1"]), ALU.mult)
            tt(v["both"][:, :, :], v["o1"][:, :, :], v["o2"][:, :, :], ALU.add)
            assert steps[0] == N_BOTH
            tt(v["wb"][:, :, :], v["o2"][:, :, :], wide(r["m2"]), ALU.mult)
            tt(v["wsum"][:, :, :], v["wa"][:, :, :], v["wb"][:, :, :], ALU.add)
            tt(r["dn"][:, :], r["m1"][:, :], r["m2"][:, :], ALU.add)
            then(dve.reciprocal(r["rd"][:, :], r["dn"][:, :]))
            tt(v["gate0"][:, :, :], v["wsum"][:, :, :], wide(r["rd"]), ALU.mult)
            dve.wait_ge(s_cn, 1)
            then(dve.tensor_copy(v["tot"][:, :, :], p[7][:, 0:TE]))
            then(dve.tensor_copy(v["tin"][:, :, :], p[6][:, 0:TE]))
            src, dst, other, d = v["tot"], v["c0"], v["c1"], 1
            while d < NB:
                then(dve.tensor_copy(dst[:, 0:d, :], src[:, 0:d, :]))
                tt(dst[:, d:NB, :], src[:, d:NB, :], src[:, 0:NB - d, :], ALU.add)
                src, dst, other, d = dst, other, dst, 2 * d
            tt(v["cnt"][:, :, :], src[:, :, :], v["tot"][:, :, :], ALU.subtract)
            tt(v["wa"][:, :, :], v["cnt"][:, :, :], v["tin"][:, :, :], ALU.add)
            then(dve.tensor_scalar(v["keep"][:, :, :], v["wa"][:, :, :], float(CAP), None, ALU.is_lt))
            tt(gates[:, :, :], v["gate0"][:, :, :], v["keep"][:, :, :], ALU.mult)

            def body(c):
                dve.wait_ge(rl, 16 * c + 16)
                if later(c):
                    dve.wait_ge(s_ac, CT * E * c)
                    dve.wait_ge(s_ln, 4 * c)
                dve.tensor_copy(gc[:, :, :], gates[:, bass.ds(4 * c, CT), :]).then_inc(s_gc, 1)
                dve.tensor_scalar(acc[:, 1, :, :], xr_t[:, :, :], 2.0, None, ALU.mult).then_inc(s_x2, 1)
                dve.wait_ge(s_gc, c + 1)
                dve.wait_ge(s_x2, c + 1)

                def add(e):
                    dve.wait_ge(s_y, E * c + e + 1)
                    for j in range(CT):
                        if e > 0:
                            dve.wait_ge(s_ac, CT * (E * c + e - 1) + j + 1)
                        dve.scalar_tensor_tensor(acc[:, e % 2, j, :], p_y[e % 2][:, j * P:(j + 1) * P],
                                                 gc[:, j, e:e + 1], acc[:, 1 - e % 2, j, :], ALU.mult,
                                                 ALU.add).then_inc(s_ac, 1)

                for e in range(E):
                    add(e)
                for j in range(CT):
                    dve.wait_ge(s_ac, CT * (E * c + E - 1) + j + 1)
                    dve.bn_stats(stats[:, j, :], acc[:, 1, j, :]).then_inc(s_bs, 1)
                if later(c):
                    dve.wait_ge(s_ve, c)
                for j in range(CT):
                    dve.wait_ge(s_bs, 4 * c + j + 1)
                    dve.tensor_copy(mark[:, j:j + 1], stats[:, j, 0:1])
                    dve.bn_aggr(mv[:, j, :], stats[:, j, :]).then_inc(s_mv, 1)
                dve.wait_ge(s_rs, c + 1)
                if later(c):
                    dve.wait_ge(stored, 16 * c)
                for j in range(CT):
                    dve.tensor_scalar(y_t[:, j, :], acc[:, 1, j, :], mv[:, j, 0:1], rstd[:, j:j + 1],
                                      ALU.subtract, ALU.mult).then_inc(s_ln, 1)

            run_chunks(dve, body)


def build_decoder(nc, d, out):
    keep = [nc.dram_tensor(f"between{k}", (NB, P, P), F32, kind="Internal").ap() for k in range(5)]

    banks = [nc.alloc_psum_tensor(f"bank{k}", [P, 512], F32) for k in range(8)]

    def chunks(a):
        return a.rearrange("(c t) p d -> c t p d", t=CT)

    linear_attention(nc, "L0a", banks, d["x"], keep[0], d["wq0"], d["wk0"], d["wv0"], d["wo0"], d["bq0"], d["bk0"],
                     d["bv0"], d["bo0"], d["feat"], d["norm"], d["ident"], d["own_head"])
    softmax_attention(nc, "L0x", banks, keep[0], d["ctx"], keep[1], d["wq1"], d["wk1"], d["wv1"], d["wo1"], d["bq1"],
                      d["bk1"], d["bv1"], d["bo1"], d["ident"], d["head8"])
    feed_forward(nc, "L0f", banks, chunks(keep[1]), chunks(keep[2]), d["w1"], d["w2"], d["h1"], d["h2"], d["w3"],
                 d["s_hidden"], d["s_out"], d["ident"])
    trig_attention(nc, "L1a", banks, keep[2], keep[3], d["w_qk"], d["b_qk"], d["quarter"], d["wv2"], d["wo2"],
                   d["ident"], d["head16"], d["causal"])
    softmax_attention(nc, "L1x", banks, keep[3], d["ctx"], keep[4], d["wq3"], d["wk3"], d["wv3"], d["wo3"], None, None,
                      None, d["bo3"], d["ident"], d["head8"])
    mixture(nc, "L1f", banks, chunks(keep[4]), chunks(out), d["router"], d["e1"], d["e2"], d["ident"], d["before"],
            d["experts"])


def lay_out(inp):
    import numpy as np

    a = {k: np.asarray(v) for k, v in inp.items()}
    f32 = np.float32
    M = a["L0_attn_orf"].shape[0]
    E, _, FF = a["L1_ffn_w1"].shape
    F = FF // P
    d = {"x": a["x"], "ctx": a["ctx_1024"]}
    for n, pre in ((0, "L0_attn_"), (1, "L0_xattn_"), (3, "L1_xattn_")):
        for w in "qkvo":
            d[f"w{w}{n}"] = a[f"{pre}W{w}"].T
        if n != 3:
            d[f"bq{n}"], d[f"bk{n}"] = a[f"{pre}bq"][:, None], a[f"{pre}bk"][:, None]
            d[f"bv{n}"] = a[f"{pre}bv"]
        d[f"bo{n}"] = a[f"{pre}bo"]
    feat, norm = np.zeros((H, DK, H, M), f32), np.zeros((H, DK, H, M), f32)
    for h in range(H):
        feat[h, :, h, :] = a["L0_attn_orf"].T
        norm[h, :, h, :] = -0.5
    d["feat"], d["norm"] = feat.reshape(P, H * M), norm.reshape(P, H * M)
    own = np.zeros((4, M, 4, 4, DK + 1), f32)
    for j in range(4):
        own[j, :, :, j, :] = 1.0
    d["own_head"] = own.reshape(P, H, DK + 1)
    d["w1"], d["w2"] = a["L0_ffn_w1_w"].T, a["L0_ffn_w2_w"].T
    for n in ("h1", "h2"):
        d[n] = a[f"L0_ffn_{n}_w"].T.reshape(F, P, FF).transpose(1, 0, 2)
    d["w3"] = a["L0_ffn_w3_w"].T.reshape(F, P, P).transpose(1, 0, 2)
    d["s_hidden"] = np.stack([a[f"L0_ffn_{n}_s"].reshape(F, P).T for n in ("w1", "w2", "h1", "h2")], 1)
    d["s_out"] = a["L0_ffn_w3_s"]

    def rows(w):
        return np.broadcast_to(w.reshape(2, 8, 1, DK), (2, 8, 2, DK)).reshape(2, P).T

    for n in "wb":
        d[f"{n}_qk"] = np.concatenate([rows(a[f"L1_attn_{n}_q"]), rows(a[f"L1_attn_{n}_k"])], 1)
    quarter = np.zeros((8, 2, DK), f32)
    quarter[:, 0] = 512 // 4
    d["quarter"] = quarter.reshape(P, 1)
    d["wv2"], d["wo2"] = a["L1_attn_v_w"].T, a["L1_attn_out_w"].T
    d["router"] = a["L1_ffn_router_w"].T
    d["e1"] = a["L1_ffn_w1"].transpose(1, 0, 2)
    d["e2"] = a["L1_ffn_w2"].reshape(E, F, P, P).transpose(2, 0, 1, 3)
    row, col = np.arange(P)[:, None], np.arange(P)[None, :]
    d["ident"] = (row == col).astype(f32)
    d["causal"] = np.where(row > col, f32(-30000), f32(0))
    d["before"] = (row < col).astype(f32)
    d["head8"] = (row // DK == np.arange(H)[None, :]).astype(f32)
    d["head16"] = (row // (2 * DK) == np.arange(8)[None, :]).astype(f32)
    d["experts"] = np.broadcast_to(np.arange(E, dtype=f32), (P, E))
    return {k: np.ascontiguousarray(v) for k, v in d.items()}


def kernel(**inputs):
    import concourse.bacc as bacc
    from concourse.bass_utils import run_bass_kernel_spmd

    arrays = lay_out(inputs)
    nc = bacc.Bacc("TRN2", target_bir_lowering=False, num_devices=1)
    d = {n: nc.dram_tensor(f"in_{n}", a.shape, mybir.dt.from_np(a.dtype), kind="ExternalInput").ap()
         for n, a in arrays.items()}
    out = nc.dram_tensor("out_0", (NB, P, P), F32, kind="ExternalOutput").ap()
    build_decoder(nc, d, out)
    r = run_bass_kernel_spmd(nc, [{f"in_{n}": a for n, a in arrays.items()}], core_ids=[0])
    return r.results[0]["out_0"]
```

```python
from contextlib import ExitStack

import concourse.bass as bass
from concourse import mybir

ALU = mybir.AluOpType
ACT = mybir.ActivationFunctionType
F32 = mybir.dt.float32
F32R = mybir.dt.float32r
BF16 = mybir.dt.bfloat16
AX_X = mybir.AxisListType.X

P = 128
NB = 32
H = 16
DK = 8
EPS_LN = 1e-5


class Tile:

    def __init__(self, i, off):
        self.i, self.off = i, off
        self.n = 4 * i + off

    def at(self, k):
        return Tile(self.i, self.off + k)

    @property
    def there(self):
        return not isinstance(self.i, int) or 0 <= self.n < NB

    @property
    def opens(self):
        return isinstance(self.i, int) and self.n == 0

    @property
    def early(self):
        return isinstance(self.i, int) and 0 <= self.n < 4

    def buf(self, m):
        return self.off % m

    def lap(self, m):
        return (4 // m) * self.i + self.off // m


def run_slots(eng, slot, first, last, laps=7):
    for t in range(first, 4):
        slot(Tile(0, t))
    with eng.Fori(1, laps) as i:
        for u in range(4):
            slot(Tile(i, u))
    for t in range(4 * laps, last):
        slot(Tile(laps, t - 4 * laps))


def done(eng, sem, tile, per=1, part=None):
    eng.wait_ge(sem, per * tile.n + (per if part is None else part))


def freed(eng, sem, tile, m, per=1):
    before = tile.at(-m)
    if before.there:
        done(eng, sem, before, per)


def loaded(eng, sems, tile):
    m = len(sems)
    eng.wait_ge(sems[tile.buf(m)], 16 * tile.lap(m) + 16)


def high(eng, out, whole):
    return eng.tensor_copy(out.bitcast(F32R), whole)


def low(eng, out, whole, high_part):
    return eng.tensor_tensor(out.bitcast(F32R), whole, high_part, ALU.subtract)


def products(pe, out, w_high, w_low, x_high, x_low, start=True, stop=True):
    passes = ((w_high, x_high), (w_high, x_low), (w_low, x_high))
    for k, (w, x) in enumerate(passes):
        mm = pe.matmul(out, w.bitcast(F32R), x.bitcast(F32R), start=start and k == 0, stop=stop and k == 2)
    return mm


class Phase:

    def __init__(self, nc, name, banks):
        self.nc, self.name, self.ctx, self.banks = nc, name, ExitStack(), list(banks)
        self.sems = []

    def sb(self, name, shape, dt=F32):
        return self.ctx.enter_context(self.nc.sbuf_tensor(f"{self.name}_{name}", shape, dt))

    def ps(self):
        return self.banks.pop(0)

    def sem(self, name, n=None):
        if n is not None:
            return [self.sem(f"{name}{k}") for k in range(n)]
        self.sems.append(self.nc.alloc_semaphore(f"{self.name}_{name}"))
        return self.sems[-1]

    def __enter__(self):
        return self

    def __exit__(self, *failed):
        self.ctx.close()
        self.nc.clear_and_free_semaphores(self.sems)
        self.nc.all_engine_barrier()


def softmax_attention(nc, name, banks, x_in, kv_in, x_out, w_qkvo, b_qk, b_vo, ident, head_of_row):
    ph = Phase(nc, name, banks)
    with ph:
        sb, ps, sem = ph.sb, ph.ps, ph.sem
        idn = sb("idn", [P, P])
        hrows = sb("hrows", [P, 2, H])
        hmask = hrows[:, 0, :]
        w_s = sb("w", [P, 4, P])
        wq_s, wk_s, wv_s, wo_s = (w_s[:, k, :] for k in range(4))
        b_s = sb("b", [P, 2])
        bq_s, bk_s = b_s[:, 0:1], b_s[:, 1:2]
        bvo_s = sb("bvo", [P, 2, P])
        bv_s, bo_s = bvo_s[:, 0, :], bvo_s[:, 1, :]
        warm = sb("warm", [P, 1]); half, eps = sb("half", [P, 1]), sb("eps", [P, 1])
        x_t = sb("x", [P, 4, P]); c_t = sb("c", [P, 4, P])
        xr_t = sb("xr", [P, 2, P]); xb_t = sb("xb", [P, 2, P])
        xT_t = sb("xT", [P, 2, P])
        qa = sb("qa", [P, 4, P]); qb = sb("qb", [P, 4, P]); kT = sb("kT", [P, 2, P])
        kd = sb("kd", [P, 4, H, P])
        va = sb("va", [P, 4, H, 32])
        nmax = sb("nmax", [P, 2, H, 8])
        probs = sb("probs", [P, 2, H, P])
        o1 = sb("o1", [P, 2, 4, P])
        rden = sb("rden", [P, 2, 4, 4])
        o_tok = sb("o_tok", [P, 2, P]); oT = sb("oT", [P, 2, P])
        z = sb("z", [P, 2, P]); mark = sb("mark", [P, 1]); stats = sb("stats", [P, 2, 6]); mv = sb("mv", [P, 2, 2])
        vare = sb("vare", [P, 2, 1]); rstd = sb("rstd", [P, 2, 1]); y_t = sb("y", [P, 4, P])
        p_tr = ps()
        p_pj = ps()
        p_mx = [ps(), ps()]
        p_st = [ps(), ps()]
        p_pv = ps()
        p_on = ps()

        first = sem("ident_loaded"); consts = sem("consts_loaded"); ready = sem("consts_ready"); blank = sem("blanks_ready")
        xl, cl, rl = sem("x_loaded", 4), sem("c_loaded", 4), sem("xr_loaded", 2)
        stored = sem("y_stored", 4)
        s_tr = sem("x_transposed"); s_xc = sem("x_copied")
        s_pj = sem("qkv_projected"); s_q = sem("q_ready"); s_k = sem("k_ready"); s_v = sem("v_ready")
        s_kd = sem("kd_ready"); s_zr = sem("q_zeroed"); s_sq = sem("scores_q"); s_mx = sem("max_ready")
        s_mt = sem("max_transposed"); s_mc = sem("max_copied")
        s_st = sem("scores_k"); s_ex = sem("exp_done"); s_pv = sem("pv_done"); s_o1 = sem("pv_copied")
        s_on = sem("pv_transposed"); s_rd = sem("reciprocals_ready"); s_ot = sem("o_normalised")
        s_oT = sem("o_transposed"); s_oc = sem("o_copied"); s_y = sem("y_projected")
        s_xb = sem("residual_ready"); s_z = sem("z_ready"); s_bs = sem("stats_ready")
        s_mv = sem("mean_var_ready"); s_ve = sem("var_eps_ready"); s_rs = sem("rstd_ready")
        s_ln = sem("normed")

        block = ph.ctx.enter_context(nc.Block())

        @block.sync
        def _(sp):
            sp.dma_start(idn[:, :], ident).then_inc(first, 16)

            def slot(t):
                a = t.at(4)
                if a.there:
                    freed(sp, s_tr, a, 4)
                    sp.dma_start(x_t[:, a.buf(4), :], x_in[a.n]).then_inc(xl[a.buf(4)], 16)
                    freed(sp, s_pj, a, 4)
                    sp.dma_start(c_t[:, a.buf(4), :], kv_in[a.n]).then_inc(cl[a.buf(4)], 16)
                r = t.at(0)
                if r.there:
                    freed(sp, s_xb, r, 2)
                    sp.dma_start(xr_t[:, r.buf(2), :], x_in[r.n]).then_inc(rl[r.buf(2)], 16)
                o = t.at(-3)
                if o.there:
                    done(sp, s_ln, o)
                    sp.dma_start(x_out[o.n], y_t[:, o.buf(4), :]).then_inc(stored[o.buf(4)], 16)

            run_slots(sp, slot, -4, NB + 3)
            for k in range(4):
                sp.wait_ge(stored[k], 16 * NB // 4)

        halves = ((slice(0, 64), slice(0, 8)), (slice(64, P), slice(8, H)))
        n_consts = 16 * (4 if b_qk is not None else 3)

        @block.gpsimd
        def _(pool):
            pool.memset(va[:, :, :, :], 0.0).then_inc(blank, 1)
            pool.wait_ge(blank, 1)
            pool.memset(va[:, :, :, DK:DK + 1], 1.0).then_inc(blank, 1)
            pool.memset(nmax[:, :, :, :], 0.0).then_inc(blank, 1)
            pool.memset(half[:, :], -0.5).then_inc(blank, 1)
            pool.memset(eps[:, :], EPS_LN).then_inc(blank, 1)
            pool.wait_ge(blank, 5)
            pool.wait_ge(consts, n_consts)

            def slot(t):
                n = t.at(-3)
                if n.there:
                    done(pool, s_mv, n)
                    freed(pool, s_rs, n, 2)
                    pool.tensor_tensor(vare[:, n.buf(2), :], mv[:, n.buf(2), 1:2], eps[:, :], ALU.add).then_inc(s_ve, 1)
                    done(pool, s_ve, n)
                    freed(pool, s_ln, n, 2)
                    pool.tensor_tensor(rstd[:, n.buf(2), :], vare[:, n.buf(2), :], half[:, :],
                                       ALU.pow).then_inc(s_rs, 1)
                k = t.at(2)
                if k.there:
                    done(pool, s_k, k)
                    freed(pool, s_st, k, 4, 4)
                    for half_no, (rows, heads) in enumerate(halves):
                        pool.tensor_tensor(kd[rows, k.buf(4), heads, :],
                                           kT[rows, k.buf(2), :].unsqueeze(1).broadcast_to([P // 2, 8, P]),
                                           hmask[rows, heads].unsqueeze(2).broadcast_to([P // 2, 8, P]),
                                           ALU.mult).then_inc(s_kd, 1)
                        done(pool, s_kd, k, 2, half_no + 1)
                r = t.at(-1)
                if r.there:
                    loaded(pool, rl, r)
                    freed(pool, s_z, r, 2)
                    pool.tensor_tensor(xb_t[:, r.buf(2), :], xr_t[:, r.buf(2), :], bo_s,
                                       ALU.add).then_inc(s_xb, 1)

            run_slots(pool, slot, -2, NB + 3)

        @block.tensor
        def _(pe):
            pe.wait_ge(first, 16)

            def slot(t):
                a = t.at(2)
                if a.there:
                    loaded(pe, xl, a)
                    if t.there:
                        done(pe, s_mc, t, 2)
                    elif a.at(-1).there:
                        done(pe, s_xc, a.at(-1))
                    pe.transpose(p_tr[:, 0:P], x_t[:, a.buf(4), :], idn[:, :]).then_inc(s_tr, 1)
                v = t.at(-1)
                if v.there:
                    done(pe, s_ex, v, 4)
                    freed(pe, s_o1, v, 1)
                    for k in range(4):
                        for c in range(4):
                            h = 4 * c + k
                            mm = pe.matmul(p_pv[32 * c:32 * c + 32, k * P:(k + 1) * P], va[:, v.buf(4), h, :],
                                           probs[:, v.buf(2), h, :], start=True, stop=True)
                    mm.then_inc(s_pv, 1)
                if a.there:
                    if a.opens:
                        pe.wait_ge(consts, n_consts)
                        pe.wait_ge(blank, 5)
                    done(pe, s_xc, a)
                    if t.at(-3).there:
                        done(pe, s_z, t.at(-3))
                    elif a.at(-1).there:
                        done(pe, s_v, a.at(-1))
                        done(pe, s_k, a.at(-1))
                    loaded(pe, cl, a)
                    xT, cT = xT_t[:, a.buf(2), :], c_t[:, a.buf(4), :]
                    pe.matmul(p_pj[:, 0:P], wq_s, xT, start=True, stop=True)
                    pe.matmul(p_pj[:, P:2 * P], wk_s, cT, start=True, stop=True)
                    pe.matmul(p_pj[:, 2 * P:3 * P], cT, wv_s, start=True, stop=True).then_inc(s_pj, 1)
                m = t.at(1)
                if m.there:
                    done(pe, s_kd, m, 2)
                    done(pe, s_q, m, 2)
                    done(pe, s_zr, m, 2)
                    if m.early:
                        pe.wait_ge(ready, 2 * m.n + 2)

                def rows_scores(g):
                    if g >= 2:
                        done(pe, s_mx, m, 4, g - 1)
                    elif m.at(-1).there:
                        done(pe, s_mx, m.at(-1), 4, g + 3)
                    q_hi = (qa if g < 2 else qb)[:, m.buf(4), :].bitcast(BF16)[:, 1:2 * P:2]
                    k_hi = kd[:, m.buf(4), 4 * g:4 * g + 4, :].bitcast(BF16)[:, :, 1:2 * P:2]
                    pe.matmul(p_mx[g % 2][:, :], q_hi, k_hi, start=True, stop=True).then_inc(s_sq, 1)

                if m.there:
                    rows_scores(0)
                    rows_scores(1)
                o = t.at(-2)
                if o.there:
                    done(pe, s_ot, o)
                    if a.there:
                        done(pe, s_xc, a)
                    elif t.there:
                        done(pe, s_mc, t, 2)
                    else:
                        done(pe, s_oc, o.at(-1))
                    pe.transpose(p_tr[:, 0:P], o_tok[:, o.buf(2), :], idn[:, :]).then_inc(s_oT, 1)
                if t.there:
                    done(pe, s_mc, t, 2)
                for g in range(4):
                    if t.there:
                        if g >= 2:
                            done(pe, s_ex, t, 4, g - 1)
                        elif t.at(-1).there:
                            done(pe, s_ex, t.at(-1), 4, g + 3)
                        for j in range(4):
                            out = p_st[g % 2][:, j * P:(j + 1) * P]
                            mm = pe.matmul(out, kd[:, t.buf(4), 4 * g + j, :],
                                           (qa if g < 2 else qb)[:, t.buf(4), :], start=True, stop=True)
                        mm.then_inc(s_st, 1)
                    if m.there and g in (1, 2):
                        rows_scores(g + 1)
                if m.there:
                    done(pe, s_mx, m, 4)
                    if o.there:
                        done(pe, s_oc, o)
                    elif a.there:
                        done(pe, s_xc, a)
                    pe.transpose(p_tr[:, 0:P], nmax[:, m.buf(2), :, :].rearrange("p s e -> p (s e)"), idn[:, :]).then_inc(s_mt, 1)
                if o.there:
                    done(pe, s_oc, o)
                    if a.there:
                        done(pe, s_v, a)
                        done(pe, s_k, a)
                    else:
                        done(pe, s_z, o.at(-1))
                    pe.matmul(p_pj[:, 0:P], oT[:, o.buf(2), :], wo_s, start=True, stop=True).then_inc(s_y, 1)
                if v.there:
                    done(pe, s_o1, v)
                    freed(pe, s_ot, v, 1)
                    for k in range(4):
                        mm = pe.transpose(p_on[:, k * P:(k + 1) * P], o1[:, v.buf(2), k, :], idn[:, :])
                    mm.then_inc(s_on, 1)

            run_slots(pe, slot, -2, NB + 2)

        @block.scalar
        def _(act):
            act.dma_start(w_s[:, :, :], w_qkvo).then_inc(consts, 16)
            if b_qk is not None:
                act.dma_start(b_s[:, :], b_qk).then_inc(consts, 16)
                act.dma_start(bvo_s[:, :, :], b_vo.partition_broadcast(P)).then_inc(consts, 16)
            else:
                act.dma_start(bo_s, b_vo.partition_broadcast(P)).then_inc(consts, 16)
            act.dma_start(hrows[:, :, :], head_of_row).then_inc(consts, 16)
            act.wait_ge(blank, 5)
            act.activation(warm[:, :], half[:, :], ACT.Exp)

            def slot(t):
                a = t.at(2)
                if a.there:
                    done(act, s_tr, a)
                    freed(act, s_pj, a, 2)
                    act.copy(xT_t[:, a.buf(2), :], p_tr[:, 0:P]).then_inc(s_xc, 1)
                    if a.opens:
                        act.wait_ge(consts, n_consts)
                    done(act, s_pj, a)
                    if a.at(-4).there:
                        done(act, s_st, a.at(-4), 4)
                    for q, (rows, heads) in zip((qa, qb), halves):
                        if b_qk is not None:
                            act.activation(q[rows, a.buf(4), :], p_pj[rows, 0:P], ACT.Identity,
                                           bias=bq_s[rows, :]).then_inc(s_q, 1)
                        else:
                            act.copy(q[rows, a.buf(4), :], p_pj[rows, 0:P]).then_inc(s_q, 1)
                    freed(act, s_kd, a, 2, 2)
                    if b_qk is not None:
                        act.activation(kT[:, a.buf(2), :], p_pj[:, P:2 * P], ACT.Identity, bias=bk_s).then_inc(s_k, 1)
                    else:
                        act.copy(kT[:, a.buf(2), :], p_pj[:, P:2 * P]).then_inc(s_k, 1)
                if t.there:
                    freed(act, s_pv, t, 2)
                    for g in range(4):
                        done(act, s_st, t, 4, g + 1)
                        act.activation(probs[:, t.buf(2), 4 * g:4 * g + 4, :], p_st[g % 2][:, :], ACT.Exp,
                                       scale=float(DK) ** -0.5).then_inc(s_ex, 1)

            run_slots(act, slot, -2, NB)

        @block.vector
        def _(dve):
            dve.wait_ge(blank, 5)
            dve.wait_ge(consts, n_consts)
            def slot(t):
                v = t.at(-1)
                if v.there:
                    done(dve, s_pv, v)
                    freed(dve, s_on, v, 2)
                    dve.tensor_copy(o1[:, v.buf(2), :, :], p_pv[:, :]).then_inc(s_o1, 1)
                m = t.at(1)

                def maxima(g):
                    done(dve, s_sq, m, 4, g + 1)
                    dve.tensor_reduce(nmax[:, m.buf(2), (8 + 4 * g) % H:(8 + 4 * g) % H + 4, 0],
                                      p_mx[g % 2][:, :].rearrange("p (h k) -> p h k", k=P), AX_X, ALU.max,
                                      negate=True).then_inc(s_mx, 1)

                if m.there:
                    freed(dve, s_mt, m, 2)
                    maxima(0)
                    maxima(1)
                a = t.at(2)
                if a.there:
                    done(dve, s_pj, a)
                    done(dve, s_k, a)
                    if a.early:
                        for rows, heads in ((halves[1][0], halves[0][1]), (halves[0][0], halves[1][1])):
                            dve.tensor_copy(kd[rows, a.n, heads, :], hrows[rows, 1, heads].unsqueeze(2)
                                            .broadcast_to([P // 2, 8, P])).then_inc(ready, 1)
                    freed(dve, s_st, a, 4, 4)
                    dve.memset(qa[64:P, a.buf(4), :], 0.0).then_inc(s_zr, 1)
                    dve.memset(qb[0:64, a.buf(4), :], 0.0).then_inc(s_zr, 1)
                    freed(dve, s_pv, a, 4)
                    vin = p_pj[:, 2 * P:3 * P].rearrange("p (h d) -> p h d", d=DK)
                    if b_qk is not None:
                        dve.tensor_tensor(va[:, a.buf(4), :, 0:DK], vin,
                                          bv_s.rearrange("p (h d) -> p h d", d=DK), ALU.add).then_inc(s_v, 1)
                    else:
                        dve.tensor_copy(va[:, a.buf(4), :, 0:DK], vin).then_inc(s_v, 1)
                n = t.at(-3)
                if n.there:
                    done(dve, s_rs, n)
                    if n.at(-4).there:
                        loaded(dve, stored, n.at(-4))
                    dve.tensor_scalar(y_t[:, n.buf(4), :], z[:, n.buf(2), :], mv[:, n.buf(2), 0:1],
                                      rstd[:, n.buf(2), :], ALU.subtract, ALU.mult).then_inc(s_ln, 1)
                o = t.at(-2)
                if o.there:
                    done(dve, s_oT, o)
                    freed(dve, s_y, o, 2)
                    dve.tensor_copy(oT[:, o.buf(2), :], p_tr[:, 0:P]).then_inc(s_oc, 1)
                if m.there:
                    maxima(2)
                    maxima(3)
                if m.there:
                    done(dve, s_mt, m)
                    dve.tensor_copy(qa[64:P, m.buf(4), :], p_tr[64:P, 0:P]).then_inc(s_mc, 1)
                    dve.tensor_copy(qb[0:64, m.buf(4), :], p_tr[0:64, 0:P]).then_inc(s_mc, 1)
                if o.there:
                    done(dve, s_y, o)
                    done(dve, s_xb, o)
                    freed(dve, s_ln, o, 2)
                    dve.tensor_tensor(z[:, o.buf(2), :], p_pj[:, 0:P], xb_t[:, o.buf(2), :], ALU.add).then_inc(s_z, 1)
                    done(dve, s_z, o)
                    dve.bn_stats(stats[:, o.buf(2), :], z[:, o.buf(2), :]).then_inc(s_bs, 1)
                    done(dve, s_bs, o)
                    freed(dve, s_ve, o, 2)
                    dve.tensor_copy(mark[:, :], stats[:, o.buf(2), 0:1])
                    dve.bn_aggr(mv[:, o.buf(2), :], stats[:, o.buf(2), :]).then_inc(s_mv, 1)
                if v.there:
                    done(dve, s_on, v)
                    on = p_on[:, :].rearrange("p (k c e) -> p k c e", k=4, c=4)
                    freed(dve, s_ot, v, 2)
                    dve.reciprocal(rden[:, v.buf(2), :, :], on[:, :, :, DK]).then_inc(s_rd, 1)
                    done(dve, s_rd, v)
                    freed(dve, s_oT, v, 2)
                    dve.tensor_tensor(o_tok[:, v.buf(2), :].rearrange("p (c k d) -> p k c d", c=4, k=4),
                                      on[:, :, :, 0:DK],
                                      rden[:, v.buf(2), :, :].unsqueeze(3).broadcast_to([P, 4, 4, DK]),
                                      ALU.mult).then_inc(s_ot, 1)

            run_slots(dve, slot, -2, NB + 3)


def trig_attention(nc, name, banks, x_in, x_out, w_qk, b_qk, quarter, wv, wo, ident, head_of_row16, causal):
    LUT = 512
    STEP = 2.0 * 3.141592653589793 / LUT
    SCALE = 0.012271845
    ROUND = 1.5 * 2.0 ** 23
    ph = Phase(nc, name, banks)
    with ph:
        sb, ps, sem = ph.sb, ph.ps, ph.sem
        idn = sb("idn", [P, P])
        hmask = sb("hmask", [P, 8])
        tri = sb("tri", [P, P])
        keep = sb("keep", [P, P])
        tri4, idn_b = sb("tri4", [P, 4, P], BF16), sb("idn_b", [P, P], BF16)
        wv_s, wo_s = sb("wv", [P, P]), sb("wo", [P, P])
        w_s, b_s, quar = sb("w", [P, 4]), sb("b", [P, 4]), sb("quar", [P, 1])
        wa, wr = sb("wa", [P, 4]), sb("wr", [P, 4])
        sc, bi = sb("sc", [P, 4]), sb("bi", [P, 4])
        half, eps = sb("half", [P, 1]), sb("eps", [P, 1])
        x_t = sb("x", [P, 4, P]); one = sb("one", [P, 8]); x2 = sb("x2", [P, 2, 2, 8, 2, DK]); xr_t = sb("xr", [P, 2, P]); xT = sb("xT", [P, 2, P])
        u = sb("u", [P, 2, 4, P]); nr = sb("nr", [P, 2, 4, P]); lap = sb("lap", [P, 2, 4, P])
        off = sb("off", [P, 2, 4, P]); an = sb("an", [P, 4, 4, P])
        sn = sb("sn", [P, 4, 4, P])
        kd = sb("kd", [P, 2, H, P])
        va = sb("va", [P, 4, H, 32])
        probs = sb("probs", [P, 2, H, P])
        o1 = sb("o1", [P, 2, 4, P]); rden = sb("rden", [P, 2, 4, 4])
        o_tok = sb("o_tok", [P, 2, P]); oT = sb("oT", [P, 2, P])
        z = sb("z", [P, 2, P]); mark = sb("mark", [P, 1]); stats = sb("stats", [P, 2, 6]); mv = sb("mv", [P, 2, 2])
        vare = sb("vare", [P, 2, 1]); rstd = sb("rstd", [P, 2, 1]); y_t = sb("y", [P, 4, P])
        p_tr, p_oT, p_pj = ps(), ps(), ps()
        p_st = [ps(), ps(), ps()]
        p_pv, p_on = ps(), ps()

        first = sem("ident_loaded"); consts = sem("consts_loaded"); ready = sem("consts_ready"); blank = sem("blanks_ready")
        xl, rl, stored = sem("x_loaded", 4), sem("xr_loaded", 2), sem("y_stored", 4)
        s_x2 = sem("x_doubled"); s_tr = sem("x_transposed"); s_xc = sem("x_copied"); s_u = sem("angles_ready")
        s_nr = sem("angles_rounded"); s_lp = sem("laps_counted"); s_of = sem("laps_scaled"); s_an = sem("angles_reduced")
        s_sn = sem("sines_ready"); s_kd = sem("kd_ready")
        s_pj = sem("v_projected"); s_v = sem("v_ready")
        s_st = sem("scores"); s_mk = sem("probs_masked"); s_ex = sem("exp_done"); s_pv = sem("pv_done")
        s_o1 = sem("pv_copied"); s_on = sem("pv_transposed"); s_rd = sem("reciprocals_ready")
        s_ot = sem("o_normalised"); s_oT = sem("o_transposed"); s_oc = sem("o_copied"); s_y = sem("y_projected")
        s_z = sem("z_ready"); s_bs = sem("stats_ready"); s_mv = sem("mean_var_ready")
        s_ve = sem("var_eps_ready"); s_rs = sem("rstd_ready"); s_ln = sem("normed")

        block = ph.ctx.enter_context(nc.Block())
        n_consts = 16 * 7

        @block.sync
        def _(sp):
            sp.dma_start(idn[:, :], ident).then_inc(first, 16)

            def slot(t):
                a = t.at(6)
                if a.there:
                    freed(sp, s_tr, a, 4)
                    sp.dma_start(x_t[:, a.buf(4), :], x_in[a.n]).then_inc(xl[a.buf(4)], 16)
                if t.there:
                    freed(sp, s_z, t, 2)
                    sp.dma_start(xr_t[:, t.buf(2), :], x_in[t.n]).then_inc(rl[t.buf(2)], 16)
                o = t.at(-3)
                if o.there:
                    done(sp, s_ln, o)
                    sp.dma_start(x_out[o.n], y_t[:, o.buf(4), :]).then_inc(stored[o.buf(4)], 16)

            run_slots(sp, slot, -6, NB + 3, 6)
            for k in range(4):
                sp.wait_ge(stored[k], 16 * NB // 4)

        @block.gpsimd
        def _(pool):
            pool.memset(va[:, :, :, :], 0.0).then_inc(blank, 1)
            pool.wait_ge(blank, 1)
            pool.memset(va[:, :, :, DK:DK + 1], 1.0).then_inc(blank, 1)
            pool.memset(half[:, :], -0.5).then_inc(blank, 1)
            pool.memset(eps[:, :], EPS_LN).then_inc(blank, 1)
            pool.memset(one[:, :], 1.0).then_inc(blank, 1)
            pool.wait_ge(blank, 5)

            def slot(t):
                n = t.at(-3)
                if n.there:
                    done(pool, s_mv, n)
                    freed(pool, s_rs, n, 2)
                    pool.tensor_tensor(vare[:, n.buf(2), :], mv[:, n.buf(2), 1:2], eps[:, :], ALU.add).then_inc(s_ve, 1)
                    done(pool, s_ve, n)
                    freed(pool, s_ln, n, 2)
                    pool.tensor_tensor(rstd[:, n.buf(2), :], vare[:, n.buf(2), :], half[:, :],
                                       ALU.pow).then_inc(s_rs, 1)
                a = t.at(5)
                if a.there:
                    loaded(pool, xl, a)
                    freed(pool, s_tr, a, 2)
                    for f in range(2):
                        pool.tensor_tensor(x2[:, a.buf(2), f],
                                           x_t[:, a.buf(4), 64 * f:64 * f + 64].rearrange("p (h d) -> p h d", d=DK)
                                           .unsqueeze(2).broadcast_to([P, 8, 2, DK]),
                                           one[:, :].unsqueeze(2).unsqueeze(3).broadcast_to([P, 8, 2, DK]),
                                           ALU.mult).then_inc(s_x2, 1)
                k = t.at(1)
                if k.there:
                    if k.opens:
                        pool.wait_ge(consts, n_consts)
                    done(pool, s_sn, k)
                    freed(pool, s_st, k, 2, 4)
                    for f in range(2):
                        pool.tensor_tensor(kd[:, k.buf(2), 8 * f:8 * f + 8, :],
                                           sn[:, k.buf(4), 2 + f, :].unsqueeze(1).broadcast_to([P, 8, P]),
                                           hmask[:, :].unsqueeze(2).broadcast_to([P, 8, P]),
                                           ALU.mult).then_inc(s_kd, 1)

            run_slots(pool, slot, -5, NB + 3, 6)

        @block.tensor
        def _(pe):
            pe.wait_ge(first, 16)

            def slot(t):
                a = t.at(4)
                if a.there:
                    loaded(pe, xl, a)
                    freed(pe, s_u, a, 1, 4)
                    freed(pe, s_xc, a, 1)
                    done(pe, s_x2, a, 2)
                    for f in range(2):
                        pe.transpose(p_tr[:, f * P:(f + 1) * P],
                                     x2[:, a.buf(2), f].rearrange("p h c d -> p (h c d)"), idn[:, :])
                    pe.transpose(p_tr[:, 2 * P:3 * P], x_t[:, a.buf(4), :], idn[:, :]).then_inc(s_tr, 1)
                def scores(g):
                    if g == 3:
                        done(pe, s_ex, t, 4, 1)
                    elif t.at(-1).there:
                        done(pe, s_ex, t.at(-1), 4, 4 if g == 0 else g + 1)
                    if g >= 2:
                        pe.matmul(p_st[g % 3][:, :], idn_b[:, :], tri4[:, :, :], start=True, stop=False,
                                  skip_group_check=True)
                    for j in range(4):
                        h = 4 * g + j
                        mm = pe.matmul(p_st[g % 3][:, j * P:(j + 1) * P], kd[:, t.buf(2), h, :],
                                       sn[:, t.buf(4), h // 8, :], start=(g < 2), stop=True, skip_group_check=True)
                    mm.then_inc(s_st, 1)

                if t.there:
                    if t.opens:
                        pe.wait_ge(ready, 8)
                    done(pe, s_kd, t, 2)
                    scores(0)
                    scores(1)
                o = t.at(-2)
                if o.there:
                    done(pe, s_ot, o)
                    freed(pe, s_oc, o, 1)
                    pe.transpose(p_oT[:, 0:P], o_tok[:, o.buf(2), :], idn[:, :]).then_inc(s_oT, 1)
                w = t.at(3)
                if w.there:
                    if w.opens:
                        pe.wait_ge(consts, n_consts)
                        pe.wait_ge(blank, 5)
                    done(pe, s_xc, w)
                    if t.at(-3).there:
                        done(pe, s_z, t.at(-3))
                    elif w.at(-1).there:
                        done(pe, s_v, w.at(-1))
                    pe.matmul(p_pj[:, 0:P], xT[:, w.buf(2), :], wv_s[:, :], start=True, stop=True).then_inc(s_pj, 1)
                v = t.at(-1)
                if v.there:
                    done(pe, s_ex, v, 4)
                    done(pe, s_mk, v, 2)
                    freed(pe, s_o1, v, 1)
                    for k in range(4):
                        for c in range(4):
                            h = 4 * c + k
                            mm = pe.matmul(p_pv[32 * c:32 * c + 32, k * P:(k + 1) * P], va[:, v.buf(4), h, :],
                                           probs[:, v.buf(2), h, :], start=True, stop=True)
                    mm.then_inc(s_pv, 1)
                if t.there:
                    scores(2)
                    scores(3)
                if o.there:
                    done(pe, s_oc, o)
                    if w.there:
                        done(pe, s_v, w)
                    else:
                        done(pe, s_z, o.at(-1))
                    pe.matmul(p_pj[:, 0:P], oT[:, o.buf(2), :], wo_s[:, :], start=True, stop=True).then_inc(s_y, 1)
                if v.there:
                    done(pe, s_o1, v)
                    freed(pe, s_ot, v, 1)
                    for k in range(4):
                        mm = pe.transpose(p_on[:, k * P:(k + 1) * P], o1[:, v.buf(2), k, :], idn[:, :])
                    mm.then_inc(s_on, 1)

            run_slots(pe, slot, -4, NB + 2, 6)

        @block.scalar
        def _(act):
            for dst, src in ((w_s, w_qk), (b_s, b_qk), (quar, quarter), (tri, causal), (hmask, head_of_row16),
                             (wv_s, wv), (wo_s, wo)):
                act.dma_start(dst[:, :], src).then_inc(consts, 16)

            def slot(t):
                a = t.at(4)
                if a.there:
                    done(act, s_tr, a)
                    freed(act, s_pj, a, 2)
                    act.copy(xT[:, a.buf(2), :], p_tr[:, 2 * P:3 * P]).then_inc(s_xc, 1)
                def exps(g):
                    done(act, s_st, t, 4, g + 1)
                    act.activation(probs[:, t.buf(2), 4 * g:4 * g + 4, :], p_st[g % 3][:, :], ACT.Exp,
                                   scale=float(2 * DK) ** -0.5).then_inc(s_ex, 1)

                if t.there:
                    freed(act, s_pv, t, 2)
                    exps(0)
                    exps(1)
                v = t.at(-1)
                if v.there:
                    done(act, s_pv, v)
                    freed(act, s_on, v, 2)
                    act.copy(o1[:, v.buf(2), :, :], p_pv[:, :]).then_inc(s_o1, 1)
                if t.there:
                    exps(2)
                    exps(3)
                b = t.at(3)
                if t.off % 2 == 0 and b.there:
                    done(act, s_an, b)
                    if b.at(-4).there:
                        done(act, s_st, b.at(-4), 4)
                        done(act, s_kd, b.at(-4), 2)
                    first = b.at(-1).buf(4)
                    act.activation(sn[:, first:first + 2, :, :], an[:, first:first + 2, :, :], ACT.Sin,
                                   scale=SCALE).then_inc(s_sn, 2)

            run_slots(act, slot, -4, NB + 1, 6)

        @block.vector
        def _(dve):
            dve.wait_ge(consts, n_consts)
            dve.wait_ge(first, 16)
            dve.wait_ge(blank, 5)
            dve.scalar_tensor_tensor(wa[:, :], w_s[:, :], -1.0, w_s[:, :], ALU.mult, ALU.max).then_inc(ready, 1)
            dve.wait_ge(ready, 1)
            dve.tensor_scalar(wa[:, :], wa[:, :], 1.0, None, ALU.add).then_inc(ready, 1)
            dve.wait_ge(ready, 2)
            dve.reciprocal(wr[:, :], wa[:, :]).then_inc(ready, 1)
            dve.wait_ge(ready, 3)
            dve.tensor_scalar(sc[:, :], wr[:, :], 1.0 / STEP, None, ALU.mult).then_inc(ready, 1)
            dve.tensor_scalar(keep[:, :], tri[:, :], 0.0, None, ALU.is_equal).then_inc(ready, 1)
            dve.tensor_copy(idn_b[:, :], idn[:, :]).then_inc(ready, 1)
            dve.tensor_copy(tri4[:, :, :], tri[:, :].unsqueeze(1).broadcast_to([P, 4, P])).then_inc(ready, 1)
            dve.tensor_scalar(bi[:, :], b_s[:, :], 1.0 / STEP, quar[:, :], ALU.mult, ALU.add).then_inc(ready, 1)

            dve.wait_ge(ready, 8)

            def slot(t):
                a = t.at(4)
                if a.there:
                    done(dve, s_tr, a)
                    freed(dve, s_nr, a, 2)
                    done(dve, s_xc, a)
                    for f in range(4):
                        dve.tensor_scalar(u[:, a.buf(2), f, :], p_tr[:, (f % 2) * P:(f % 2 + 1) * P], sc[:, f:f + 1],
                                          bi[:, f:f + 1], ALU.mult, ALU.add).then_inc(s_u, 1)
                o = t.at(-2)
                if o.there:
                    done(dve, s_oT, o)
                    freed(dve, s_y, o, 2)
                    dve.tensor_copy(oT[:, o.buf(2), :], p_oT[:, 0:P]).then_inc(s_oc, 1)
                w = t.at(3)
                if w.there:
                    done(dve, s_pj, w)
                    freed(dve, s_pv, w, 4)
                    dve.tensor_copy(va[:, w.buf(4), :, 0:DK],
                                    p_pj[:, 0:P].rearrange("p (h d) -> p h d", d=DK)).then_inc(s_v, 1)
                if t.there:
                    for g in range(2):
                        done(dve, s_ex, t, 4, g + 1)
                        pr = probs[:, t.buf(2), 4 * g:4 * g + 4, :]
                        dve.tensor_tensor(pr, pr, keep[:, :].unsqueeze(1).broadcast_to([P, 4, P]),
                                          ALU.mult).then_inc(s_mk, 1)
                n = t.at(-3)
                if n.there:
                    done(dve, s_rs, n)
                    if n.at(-4).there:
                        loaded(dve, stored, n.at(-4))
                    dve.tensor_scalar(y_t[:, n.buf(4), :], z[:, n.buf(2), :], mv[:, n.buf(2), 0:1],
                                      rstd[:, n.buf(2), :], ALU.subtract, ALU.mult).then_inc(s_ln, 1)
                if o.there:
                    done(dve, s_y, o)
                    loaded(dve, rl, o)
                    freed(dve, s_ln, o, 2)
                    dve.tensor_tensor(z[:, o.buf(2), :], p_pj[:, 0:P], xr_t[:, o.buf(2), :], ALU.add).then_inc(s_z, 1)
                    done(dve, s_z, o)
                    dve.bn_stats(stats[:, o.buf(2), :], z[:, o.buf(2), :]).then_inc(s_bs, 1)
                    done(dve, s_bs, o)
                    freed(dve, s_ve, o, 2)
                    dve.tensor_copy(mark[:, :], stats[:, o.buf(2), 0:1])
                    dve.bn_aggr(mv[:, o.buf(2), :], stats[:, o.buf(2), :]).then_inc(s_mv, 1)
                v = t.at(-1)
                if v.there:
                    done(dve, s_on, v)
                    on = p_on[:, :].rearrange("p (k c e) -> p k c e", k=4, c=4)
                    freed(dve, s_ot, v, 2)
                    dve.reciprocal(rden[:, v.buf(2), :, :], on[:, :, :, DK]).then_inc(s_rd, 1)
                    done(dve, s_rd, v)
                    freed(dve, s_oT, v, 2)
                    dve.tensor_tensor(o_tok[:, v.buf(2), :].rearrange("p (c k d) -> p k c d", c=4, k=4),
                                      on[:, :, :, 0:DK],
                                      rden[:, v.buf(2), :, :].unsqueeze(3).broadcast_to([P, 4, 4, DK]),
                                      ALU.mult).then_inc(s_ot, 1)
                if a.there:
                    done(dve, s_u, a, 4)
                    freed(dve, s_an, a, 2)
                    b = a.buf(2)
                    dve.tensor_scalar(nr[:, b], u[:, b], ROUND, ROUND, ALU.add, ALU.subtract).then_inc(s_nr, 1)
                    done(dve, s_nr, a)
                    dve.tensor_scalar(lap[:, b], nr[:, b], 1.0 / LUT, ROUND, ALU.mult, ALU.add).then_inc(s_lp, 1)
                    done(dve, s_lp, a)
                    dve.tensor_scalar(off[:, b], lap[:, b], ROUND, -float(LUT), ALU.subtract, ALU.mult).then_inc(s_of, 1)
                    done(dve, s_of, a)
                    freed(dve, s_sn, a, 4)
                    dve.tensor_tensor(an[:, a.buf(4)], nr[:, b], off[:, b], ALU.add).then_inc(s_an, 1)

            run_slots(dve, slot, -4, NB + 3, 6)


def linear_attention(nc, name, banks, x_in, x_out, w_qkvo, b_qk, b_vo, feat_norm, ident, own_head):
    M = 32
    G = 4
    VW = DK + 1
    root = float(DK) ** -0.25
    ph = Phase(nc, name, banks)
    with ph:
        sb, ps, sem = ph.sb, ph.ps, ph.sem
        idn = sb("idn", [P, P]); own = sb("own", [P, H, VW])
        w_s = sb("w", [P, 4, P])
        wq_s, wk_s, wv_s, wo_s = (w_s[:, k, :] for k in range(4))
        b_s = sb("b", [P, 2])
        bq_s, bk_s = b_s[:, 0:1], b_s[:, 1:2]
        bvo_s = sb("bvo", [P, 2, P])
        bv_s, bo_s = bvo_s[:, 0, :], bvo_s[:, 1, :]
        fn_s, ft = sb("feat_norm", [P, 2, H * M]), sb("ft", [P, H * M])
        ft_raw, nm = fn_s[:, 0, :], fn_s[:, 1, :]
        half, eps = sb("half", [P, 1]), sb("eps", [P, 1]); lnm = sb("lnm", [P, 1]); warm = sb("warm", [P, 1])
        bqs, bks = sb("bqs", [P, 1]), sb("bks", [P, 1])
        ft_h, ft_l, nm_h = sb("ft_high", [P, H * M]), sb("ft_low", [P, H * M]), sb("nm_high", [P, H * M])
        k_h, k_l = sb("k_high", [P, 2, P]), sb("k_low", [P, 2, P])
        ks_h, ks_l = sb("ks_high", [P, 2, P]), sb("ks_low", [P, 2, P])
        x_t = sb("x", [P, 4, P]); xr_t = sb("xr", [P, 2, P]); xb_t = sb("xb", [P, 2, P])
        xT = sb("xT", [P, 2, P])
        qT = sb("qT", [P, 2, P]); qs = sb("qs", [P, 2, P]); kT = sb("kT", [P, 2, P]); ks = sb("ks", [P, 2, P])
        va = sb("va", [P, 4, H, VW])
        ek = sb("ek", [P, 2, H * M]); eq = sb("eq", [P, 2, G, P])
        kvm = sb("kvm", [P, 2, H, VW]); rden = sb("rden", [P, 2, H])
        o_tok = sb("o_tok", [P, 2, P]); oT = sb("oT", [P, 2, P])
        z = sb("z", [P, 2, P]); mark = sb("mark", [P, 1]); stats = sb("stats", [P, 2, 6]); mv = sb("mv", [P, 2, 2])
        vare = sb("vare", [P, 2, 1]); rstd = sb("rstd", [P, 2, 1]); y_t = sb("y", [P, 4, P])
        p_tr, p_oT, p_pj, p_y = ps(), ps(), ps(), ps()
        p_zq, p_zk, p_kv, p_on = ps(), ps(), ps(), ps()

        first = sem("ident_loaded"); consts = sem("consts_loaded"); ready = sem("feat_ready"); blank = sem("blanks_ready")
        xl, rl, stored = sem("x_loaded", 4), sem("xr_loaded", 2), sem("y_stored", 4)
        s_tr = sem("x_transposed"); s_xc = sem("x_copied"); s_pj = sem("qkv_projected")
        s_q = sem("q_and_k_ready"); s_v = sem("v_ready"); s_zq = sem("zq_done"); s_zk = sem("zk_done")
        s_eq = sem("q_features"); s_ek = sem("k_features"); s_kv = sem("kv_done"); s_kc = sem("kv_copied")
        s_on = sem("outputs_done"); s_rd = sem("reciprocals_ready")
        s_ot = sem("o_normalised"); s_oT = sem("o_transposed"); s_oc = sem("o_copied"); s_y = sem("y_projected")
        s_kh = sem("k_high_parts"); s_kl = sem("k_low_parts"); s_ee = sem("k_features_raised")
        s_qe = sem("q_features_raised")
        s_xb = sem("residual_ready"); s_z = sem("z_ready"); s_bs = sem("stats_ready"); s_mv = sem("mean_var_ready")
        s_ve = sem("var_eps_ready"); s_rs = sem("rstd_ready"); s_ln = sem("normed")

        block = ph.ctx.enter_context(nc.Block())
        n_consts = 16 * 5

        @block.sync
        def _(sp):
            sp.dma_start(idn[:, :], ident).then_inc(first, 16)

            def slot(t):
                a = t.at(4)
                if a.there:
                    freed(sp, s_tr, a, 4)
                    sp.dma_start(x_t[:, a.buf(4), :], x_in[a.n]).then_inc(xl[a.buf(4)], 16)
                if t.there:
                    freed(sp, s_xb, t, 2)
                    sp.dma_start(xr_t[:, t.buf(2), :], x_in[t.n]).then_inc(rl[t.buf(2)], 16)
                o = t.at(-2)
                if o.there:
                    done(sp, s_ln, o)
                    sp.dma_start(x_out[o.n], y_t[:, o.buf(4), :]).then_inc(stored[o.buf(4)], 16)

            run_slots(sp, slot, -4, NB + 2)
            for k in range(4):
                sp.wait_ge(stored[k], 16 * NB // 4)

        @block.gpsimd
        def _(pool):
            pool.memset(va[:, :, :, DK:DK + 1], 1.0).then_inc(blank, 1)
            pool.memset(half[:, :], -0.5).then_inc(blank, 1)
            pool.memset(eps[:, :], EPS_LN).then_inc(blank, 1)
            pool.memset(lnm[:, :], -1.7328679513998633).then_inc(blank, 1)
            pool.wait_ge(blank, 4)
            pool.wait_ge(consts, n_consts)

            def slot(t):
                n = t.at(-2)
                if n.there:
                    done(pool, s_mv, n)
                    freed(pool, s_rs, n, 2)
                    pool.tensor_tensor(vare[:, n.buf(2), :], mv[:, n.buf(2), 1:2], eps[:, :], ALU.add).then_inc(s_ve, 1)
                    done(pool, s_ve, n)
                    freed(pool, s_ln, n, 2)
                    pool.tensor_tensor(rstd[:, n.buf(2), :], vare[:, n.buf(2), :], half[:, :],
                                       ALU.pow).then_inc(s_rs, 1)
                if t.there:
                    loaded(pool, rl, t)
                    freed(pool, s_z, t, 2)
                    pool.tensor_tensor(xb_t[:, t.buf(2), :], xr_t[:, t.buf(2), :], bo_s,
                                       ALU.add).then_inc(s_xb, 1)

            run_slots(pool, slot, 0, NB + 2)

        @block.tensor
        def _(pe):
            pe.wait_ge(first, 16)

            def slot(t):
                a = t.at(2)
                if a.there:
                    loaded(pe, xl, a)
                    freed(pe, s_xc, a, 1)
                    pe.transpose(p_tr[:, 0:P], x_t[:, a.buf(4), :], idn[:, :]).then_inc(s_tr, 1)
                if t.there:
                    done(pe, s_ee, t)
                    freed(pe, s_kc, t, 1)
                    for g in range(G):
                        mm = pe.matmul(p_kv[:, 4 * g * VW:4 * (g + 1) * VW], ek[:, t.buf(2), g * P:(g + 1) * P],
                                       va[:, t.buf(4), 4 * g:4 * g + 4, :], start=True, stop=True)
                    mm.then_inc(s_kv, 1)
                if a.there:
                    if a.opens:
                        pe.wait_ge(consts, n_consts)
                        pe.wait_ge(blank, 4)
                    done(pe, s_xc, a)
                    freed(pe, s_v, a, 1)
                    freed(pe, s_q, a, 1, 4)
                    x = xT[:, a.buf(2), :]
                    pe.matmul(p_pj[:, 0:P], wq_s, x, start=True, stop=True)
                    pe.matmul(p_pj[:, P:2 * P], wk_s, x, start=True, stop=True)
                    pe.matmul(p_pj[:, 2 * P:3 * P], x, wv_s, start=True, stop=True).then_inc(s_pj, 1)
                o = t.at(-1)
                if o.there:
                    done(pe, s_ot, o)
                    freed(pe, s_oc, o, 1)
                    pe.transpose(p_oT[:, 0:P], o_tok[:, o.buf(2), :], idn[:, :]).then_inc(s_oT, 1)
                b = t.at(1)
                if b.there:
                    if b.opens:
                        pe.wait_ge(ready, 6)
                    done(pe, s_kl, b, 2)
                    freed(pe, s_ek, b, 1)
                    i = b.buf(2)
                    products(pe, p_zk[:, :], k_h[:, i, :], k_l[:, i, :], ft_h[:, :], ft_l[:, :], stop=False)
                    pe.matmul(p_zk[:, :], ks_h[:, i, :].bitcast(F32R), nm_h[:, :].bitcast(F32R), start=False,
                              stop=False)
                    pe.matmul(p_zk[:, :], ks_l[:, i, :].bitcast(F32R), nm_h[:, :].bitcast(F32R), start=False,
                              stop=True).then_inc(s_zk, 1)
                if t.there:
                    done(pe, s_kc, t)
                    done(pe, s_qe, t)
                    freed(pe, s_ot, t, 1)
                    for g in range(G):
                        mm = pe.matmul(p_on[:, 4 * g * VW:4 * (g + 1) * VW], eq[:, t.buf(2), g, :],
                                       kvm[:, t.buf(2), 4 * g:4 * g + 4, :], start=True, stop=True)
                    mm.then_inc(s_on, 1)
                if b.there:
                    done(pe, s_q, b, 4)
                    freed(pe, s_eq, b, 1)
                    for g in range(G):
                        out = p_zq[:, g * P:(g + 1) * P]
                        pe.matmul(out, ft[:, g * P:(g + 1) * P], qT[:, b.buf(2), :], start=True, stop=False)
                        mm = pe.matmul(out, nm[:, g * P:(g + 1) * P], qs[:, b.buf(2), :], start=False, stop=True)
                    mm.then_inc(s_zq, 1)
                if o.there:
                    done(pe, s_oc, o)
                    freed(pe, s_z, o, 1)
                    pe.matmul(p_y[:, 0:P], oT[:, o.buf(2), :], wo_s, start=True, stop=True).then_inc(s_y, 1)

            run_slots(pe, slot, -2, NB + 1)

        @block.scalar
        def _(act):
            act.dma_start(w_s[:, :, :], w_qkvo).then_inc(consts, 16)
            act.dma_start(b_s[:, :], b_qk).then_inc(consts, 16)
            act.dma_start(bvo_s[:, :, :], b_vo.partition_broadcast(P)).then_inc(consts, 16)
            act.dma_start(fn_s[:, :, :], feat_norm).then_inc(consts, 16)
            act.dma_start(own[:, :, :], own_head).then_inc(consts, 16)
            act.wait_ge(blank, 4)
            act.activation(warm[:, :], half[:, :], ACT.Exp)

            def slot(t):
                a = t.at(2)
                if a.there:
                    done(act, s_tr, a)
                    freed(act, s_pj, a, 2)
                    act.copy(xT[:, a.buf(2), :], p_tr[:, 0:P]).then_inc(s_xc, 1)
                    if a.opens:
                        act.wait_ge(consts, n_consts)
                        act.wait_ge(ready, 2)
                    done(act, s_pj, a)
                    freed(act, s_zq, a, 2)
                    freed(act, s_kl, a, 2, 2)
                    for dst, fn, k, bias, scale in ((qT, ACT.Identity, 0, bq_s, 1.0), (qs, ACT.Square, 0, bqs[:, :], root),
                                                    (kT, ACT.Identity, 1, bk_s, 1.0), (ks, ACT.Square, 1, bks[:, :], root)):
                        act.activation(dst[:, a.buf(2), :], p_pj[:, k * P:(k + 1) * P], fn,
                                       bias=bias, scale=scale).then_inc(s_q, 1)
                b = t.at(1)
                if b.there:
                    done(act, s_zk, b)
                    freed(act, s_kv, b, 2)
                    act.activation(ek[:, b.buf(2), :], p_zk[:, :], ACT.Exp, bias=lnm[:, :]).then_inc(s_ek, 1)
                    done(act, s_zq, b)
                    freed(act, s_on, b, 2)
                    act.activation(eq[:, b.buf(2)], p_zq[:, :], ACT.Exp, bias=lnm[:, :]).then_inc(s_eq, 1)

            run_slots(act, slot, -2, NB)

        @block.vector
        def _(dve):
            dve.wait_ge(consts, n_consts)
            dve.wait_ge(blank, 4)
            dve.tensor_scalar(bqs[:, :], bq_s, root, None, ALU.mult).then_inc(ready, 1)
            dve.tensor_scalar(bks[:, :], bk_s, root, None, ALU.mult).then_inc(ready, 1)
            dve.tensor_scalar(ft[:, :], ft_raw, root, None, ALU.mult).then_inc(ready, 1)
            high(dve, nm_h[:, :], nm).then_inc(ready, 1)
            dve.wait_ge(ready, 4)
            high(dve, ft_h[:, :], ft[:, :]).then_inc(ready, 1)
            dve.wait_ge(ready, 5)
            low(dve, ft_l[:, :], ft[:, :], ft_h[:, :]).then_inc(ready, 1)

            def slot(t):
                if t.there:
                    done(dve, s_kv, t)
                    freed(dve, s_on, t, 2)
                    dve.tensor_tensor(kvm[:, t.buf(2)], p_kv[:, 0:H * VW], own[:, :, :],
                                      ALU.mult).then_inc(s_kc, 1)
                a = t.at(2)
                if a.there:
                    done(dve, s_pj, a)
                    done(dve, s_q, a, 4)
                    freed(dve, s_kv, a, 4)
                    dve.tensor_tensor(va[:, a.buf(4), :, 0:DK], p_pj[:, 2 * P:3 * P].rearrange("p (h d) -> p h d", d=DK),
                                      bv_s.rearrange("p (h d) -> p h d", d=DK), ALU.add).then_inc(s_v, 1)
                    i = a.buf(2)
                    freed(dve, s_zk, a, 2)
                    high(dve, k_h[:, i, :], kT[:, i, :]).then_inc(s_kh, 1)
                    high(dve, ks_h[:, i, :], ks[:, i, :]).then_inc(s_kh, 1)
                    done(dve, s_kh, a, 2)
                    low(dve, k_l[:, i, :], kT[:, i, :], k_h[:, i, :]).then_inc(s_kl, 1)
                    low(dve, ks_l[:, i, :], ks[:, i, :], ks_h[:, i, :]).then_inc(s_kl, 1)
                n = t.at(-2)
                if n.there:
                    done(dve, s_rs, n)
                    if n.at(-4).there:
                        loaded(dve, stored, n.at(-4))
                    dve.tensor_scalar(y_t[:, n.buf(4), :], z[:, n.buf(2), :], mv[:, n.buf(2), 0:1],
                                      rstd[:, n.buf(2), :], ALU.subtract, ALU.mult).then_inc(s_ln, 1)
                o = t.at(-1)
                if o.there:
                    done(dve, s_oT, o)
                    freed(dve, s_y, o, 2)
                    dve.tensor_copy(oT[:, o.buf(2), :], p_oT[:, 0:P]).then_inc(s_oc, 1)
                b = t.at(1)
                if b.there:
                    done(dve, s_ek, b)
                    dve.tensor_scalar(ek[:, b.buf(2), :], ek[:, b.buf(2), :], 1e-6 / M ** 0.5, None,
                                      ALU.add).then_inc(s_ee, 1)
                if t.there:
                    done(dve, s_on, t)
                    on = p_on[:, 0:H * VW].rearrange("p (h e) -> p h e", e=VW)
                    freed(dve, s_ot, t, 2)
                    dve.reciprocal(rden[:, t.buf(2), :], on[:, :, DK]).then_inc(s_rd, 1)
                    done(dve, s_rd, t)
                    freed(dve, s_oT, t, 2)
                    dve.tensor_tensor(o_tok[:, t.buf(2), :].rearrange("p (h d) -> p h d", d=DK), on[:, :, 0:DK],
                                      rden[:, t.buf(2), :].unsqueeze(2).broadcast_to([P, H, DK]),
                                      ALU.mult).then_inc(s_ot, 1)
                if o.there:
                    done(dve, s_y, o)
                    done(dve, s_xb, o)
                    freed(dve, s_ln, o, 2)
                    dve.tensor_tensor(z[:, o.buf(2), :], p_y[:, 0:P], xb_t[:, o.buf(2), :], ALU.add).then_inc(s_z, 1)
                    done(dve, s_z, o)
                    dve.bn_stats(stats[:, o.buf(2), :], z[:, o.buf(2), :]).then_inc(s_bs, 1)
                    done(dve, s_bs, o)
                    freed(dve, s_ve, o, 2)
                    dve.tensor_copy(mark[:, :], stats[:, o.buf(2), 0:1])
                    dve.bn_aggr(mv[:, o.buf(2), :], stats[:, o.buf(2), :]).then_inc(s_mv, 1)
                if b.there:
                    done(dve, s_eq, b)
                    dve.tensor_scalar(eq[:, b.buf(2)], eq[:, b.buf(2)], 1e-6 / M ** 0.5, None,
                                      ALU.add).then_inc(s_qe, 1)

            run_slots(dve, slot, -2, NB + 2)


CT = 4
NC = NB // CT


def run_chunks(eng, body):
    body(0)
    with eng.Fori(1, NC) as c:
        body(c)


def later(c):
    return not isinstance(c, int) or c > 0


def has(c):
    return not isinstance(c, int) or 0 <= c < NC


def since(eng, sem, count):
    if not isinstance(count, int) or count > 0:
        eng.wait_ge(sem, count)


def run_paired(eng, slot):
    for c in (0, 1):
        slot(c, c, 0)
    with eng.Fori(1, NC // 2 - 1) as lap:
        for u in (0, 1):
            slot(2 * lap + u, u, lap)
    for c in (NC - 2, NC - 1, NC):
        slot(c, c % 2, c // 2)


def run_staggered(eng, slot):
    slot(0)
    slot(1)
    with eng.Fori(2, NC - 1) as c:
        slot(c)
    slot(NC - 1)
    slot(NC)


def feed_forward(nc, name, banks, x_in, x_out, w1, w2, h1, h2, w3, s_hidden, s_out, ident):
    F = 4
    ph = Phase(nc, name, banks)
    with ph:
        sb, ps, sem = ph.sb, ph.ps, ph.sem
        idn = sb("idn", [P, P])
        w1_s, w2_s = sb("w1", [P, F * P]), sb("w2", [P, F * P])
        w1_h, w2_h = sb("w1_high", [P, F * P]), sb("w2_high", [P, F * P])
        w1_l, w2_l = sb("w1_low", [P, F * P]), sb("w2_low", [P, F * P])
        h1_s, h2_s, w3_s = sb("h1", [P, F, F * P]), sb("h2", [P, F, F * P]), sb("w3", [P, F, P])
        h1_h, h2_h = sb("h1_high", [P, F, F * P]), sb("h2_high", [P, F, F * P])
        h1_l, h2_l = sb("h1_low", [P, F, F * P]), sb("h2_low", [P, F, F * P])
        sh = sb("sh", [P, 4, F])
        so = sb("so", [P, P]); w3_o = sb("w3o", [P, F, P])
        half, eps = sb("half", [P, CT]), sb("eps", [P, CT])
        x_t = sb("x", [P, CT, P]); xr_t = sb("xr", [P, CT, P])
        xT = sb("xT", [P, CT, P]); xT_h = sb("xT_high", [P, CT, P]); xT_l = sb("xT_low", [P, CT, P])
        gate = sb("gate", [P, 2, CT * P])
        a0, a0_h, a0_l = sb("a0", [P, F, CT * P]), sb("a0_high", [P, F, CT * P]), sb("a0_low", [P, F, CT * P])
        a1, a1_h, a1_l = sb("a1", [P, F, CT * P]), sb("a1_high", [P, F, CT * P]), sb("a1_low", [P, F, CT * P])
        a2 = sb("a2", [P, F, CT * P])
        z = sb("z", [P, CT, P]); mark = sb("mark", [P, CT]); stats = sb("stats", [P, CT, 6])
        mv = sb("mv", [P, CT, 2]); vare = sb("vare", [P, CT]); rstd = sb("rstd", [P, CT])
        y_t = sb("y", [P, CT, P])
        p_u = [ps(), ps()]; p_v = [ps(), ps()]
        p_h = [ps(), ps()]; p_tr, p_y = ps(), ps()

        consts = sem("gate_loaded"); hidden = sem("hidden_loaded")
        ready = sem("w3_scaled"); blank = sem("blanks_ready")
        s_wh = sem("weights_high"); s_wl = sem("weights_low")
        xl, rl, stored = sem("x_loaded"), sem("xr_loaded"), sem("y_stored")
        s_tr = sem("x_transposed"); s_xc = sem("x_copied"); s_xh = sem("x_high"); s_xl = sem("x_low")
        s_u = sem("u_done"); s_v = sem("v_done"); s_g = sem("gate_ready"); s_a0 = sem("a0_ready")
        s_h0 = sem("a0_high_ready"); s_l0 = sem("a0_low_ready")
        s_m1 = sem("h1_done"); s_a1 = sem("a1_ready"); s_m2 = sem("h2_done"); s_a2 = sem("a2_ready")
        s_h1 = sem("a1_high_ready"); s_l1 = sem("a1_low_ready")
        s_y = sem("y_done"); s_z = sem("z_ready"); s_bs = sem("stats_ready"); s_mv = sem("mean_var_ready")
        s_ve = sem("var_eps_ready"); s_rs = sem("rstd_ready"); s_ln = sem("normed")

        block = ph.ctx.enter_context(nc.Block())

        def rows(a):
            return a.rearrange("t p d -> p t d")

        @block.sync
        def _(sp):
            sp.dma_start(x_t[:, :, :], rows(x_in[0])).then_inc(xl, 16)
            for dst, src in ((idn[:, :], ident), (sh[:, :, :], s_hidden), (w1_s[:, :], w1), (w2_s[:, :], w2)):
                sp.dma_start(dst, src).then_inc(consts, 16)
            for dst, src in ((h1_s[:, :, :], h1), (h2_s[:, :, :], h2), (w3_s[:, :, :], w3),
                             (so[:, :], s_out.partition_broadcast(P))):
                sp.dma_start(dst, src).then_inc(hidden, 16)

            def slot(c):
                if has(c + 1):
                    sp.wait_ge(s_tr, c + 1)
                    sp.dma_start(x_t[:, :, :], rows(x_in[c + 1])).then_inc(xl, 16)
                if has(c - 1):
                    since(sp, s_z, c - 1)
                    sp.dma_start(xr_t[:, :, :], rows(x_in[c - 1])).then_inc(rl, 16)
                if has(c - 2):
                    sp.wait_ge(s_ln, 4 * (c - 1))
                    sp.dma_start(rows(x_out[c - 2]), y_t[:, :, :]).then_inc(stored, 16)

            run_staggered(sp, slot)
            sp.wait_ge(s_ln, 4 * NC)
            sp.dma_start(rows(x_out[NC - 1]), y_t[:, :, :]).then_inc(stored, 16)
            sp.wait_ge(stored, 16 * NC)

        @block.gpsimd
        def _(pool):
            pool.memset(half[:, :], -0.5).then_inc(blank, 1)
            pool.memset(eps[:, :], EPS_LN).then_inc(blank, 1)
            pool.wait_ge(blank, 2)
            for n, (w_l, w, w_h) in enumerate(((w1_l[:, :], w1_s[:, :], w1_h[:, :]),
                                               (w2_l[:, :], w2_s[:, :], w2_h[:, :]),
                                               (h1_l[:, :, :], h1_s[:, :, :], h1_h[:, :, :]),
                                               (h2_l[:, :, :], h2_s[:, :, :], h2_h[:, :, :]))):
                pool.wait_ge(s_wh, n + 1)
                low(pool, w_l, w, w_h).then_inc(s_wl, 1)

            def slot(c):
                if has(c - 1):
                    pool.wait_ge(s_mv, 4 * c)
                    pool.tensor_tensor(vare[:, :], mv[:, :, 1], eps[:, :], ALU.add).then_inc(s_ve, 1)
                    pool.wait_ge(s_ve, c)
                    since(pool, s_ln, 4 * (c - 1))
                    pool.tensor_tensor(rstd[:, :], vare[:, :], half[:, :], ALU.pow).then_inc(s_rs, 1)

            run_staggered(pool, slot)

        @block.tensor
        def _(pe):
            def transposes(c):
                pe.wait_ge(xl, 16 * (c + 1))
                since(pe, s_xc, c)
                for k in range(CT):
                    mm = pe.transpose(p_tr[:, k * P:(k + 1) * P], x_t[:, k, :], idn[:, :])
                mm.then_inc(s_tr, 1)

            def gated(c):
                pe.wait_ge(s_xl, c + 1)
                for m in range(F):
                    if m == 2 and has(c - 1):
                        output(c - 1)
                    cols = slice(m * P, (m + 1) * P)
                    since(pe, s_a0, F * c + m - 1)
                    products(pe, p_u[m % 2][:, :], w1_h[:, cols], w1_l[:, cols], xT_h[:, :, :],
                             xT_l[:, :, :]).then_inc(s_u, 1)
                    products(pe, p_v[m % 2][:, :], w2_h[:, cols], w2_l[:, cols], xT_h[:, :, :],
                             xT_l[:, :, :]).then_inc(s_v, 1)

            def hidden_layer(c, w_l, w_h, a_l, a_h, s_low, s_done, s_read, s_before):
                for m in range(F):
                    if m >= 2:
                        pe.wait_ge(s_read, F * c + m - 1)
                    else:
                        since(pe, *s_before(m))
                    cols = slice(m * P, (m + 1) * P)
                    for k in range(F):
                        if m == 0:
                            pe.wait_ge(s_low, F * c + k + 1)
                        mm = products(pe, p_h[m % 2][:, :], w_h[:, k, cols], w_l[:, k, cols], a_h[:, k, :],
                                      a_l[:, k, :], start=(k == 0), stop=(k == F - 1))
                    mm.then_inc(s_done, 1)

            def output(c):
                since(pe, s_z, c)
                pe.wait_ge(s_a2, F * c + F)
                for j in range(CT):
                    for k in range(F):
                        mm = pe.matmul(p_y[:, j * P:(j + 1) * P], a2[:, k, j * P:(j + 1) * P], w3_o[:, k, :],
                                       start=(k == 0), stop=(k == F - 1))
                mm.then_inc(s_y, 1)

            def slot(c):
                first = isinstance(c, int) and c == 0
                if has(c):
                    gated(c)
                else:
                    output(c - 1)
                if has(c):
                    if first:
                        pe.wait_ge(s_wl, 3)
                    hidden_layer(c, h1_l, h1_h, a0_l, a0_h, s_l0, s_m1, s_a1, lambda m: (s_a2, F * c - 2 + m + 1))
                if has(c + 1):
                    transposes(c + 1)
                if has(c):
                    if first:
                        pe.wait_ge(s_wl, 4)
                        pe.wait_ge(ready, F)
                    hidden_layer(c, h2_l, h2_h, a1_l, a1_h, s_l1, s_m2, s_a2, lambda m: (s_a1, F * c + m + 3))

            pe.wait_ge(consts, 64)
            transposes(0)
            pe.wait_ge(s_wl, 2)
            run_staggered(pe, slot)

        @block.scalar
        def _(act):
            def copy_x(c):
                act.wait_ge(s_tr, c + 1)
                since(act, s_v, F * c)
                act.copy(xT[:, :, :], p_tr[:, :]).then_inc(s_xc, 1)

            def slot(c):
                if has(c):
                    for m in range(F):
                        act.wait_ge(s_u, F * c + m + 1)
                        since(act, s_a0, F * c + m - 1)
                        act.activation(gate[:, m % 2, :], p_u[m % 2][:, :], ACT.Silu,
                                       scale=sh[:, 0, m:m + 1]).then_inc(s_g, 1)
                    for m in range(F):
                        act.wait_ge(s_m1, F * c + m + 1)
                        if m == 0:
                            since(act, s_m2, F * c)
                        act.activation(a1[:, m, :], p_h[m % 2][:, :], ACT.Gelu,
                                       scale=sh[:, 2, m:m + 1]).then_inc(s_a1, 1)
                if has(c + 1):
                    copy_x(c + 1)
                if has(c):
                    for m in range(F):
                        act.wait_ge(s_m2, F * c + m + 1)
                        if m == 0:
                            since(act, s_y, c)
                        act.activation(a2[:, m, :], p_h[m % 2][:, :], ACT.Gelu,
                                       scale=sh[:, 3, m:m + 1]).then_inc(s_a2, 1)

            act.wait_ge(consts, 64)
            copy_x(0)
            run_staggered(act, slot)

        @block.vector
        def _(dve):
            def split(whole, high_part, low_part, s_whole, s_high, s_low, count):
                dve.wait_ge(s_whole, count)
                high(dve, high_part, whole).then_inc(s_high, 1)
                dve.wait_ge(s_high, count)
                low(dve, low_part, whole, high_part).then_inc(s_low, 1)

            def split_x(c):
                since(dve, s_v, F * c)
                split(xT[:, :, :], xT_h[:, :, :], xT_l[:, :, :], s_xc, s_xh, s_xl, c + 1)

            def slot(c):
                if has(c):
                    since(dve, s_m1, F * c)
                    for m in range(F):
                        dve.wait_ge(s_g, F * c + m + 1)
                        dve.wait_ge(s_v, F * c + m + 1)
                        dve.scalar_tensor_tensor(a0[:, m, :], p_v[m % 2][:, :], sh[:, 1, m:m + 1],
                                                 gate[:, m % 2, :], ALU.mult, ALU.mult).then_inc(s_a0, 1)
                        split(a0[:, m, :], a0_h[:, m, :], a0_l[:, m, :], s_a0, s_h0, s_l0, F * c + m + 1)
                if has(c - 1):
                    dve.wait_ge(s_y, c)
                    dve.wait_ge(rl, 16 * c)
                    since(dve, s_ln, 4 * (c - 1))
                    dve.tensor_tensor(z[:, :, :], p_y[:, :].rearrange("p (t d) -> p t d", d=P), xr_t[:, :, :],
                                      ALU.add).then_inc(s_z, 1)
                    dve.wait_ge(s_z, c)
                    for j in range(CT):
                        dve.bn_stats(stats[:, j, :], z[:, j, :]).then_inc(s_bs, 1)
                    since(dve, s_ve, c - 1)
                    for j in range(CT):
                        dve.wait_ge(s_bs, 4 * (c - 1) + j + 1)
                        dve.tensor_copy(mark[:, j:j + 1], stats[:, j, 0:1])
                        dve.bn_aggr(mv[:, j, :], stats[:, j, :]).then_inc(s_mv, 1)
                if has(c):
                    since(dve, s_m2, F * c)
                    for m in range(F):
                        split(a1[:, m, :], a1_h[:, m, :], a1_l[:, m, :], s_a1, s_h1, s_l1, F * c + m + 1)
                if has(c - 1):
                    dve.wait_ge(s_rs, c)
                    since(dve, stored, 16 * (c - 1))
                    for j in range(CT):
                        dve.tensor_scalar(y_t[:, j, :], z[:, j, :], mv[:, j, 0:1], rstd[:, j:j + 1],
                                          ALU.subtract, ALU.mult).then_inc(s_ln, 1)
                if has(c + 1):
                    split_x(c + 1)

            dve.wait_ge(consts, 64)
            high(dve, w1_h[:, :], w1_s[:, :]).then_inc(s_wh, 1)
            high(dve, w2_h[:, :], w2_s[:, :]).then_inc(s_wh, 1)
            split_x(0)
            dve.wait_ge(hidden, 64)
            high(dve, h1_h[:, :, :], h1_s[:, :, :]).then_inc(s_wh, 1)
            high(dve, h2_h[:, :, :], h2_s[:, :, :]).then_inc(s_wh, 1)
            for k in range(F):
                dve.tensor_tensor(w3_o[:, k, :], w3_s[:, k, :], so[:, :], ALU.mult).then_inc(ready, 1)
            run_staggered(dve, slot)


def mixture(nc, name, banks, x_in, x_out, router, w1, w2, ident, before, iota):
    E, TOP_K, F = 8, 2, 4
    CAP = int(1.25 * NB * P * TOP_K / E) + 1
    TE = NB * E
    ph = Phase(nc, name, banks)
    with ph:
        sb, ps, sem = ph.sb, ph.ps, ph.sem
        xh, xl_ = sb("x_high", [P, NB, P]), sb("x_low", [P, NB, P])
        w1_h, w1_l = sb("w1_high", [P, E, F * P]), sb("w1_low", [P, E, F * P])
        w1_s, w2_s = sb("w1", [P, E, F * P]), sb("w2", [P, E, F, P])
        gates = sb("gates", [P, NB, E])
        half, eps = sb("half", [P, CT]), sb("eps", [P, CT])
        p = [ps() for k in range(8)]
        wl, wl2 = sem("w1_loaded"), sem("w2_loaded")
        idn, bef, io, rw = sb("idn", [P, P]), sb("bef", [P, P]), sb("io", [P, E]), sb("rw", [P, E])
        ones = sb("ones", [P, P])
        x_t, xc = sb("x", [P, 2, CT, P]), sb("xc", [P, 2, CT, P])
        lg = sb("lg", [P, NB, E])
        v = {n: sb(n, [P, NB, E]) for n in ("sh", "ex", "pr", "eq", "far", "o1", "p2", "eq2", "far2", "o2",
                                             "both", "wa", "wb", "wsum", "cnt", "keep", "gate0", "tot", "c0", "c1", "tin")}
        r = {n: sb(n, [P, NB]) for n in ("mx", "sm", "rs", "m1", "i1", "m2", "i2", "dn", "rd")}
        consts, xl, s_tr, s_xc = sem("consts"), sem("x_loaded", 2), sem("x_transposed"), sem("x_copied")
        s_xh = sem("x_high_kept")
        s_xa, s_lg, s_lc = sem("x_low_kept"), sem("logits_done"), sem("logits_copied")
        chain = sem("vector_steps"); s_ex = sem("exp_done"); s_cn = sem("counts_done"); blank = sem("blank")
        N_BOTH = 18
        xr_t = sb("xr", [P, CT, P]); gc = sb("gc", [P, CT, E])
        hid = sb("hid", [P, 2, F, CT * P])
        acc = sb("acc", [P, 2, CT, P])
        mark = sb("mark", [P, CT]); stats = sb("stats", [P, CT, 6]); mv = sb("mv", [P, CT, 2])
        vare = sb("vare", [P, CT]); rstd = sb("rstd", [P, CT]); y_t = sb("y", [P, CT, P])
        rl, stored = sem("xr_loaded"), sem("y_stored")
        s_gc, s_x2, s_h, s_si = sem("gates_copied"), sem("sum_started"), sem("hidden_done"), sem("silu_done")
        s_y, s_ac = sem("expert_done"), sem("expert_added")
        s_bs, s_mv, s_ve, s_rs, s_ln = (sem(n) for n in ("stats_ready", "mean_var_ready", "var_eps_ready",
                                                           "rstd_ready", "normed"))
        s_wh, s_wl = sem("expert_high"), sem("expert_low")
        p_h, p_y = p[0:4], p[4:6]
        block = ph.ctx.enter_context(nc.Block())

        @block.sync
        def _(sp):
            for dst, src in ((idn, ident), (bef, before), (io, iota), (rw, router)):
                sp.dma_start(dst[:, :], src).then_inc(consts, 16)

            def routed(c, u, lap):
                if has(c):
                    since(sp, s_tr, c - 1)
                    sp.dma_start(x_t[:, u, :, :], x_in[c].rearrange("t p d -> p t d")).then_inc(xl[u], 16)

            run_paired(sp, routed)
            sp.dma_start(w1_s[:, :, :], w1).then_inc(wl, 16)
            sp.dma_start(w2_s[:, :, :, :], w2).then_inc(wl2, 16)

            def body(c):
                if later(c):
                    sp.wait_ge(s_x2, c)
                sp.dma_start(xr_t[:, :, :], x_in[c].rearrange("t p d -> p t d")).then_inc(rl, 16)
                sp.wait_ge(s_ln, 4 * c + 4)
                sp.dma_start(x_out[c].rearrange("t p d -> p t d"), y_t[:, :, :]).then_inc(stored, 16)

            run_chunks(sp, body)
            sp.wait_ge(stored, 16 * NC)

        @block.gpsimd
        def _(pool):
            pool.memset(ones[:, :], 1.0).then_inc(blank, 1)
            pool.memset(half[:, :], -0.5).then_inc(blank, 1)
            pool.memset(eps[:, :], EPS_LN).then_inc(blank, 1)
            pool.wait_ge(blank, 3)
            for e in range(E):
                pool.wait_ge(s_wh, e + 1)
                low(pool, w1_l[:, e, :], w1_s[:, e, :], w1_h[:, e, :]).then_inc(s_wl, 1)

            def body(c):
                pool.wait_ge(s_mv, 4 * c + 4)
                pool.tensor_tensor(vare[:, :], mv[:, :, 1], eps[:, :], ALU.add).then_inc(s_ve, 1)
                pool.wait_ge(s_ve, c + 1)
                if later(c):
                    pool.wait_ge(s_ln, 4 * c)
                pool.tensor_tensor(rstd[:, :], vare[:, :], half[:, :], ALU.pow).then_inc(s_rs, 1)

            run_chunks(pool, body)

        @block.tensor
        def _(pe):
            pe.wait_ge(consts, 64)
            pe.wait_ge(blank, 3)

            def routed(c, u, lap):
                if has(c):
                    pe.wait_ge(xl[u], 16 * (lap + 1))
                    since(pe, s_xc, c - 1)
                    for k in range(CT):
                        mm = pe.transpose(p[u][:, k * P:(k + 1) * P], x_t[:, u, k, :], idn[:, :])
                    mm.then_inc(s_tr, 1)
                if has(c - 1):
                    pe.wait_ge(s_xc, c)
                    since(pe, s_lc, c - 1)
                    for k in range(CT):
                        mm = pe.matmul(p[2][:, k * E:(k + 1) * E], xc[:, 1 - u, k, :], rw[:, :], start=True,
                                       stop=True)
                    mm.then_inc(s_lg, 1)

            def counts():
                pe.wait_ge(chain, N_BOTH)
                pe.matmul(p[6][:, 0:TE], bef[:, :], v["both"][:, :, :], start=True, stop=True)
                pe.matmul(p[7][:, 0:TE], ones[:, :], v["both"][:, :, :], start=True, stop=True).then_inc(s_cn, 1)

            run_paired(pe, routed)
            pe.wait_ge(s_lc, NC)
            pe.wait_ge(s_xa, NC)

            def body(c):
                def hidden(e):
                    if not later(c):
                        pe.wait_ge(s_wl, e + 1)
                    for f in range(F):
                        if e > 0:
                            pe.wait_ge(s_si, F * (E * c + e - 1) + f + 1)
                        elif later(c):
                            pe.wait_ge(s_si, F * (E * c - 1) + f + 1)
                        cols, toks = slice(f * P, (f + 1) * P), bass.ds(4 * c, CT)
                        products(pe, p_h[f][:, :], w1_h[:, e, cols], w1_l[:, e, cols], xh[:, toks, :],
                                 xl_[:, toks, :]).then_inc(s_h, 1)

                def output(e):
                    pe.wait_ge(s_si, F * (E * c + e) + F)
                    if e >= 2:
                        pe.wait_ge(s_ac, CT * (E * c + e - 1))
                    elif later(c):
                        pe.wait_ge(s_ac, CT * (E * c + e - 1))
                    for j in range(CT):
                        for f in range(F):
                            toks = slice(j * P, (j + 1) * P)
                            mm = pe.matmul(p_y[e % 2][:, toks], hid[:, e % 2, f, toks], w2_s[:, e, f, :],
                                           start=(f == 0), stop=(f == F - 1))
                    mm.then_inc(s_y, 1)

                for e in range(E + 1):
                    if e < E:
                        hidden(e)
                    if e == 1 and not later(c):
                        pe.wait_ge(wl2, 16)
                    if e > 0:
                        output(e - 1)
                    if e == 1 and not later(c):
                        counts()

            run_chunks(pe, body)

        @block.scalar
        def _(act):

            def routed(c, u, lap):
                if has(c):
                    act.wait_ge(s_tr, c + 1)
                    since(act, s_lg, c - 1)
                    since(act, s_xa, c - 1)
                    act.copy(xc[:, u, :, :], p[u][:, :]).then_inc(s_xc, 1)

            run_paired(act, routed)
            act.wait_ge(wl, 16)
            for e in range(E):
                act.copy(w1_h[:, e, :].bitcast(F32R), w1_s[:, e, :]).then_inc(s_wh, 1)
            act.wait_ge(chain, 2)
            act.activation(v["ex"][:, :, :], v["sh"][:, :, :], ACT.Exp).then_inc(s_ex, 1)

            def body(c):
                for e in range(E):
                    if e >= 2 or later(c):
                        act.wait_ge(s_y, E * c + e - 1)
                    for f in range(F):
                        act.wait_ge(s_h, F * (E * c + e) + f + 1)
                        act.activation(hid[:, e % 2, f, :], p_h[f][:, :], ACT.Silu).then_inc(s_si, 1)

            run_chunks(act, body)

        @block.vector
        def _(dve):
            steps = [0]

            def then(ins):
                steps[0] += 1
                ins.then_inc(chain, 1)
                dve.wait_ge(chain, steps[0])

            def wide(a):
                return a[:, :].unsqueeze(2).broadcast_to([P, NB, E])

            def tt(out, a, b, op):
                then(dve.tensor_tensor(out, a, b, op))

            def routed(c, u, lap):
                if has(c):
                    dve.wait_ge(s_xc, c + 1)
                    toks = bass.ds(4 * c, CT)
                    high(dve, xh[:, toks, :], xc[:, u, :, :]).then_inc(s_xh, 1)
                    dve.wait_ge(s_xh, c + 1)
                    low(dve, xl_[:, toks, :], xc[:, u, :, :], xh[:, toks, :]).then_inc(s_xa, 1)
                if has(c - 1):
                    dve.wait_ge(s_lg, c)
                    dve.tensor_copy(lg[:, bass.ds(4 * (c - 1), CT), :], p[2][:, 0:CT * E]).then_inc(s_lc, 1)

            dve.wait_ge(consts, 64)
            run_paired(dve, routed)
            dve.wait_ge(s_lc, NC)
            col = io[:, :].unsqueeze(1).broadcast_to([P, NB, E])
            then(dve.tensor_reduce(r["mx"][:, :], lg[:, :, :], AX_X, ALU.max))
            tt(v["sh"][:, :, :], lg[:, :, :], wide(r["mx"]), ALU.subtract)
            dve.wait_ge(s_ex, 1)
            then(dve.tensor_reduce(r["sm"][:, :], v["ex"][:, :, :], AX_X, ALU.add))
            then(dve.reciprocal(r["rs"][:, :], r["sm"][:, :]))
            tt(v["pr"][:, :, :], v["ex"][:, :, :], wide(r["rs"]), ALU.mult)
            then(dve.tensor_reduce(r["m1"][:, :], v["pr"][:, :, :], AX_X, ALU.max))
            tt(v["eq"][:, :, :], v["pr"][:, :, :], wide(r["m1"]), ALU.is_equal)
            then(dve.scalar_tensor_tensor(v["far"][:, :, :], v["eq"][:, :, :], -float(E), col, ALU.mult, ALU.add))
            then(dve.tensor_reduce(r["i1"][:, :], v["far"][:, :, :], AX_X, ALU.min))
            tt(v["o1"][:, :, :], v["far"][:, :, :], wide(r["i1"]), ALU.is_equal)
            then(dve.scalar_tensor_tensor(v["p2"][:, :, :], v["o1"][:, :, :], -2.0, v["pr"][:, :, :], ALU.mult, ALU.add))
            then(dve.tensor_reduce(r["m2"][:, :], v["p2"][:, :, :], AX_X, ALU.max))
            tt(v["eq2"][:, :, :], v["p2"][:, :, :], wide(r["m2"]), ALU.is_equal)
            then(dve.scalar_tensor_tensor(v["far2"][:, :, :], v["eq2"][:, :, :], -float(E), col, ALU.mult, ALU.add))
            then(dve.tensor_reduce(r["i2"][:, :], v["far2"][:, :, :], AX_X, ALU.min))
            tt(v["o2"][:, :, :], v["far2"][:, :, :], wide(r["i2"]), ALU.is_equal)
            tt(v["wa"][:, :, :], v["o1"][:, :, :], wide(r["m1"]), ALU.mult)
            tt(v["both"][:, :, :], v["o1"][:, :, :], v["o2"][:, :, :], ALU.add)
            assert steps[0] == N_BOTH
            tt(v["wb"][:, :, :], v["o2"][:, :, :], wide(r["m2"]), ALU.mult)
            tt(v["wsum"][:, :, :], v["wa"][:, :, :], v["wb"][:, :, :], ALU.add)
            tt(r["dn"][:, :], r["m1"][:, :], r["m2"][:, :], ALU.add)
            then(dve.reciprocal(r["rd"][:, :], r["dn"][:, :]))
            tt(v["gate0"][:, :, :], v["wsum"][:, :, :], wide(r["rd"]), ALU.mult)
            dve.wait_ge(s_cn, 1)
            then(dve.tensor_copy(v["tot"][:, :, :], p[7][:, 0:TE]))
            then(dve.tensor_copy(v["tin"][:, :, :], p[6][:, 0:TE]))
            src, dst, other, d = v["tot"], v["c0"], v["c1"], 1
            while d < NB:
                then(dve.tensor_copy(dst[:, 0:d, :], src[:, 0:d, :]))
                tt(dst[:, d:NB, :], src[:, d:NB, :], src[:, 0:NB - d, :], ALU.add)
                src, dst, other, d = dst, other, dst, 2 * d
            tt(v["cnt"][:, :, :], src[:, :, :], v["tot"][:, :, :], ALU.subtract)
            tt(v["wa"][:, :, :], v["cnt"][:, :, :], v["tin"][:, :, :], ALU.add)
            then(dve.tensor_scalar(v["keep"][:, :, :], v["wa"][:, :, :], float(CAP), None, ALU.is_lt))
            tt(gates[:, :, :], v["gate0"][:, :, :], v["keep"][:, :, :], ALU.mult)

            def body(c):
                dve.wait_ge(rl, 16 * c + 16)
                if later(c):
                    dve.wait_ge(s_ac, CT * E * c)
                    dve.wait_ge(s_ln, 4 * c)
                dve.tensor_copy(gc[:, :, :], gates[:, bass.ds(4 * c, CT), :]).then_inc(s_gc, 1)
                dve.tensor_scalar(acc[:, 1, :, :], xr_t[:, :, :], 2.0, None, ALU.mult).then_inc(s_x2, 1)
                dve.wait_ge(s_gc, c + 1)
                dve.wait_ge(s_x2, c + 1)

                def add(e):
                    dve.wait_ge(s_y, E * c + e + 1)
                    for j in range(CT):
                        if e > 0:
                            dve.wait_ge(s_ac, CT * (E * c + e - 1) + j + 1)
                        dve.scalar_tensor_tensor(acc[:, e % 2, j, :], p_y[e % 2][:, j * P:(j + 1) * P],
                                                 gc[:, j, e:e + 1], acc[:, 1 - e % 2, j, :], ALU.mult,
                                                 ALU.add).then_inc(s_ac, 1)

                for e in range(E):
                    add(e)
                for j in range(CT):
                    dve.wait_ge(s_ac, CT * (E * c + E - 1) + j + 1)
                    dve.bn_stats(stats[:, j, :], acc[:, 1, j, :]).then_inc(s_bs, 1)
                if later(c):
                    dve.wait_ge(s_ve, c)
                for j in range(CT):
                    dve.wait_ge(s_bs, 4 * c + j + 1)
                    dve.tensor_copy(mark[:, j:j + 1], stats[:, j, 0:1])
                    dve.bn_aggr(mv[:, j, :], stats[:, j, :]).then_inc(s_mv, 1)
                dve.wait_ge(s_rs, c + 1)
                if later(c):
                    dve.wait_ge(stored, 16 * c)
                for j in range(CT):
                    dve.tensor_scalar(y_t[:, j, :], acc[:, 1, j, :], mv[:, j, 0:1], rstd[:, j:j + 1],
                                      ALU.subtract, ALU.mult).then_inc(s_ln, 1)

            run_chunks(dve, body)


def build_decoder(nc, d, out):
    keep = [nc.dram_tensor(f"between{k}", (NB, P, P), F32, kind="Internal").ap() for k in range(5)]

    banks = [nc.alloc_psum_tensor(f"bank{k}", [P, 512], F32) for k in range(8)]

    def chunks(a):
        return a.rearrange("(c t) p d -> c t p d", t=CT)

    linear_attention(nc, "L0a", banks, d["x"], keep[0], d["w_qkvo0"], d["b_qk0"], d["b_vo0"], d["feat_norm"],
                     d["ident"], d["own_head"])
    softmax_attention(nc, "L0x", banks, keep[0], d["ctx"], keep[1], d["w_qkvo1"], d["b_qk1"],
                      d["b_vo1"], d["ident"], d["head8"])
    feed_forward(nc, "L0f", banks, chunks(keep[1]), chunks(keep[2]), d["w1"], d["w2"], d["h1"], d["h2"], d["w3"],
                 d["s_hidden"], d["s_out"], d["ident"])
    trig_attention(nc, "L1a", banks, keep[2], keep[3], d["w_qk"], d["b_qk"], d["quarter"], d["wv2"], d["wo2"],
                   d["ident"], d["head16"], d["causal"])
    softmax_attention(nc, "L1x", banks, keep[3], d["ctx"], keep[4], d["w_qkvo3"], None,
                      d["b_vo3"], d["ident"], d["head8"])
    mixture(nc, "L1f", banks, chunks(keep[4]), chunks(out), d["router"], d["e1"], d["e2"], d["ident"], d["before"],
            d["experts"])


def lay_out(inp):
    import numpy as np

    a = {k: np.asarray(v) for k, v in inp.items()}
    f32 = np.float32
    M = a["L0_attn_orf"].shape[0]
    E, _, FF = a["L1_ffn_w1"].shape
    F = FF // P
    d = {"x": a["x"], "ctx": a["ctx_1024"].transpose(0, 2, 1)}
    for n, pre in ((0, "L0_attn_"), (1, "L0_xattn_"), (3, "L1_xattn_")):
        d[f"w_qkvo{n}"] = np.stack([a[f"{pre}W{w}"].T for w in "qkvo"], 1)
        if n != 3:
            d[f"b_qk{n}"] = np.stack([a[f"{pre}bq"], a[f"{pre}bk"]], 1)
            d[f"b_vo{n}"] = np.stack([a[f"{pre}bv"], a[f"{pre}bo"]])
        else:
            d[f"b_vo{n}"] = a[f"{pre}bo"]
    feat, norm = np.zeros((H, DK, H, M), f32), np.zeros((H, DK, H, M), f32)
    for h in range(H):
        feat[h, :, h, :] = a["L0_attn_orf"].T
        norm[h, :, h, :] = -0.5
    d["feat_norm"] = np.stack([feat.reshape(P, H * M), norm.reshape(P, H * M)], 1)
    own = np.zeros((4, M, 4, 4, DK + 1), f32)
    for j in range(4):
        own[j, :, :, j, :] = 1.0
    d["own_head"] = own.reshape(P, H, DK + 1)
    d["w1"], d["w2"] = a["L0_ffn_w1_w"].T, a["L0_ffn_w2_w"].T
    for n in ("h1", "h2"):
        d[n] = a[f"L0_ffn_{n}_w"].T.reshape(F, P, FF).transpose(1, 0, 2)
    d["w3"] = a["L0_ffn_w3_w"].T.reshape(F, P, P).transpose(1, 0, 2)
    d["s_hidden"] = np.stack([a[f"L0_ffn_{n}_s"].reshape(F, P).T for n in ("w1", "w2", "h1", "h2")], 1)
    d["s_out"] = a["L0_ffn_w3_s"]

    def rows(w):
        return np.broadcast_to(w.reshape(2, 8, 1, DK), (2, 8, 2, DK)).reshape(2, P).T

    for n in "wb":
        d[f"{n}_qk"] = np.concatenate([rows(a[f"L1_attn_{n}_q"]), rows(a[f"L1_attn_{n}_k"])], 1)
    quarter = np.zeros((8, 2, DK), f32)
    quarter[:, 0] = 512 // 4
    d["quarter"] = quarter.reshape(P, 1)
    d["wv2"], d["wo2"] = a["L1_attn_v_w"].T, a["L1_attn_out_w"].T
    d["router"] = a["L1_ffn_router_w"].T
    d["e1"] = a["L1_ffn_w1"].transpose(1, 0, 2)
    d["e2"] = a["L1_ffn_w2"].reshape(E, F, P, P).transpose(2, 0, 1, 3)
    row, col = np.arange(P)[:, None], np.arange(P)[None, :]
    d["ident"] = (row == col).astype(f32)
    d["causal"] = np.where(row > col, f32(-30000), f32(0))
    d["before"] = (row < col).astype(f32)
    of_head, of_max = row // DK == np.arange(H)[None, :], row == DK * ((np.arange(H)[None, :] + 8) % H)
    d["head8"] = np.stack([of_head, of_max], 1).astype(f32)
    d["head16"] = (row // (2 * DK) == np.arange(8)[None, :]).astype(f32)
    d["experts"] = np.broadcast_to(np.arange(E, dtype=f32), (P, E))
    return {k: np.ascontiguousarray(v) for k, v in d.items()}


def kernel(**inputs):
    import concourse.bacc as bacc
    from concourse.bass_utils import run_bass_kernel_spmd

    arrays = lay_out(inputs)
    nc = bacc.Bacc("TRN2", target_bir_lowering=False, num_devices=1)
    d = {n: nc.dram_tensor(f"in_{n}", a.shape, mybir.dt.from_np(a.dtype), kind="ExternalInput").ap()
         for n, a in arrays.items()}
    out = nc.dram_tensor("out_0", (NB, P, P), F32, kind="ExternalOutput").ap()
    build_decoder(nc, d, out)
    r = run_bass_kernel_spmd(nc, [{f"in_{n}": a for n, a in arrays.items()}], core_ids=[0])
    return r.results[0]["out_0"]
```
